# Optimizing a Trainium2 kernel written in Bass

```python
import numpy as np
import jax
import jax.numpy as jnp

def _softmax(x, axis=-1):
    return jax.nn.softmax(x, axis=axis)

def _gelu(x):
    return jax.nn.gelu(x, approximate=True)

def _silu(x):
    return jax.nn.silu(x)

def _sigmoid(x):
    return jax.nn.sigmoid(x)

def _layernorm(x, axis=-1, eps=1e-05):
    m = jnp.mean(x, axis=axis, keepdims=True)
    v = jnp.var(x, axis=axis, keepdims=True)
    return (x - m) / jnp.sqrt(v + eps)

def _scatter_add(tgt, idx, src, axis=0):
    return tgt.at[idx].add(src)

def _segment_sum(src, seg, n):
    return jax.ops.segment_sum(src, seg, n)
kernel_name = 'mk_recurrent_d2_jaxref_r8_737e60'

def setup_inputs(seed: int=0):
    np.random.seed(seed)
    _w = jnp.asarray

    def _L0_attn_setup():
        import jax, jax.numpy as jnp
        import numpy as np
        from jax import lax
        B, S, H = (8, 512, 128)
        key = jax.random.key(seed)
        ks = jax.random.split(key, 9)
        x = jax.random.normal(ks[0], (B, S, H), dtype=jnp.float32)
        time_decay = jax.random.normal(ks[1], (H,), dtype=jnp.float32) * 0.01
        time_mix_k = jnp.ones((H,), dtype=jnp.float32) * 0.5
        time_mix_v = jnp.ones((H,), dtype=jnp.float32) * 0.5
        time_mix_r = jnp.ones((H,), dtype=jnp.float32) * 0.5
        sc = 1.0 / np.sqrt(H)
        Wk = jax.random.uniform(ks[2], (H, H), jnp.float32, -sc, sc)
        Wv = jax.random.uniform(ks[3], (H, H), jnp.float32, -sc, sc)
        Wr = jax.random.uniform(ks[4], (H, H), jnp.float32, -sc, sc)
        Wo = jax.random.uniform(ks[5], (H, H), jnp.float32, -sc, sc)
        return {'x': x, 'time_decay': time_decay, 'time_mix_k': time_mix_k, 'time_mix_v': time_mix_v, 'time_mix_r': time_mix_r, 'Wk': Wk, 'Wv': Wv, 'Wr': Wr, 'Wo': Wo}
    _L0_attn_in = _L0_attn_setup()

    def _L0_ffn_setup():
        import jax, jax.numpy as jnp
        import numpy as np
        D, H, O, E, TOPK = (128, 512, 128, 8, 2)
        B, S = (4, 128)
        key = jax.random.key(seed)
        ks = jax.random.split(key, 12)
        std = 0.02
        return {'hidden_states': jax.random.normal(ks[0], (B, S, D), dtype=jnp.float32), 'norm_weight': jnp.ones((D,), dtype=jnp.float32), 'router_w': jax.random.normal(ks[1], (E, D), dtype=jnp.float32) * std, 'sw1': jax.random.normal(ks[2], (D, H), dtype=jnp.float32) * (1.0 / np.sqrt(D)), 'sb1': jnp.zeros((H,), dtype=jnp.float32), 'sw2': jax.random.normal(ks[3], (H, O), dtype=jnp.float32) * (1.0 / np.sqrt(H)), 'sb2': jnp.zeros((O,), dtype=jnp.float32), 'ew1': jax.random.normal(ks[4], (E, D, H), dtype=jnp.float32) * (1.0 / np.sqrt(D)), 'eb1': jnp.zeros((E, H), dtype=jnp.float32), 'ew2': jax.random.normal(ks[5], (E, H, O), dtype=jnp.float32) * (1.0 / np.sqrt(H)), 'eb2': jnp.zeros((E, O), dtype=jnp.float32)}
    _L0_ffn_in = _L0_ffn_setup()

    def _L1_attn_setup():
        import jax, jax.numpy as jnp
        import numpy as np
        import math
        D_MODEL, D_STATE, N_HEADS, DT_RANK = (128, 16, 16, 64)
        D_HEAD = D_MODEL // N_HEADS
        B, L = (2, 256)

        def _mhssm(x, A_log, Wx, Wdt, bdt, Wout, bout):
            b, l, d = x.shape
            xh = x.reshape(b, l, N_HEADS, D_HEAD)
            xp = jnp.einsum('blhd,ed->blhe', xh, Wx)
            dt_x = xp[..., :DT_RANK]
            B_x = xp[..., DT_RANK:DT_RANK + D_STATE]
            C_x = xp[..., DT_RANK + D_STATE:]
            dt = jax.nn.softplus(jnp.einsum('blhr,dr->blhd', dt_x, Wdt) + bdt)
            A = -jnp.exp(A_log)

            def step(h, inp):
                dt_t, B_t, C_t, x_t = inp
                A_bar = jnp.exp(dt_t[..., None] * A[None, :, None, :])
                h = A_bar * h + (dt_t * x_t)[..., None] * B_t[:, :, None, :]
                y_t = jnp.einsum('bhdn,bhn->bhd', h, C_t)
                return (h, y_t)
            h0 = jnp.zeros((b, N_HEADS, D_HEAD, D_STATE), dtype=x.dtype)
            inps = (jnp.moveaxis(dt, 1, 0), jnp.moveaxis(B_x, 1, 0), jnp.moveaxis(C_x, 1, 0), jnp.moveaxis(xh, 1, 0))
            _, ys = jax.lax.scan(step, h0, inps)
            y = jnp.moveaxis(ys, 0, 1).reshape(b, l, d)
            return y @ Wout.T + bout
        key = jax.random.key(seed)
        ks = jax.random.split(key, 6)
        x = jax.random.normal(ks[0], (B, L, D_MODEL), dtype=jnp.float32)
        A_log = jnp.broadcast_to(jnp.log(jnp.arange(1, D_STATE + 1, dtype=jnp.float32))[None, :], (N_HEADS, D_STATE))
        s = 1.0 / math.sqrt(D_HEAD)
        Wx = jax.random.uniform(ks[1], (DT_RANK + 2 * D_STATE, D_HEAD), minval=-s, maxval=s, dtype=jnp.float32)
        s2 = 1.0 / math.sqrt(DT_RANK)
        Wdt = jax.random.uniform(ks[2], (D_HEAD, DT_RANK), minval=-s2, maxval=s2, dtype=jnp.float32)
        dt = jnp.exp(jax.random.uniform(ks[3], (D_HEAD,)) * (math.log(0.1) - math.log(0.001)) + math.log(0.001))
        bdt = dt + jnp.log(-jnp.expm1(-dt))
        s3 = 1.0 / math.sqrt(D_MODEL)
        Wout = jax.random.uniform(ks[4], (D_MODEL, D_MODEL), minval=-s3, maxval=s3, dtype=jnp.float32)
        bout = jax.random.uniform(ks[5], (D_MODEL,), minval=-s3, maxval=s3, dtype=jnp.float32)
        return {'x': x, 'A_log': A_log, 'Wx': Wx, 'Wdt': Wdt, 'bdt': bdt, 'Wout': Wout, 'bout': bout}
    _L1_attn_in = _L1_attn_setup()

    def _L1_ffn_setup():
        import jax, jax.numpy as jnp
        import numpy as np
        TOP_K = 2
        TEMP = 0.9
        EPS = 1e-05
        B, S, D, F, E = (2, 256, 128, 512, 8)

        def _moe_forward(x, gate_w, gate_b, w1, b1, w2, b2, ln_g, ln_b):
            logits = (x @ gate_w + gate_b) / TEMP
            topk_vals, topk_idx = jax.lax.top_k(logits, TOP_K)
            keep = jax.nn.one_hot(topk_idx, E, dtype=jnp.bool_).any(-2)
            masked = jnp.where(keep, logits, -jnp.inf)
            gate_probs = jax.nn.softmax(masked, axis=-1)
            h = jnp.einsum('bsd,edf->bsef', x, w1) + b1
            h = jax.nn.gelu(h, approximate=False)
            expert_out = jnp.einsum('bsef,efd->bsed', h, w2) + b2
            out = jnp.einsum('bse,bsed->bsd', gate_probs, expert_out)
            mu = out.mean(-1, keepdims=True)
            var = out.var(-1, keepdims=True)
            out = (out - mu) / jnp.sqrt(var + EPS) * ln_g + ln_b
            return out
        key = jax.random.key(seed)
        ks = jax.random.split(key, 4)
        scale_in = 1.0 / np.sqrt(D)
        scale_ff = 1.0 / np.sqrt(F)
        return {'x': jax.random.normal(ks[0], (B, S, D), jnp.float32), 'gate_w': jax.random.normal(ks[1], (D, E), jnp.float32) * scale_in, 'gate_b': jnp.zeros((E,), jnp.float32), 'w1': jax.random.normal(ks[2], (E, D, F), jnp.float32) * scale_in, 'b1': jnp.zeros((E, F), jnp.float32), 'w2': jax.random.normal(ks[3], (E, F, D), jnp.float32) * scale_ff, 'b2': jnp.zeros((E, D), jnp.float32), 'ln_g': jnp.ones((D,), jnp.float32), 'ln_b': jnp.zeros((D,), jnp.float32)}
    _L1_ffn_in = _L1_ffn_setup()
    _d = {'L0_attn_x': _L0_attn_in['x'], 'L0_attn_time_decay': _L0_attn_in['time_decay'], 'L0_attn_time_mix_k': _L0_attn_in['time_mix_k'], 'L0_attn_time_mix_v': _L0_attn_in['time_mix_v'], 'L0_attn_time_mix_r': _L0_attn_in['time_mix_r'], 'L0_attn_Wk': _L0_attn_in['Wk'], 'L0_attn_Wv': _L0_attn_in['Wv'], 'L0_attn_Wr': _L0_attn_in['Wr'], 'L0_attn_Wo': _L0_attn_in['Wo'], 'L0_ffn_norm_weight': _L0_ffn_in['norm_weight'], 'L0_ffn_router_w': _L0_ffn_in['router_w'], 'L0_ffn_sw1': _L0_ffn_in['sw1'], 'L0_ffn_sb1': _L0_ffn_in['sb1'], 'L0_ffn_sw2': _L0_ffn_in['sw2'], 'L0_ffn_sb2': _L0_ffn_in['sb2'], 'L0_ffn_ew1': _L0_ffn_in['ew1'], 'L0_ffn_eb1': _L0_ffn_in['eb1'], 'L0_ffn_ew2': _L0_ffn_in['ew2'], 'L0_ffn_eb2': _L0_ffn_in['eb2'], 'L1_attn_A_log': _L1_attn_in['A_log'], 'L1_attn_Wx': _L1_attn_in['Wx'], 'L1_attn_Wdt': _L1_attn_in['Wdt'], 'L1_attn_bdt': _L1_attn_in['bdt'], 'L1_attn_Wout': _L1_attn_in['Wout'], 'L1_attn_bout': _L1_attn_in['bout'], 'L1_ffn_gate_w': _L1_ffn_in['gate_w'], 'L1_ffn_gate_b': _L1_ffn_in['gate_b'], 'L1_ffn_w1': _L1_ffn_in['w1'], 'L1_ffn_b1': _L1_ffn_in['b1'], 'L1_ffn_w2': _L1_ffn_in['w2'], 'L1_ffn_b2': _L1_ffn_in['b2'], 'L1_ffn_ln_g': _L1_ffn_in['ln_g'], 'L1_ffn_ln_b': _L1_ffn_in['ln_b']}
    _x0 = _d['L0_attn_x']
    _d['L0_attn_x'] = jax.random.normal(jax.random.fold_in(jax.random.key(seed), 1), (8, 512, 128), dtype=_x0.dtype)
    del _x0
    return _d

def reference(L0_attn_x, L0_attn_time_decay, L0_attn_time_mix_k, L0_attn_time_mix_v, L0_attn_time_mix_r, L0_attn_Wk, L0_attn_Wv, L0_attn_Wr, L0_attn_Wo, L0_ffn_norm_weight, L0_ffn_router_w, L0_ffn_sw1, L0_ffn_sb1, L0_ffn_sw2, L0_ffn_sb2, L0_ffn_ew1, L0_ffn_eb1, L0_ffn_ew2, L0_ffn_eb2, L1_attn_A_log, L1_attn_Wx, L1_attn_Wdt, L1_attn_bdt, L1_attn_Wout, L1_attn_bout, L1_ffn_gate_w, L1_ffn_gate_b, L1_ffn_w1, L1_ffn_b1, L1_ffn_w2, L1_ffn_b2, L1_ffn_ln_g, L1_ffn_ln_b):

    def _L0_attn_ref(x, time_decay, time_mix_k, time_mix_v, time_mix_r, Wk, Wv, Wr, Wo):
        import jax, jax.numpy as jnp
        import numpy as np
        from jax import lax
        B, S, H = (8, 512, 128)
        d = jnp.exp(-jnp.exp(time_decay))
        b, s, h = x.shape

        def step(state, xt):
            new_state = xt + state * d
            return (new_state, state)
        init = jnp.zeros((b, h), dtype=x.dtype)
        _, prev = lax.scan(step, init, jnp.swapaxes(x, 0, 1))
        prev = jnp.swapaxes(prev, 0, 1)
        k_in = x * time_mix_k + prev * (1.0 - time_mix_k)
        v_in = x * time_mix_v + prev * (1.0 - time_mix_v)
        r_in = x * time_mix_r + prev * (1.0 - time_mix_r)
        _k = jnp.einsum('bsh,oh->bso', k_in, Wk)
        v = jnp.einsum('bsh,oh->bso', v_in, Wv)
        r = jax.nn.sigmoid(jnp.einsum('bsh,oh->bso', r_in, Wr))
        out = r * jnp.einsum('bsh,oh->bso', v, Wo)
        return out

    def _L0_ffn_ref(hidden_states, norm_weight, router_w, sw1, sb1, sw2, sb2, ew1, eb1, ew2, eb2):
        import jax, jax.numpy as jnp
        import numpy as np
        D, H, O, E, TOPK = (128, 512, 128, 8, 2)
        B, S = (4, 128)
        b, s, d = hidden_states.shape
        var = jnp.mean(jnp.square(hidden_states), axis=-1, keepdims=True)
        normed = hidden_states * jax.lax.rsqrt(var + 1e-08) * norm_weight
        shared = jnp.maximum(normed @ sw1 + sb1, 0.0) @ sw2 + sb2
        flat = normed.reshape(-1, d)
        T = flat.shape[0]
        probs = jax.nn.sigmoid(flat @ router_w.T)
        scores, idx = jax.lax.top_k(probs, TOPK)
        w = scores / (jnp.sum(scores, axis=-1, keepdims=True) + 1e-06)
        comb = jnp.zeros((T, E), dtype=flat.dtype)
        comb = comb.at[jnp.arange(T)[:, None], idx].add(w)
        h = jnp.maximum(jnp.einsum('td,edh->teh', flat, ew1) + eb1[None, :, :], 0.0)
        eo = jnp.einsum('teh,eho->teo', h, ew2) + eb2[None, :, :]
        routed = jnp.einsum('teo,te->to', eo, comb)
        return shared + routed.reshape(b, s, -1)

    def _L1_attn_ref(x, A_log, Wx, Wdt, bdt, Wout, bout):
        import jax, jax.numpy as jnp
        import numpy as np
        import math
        D_MODEL, D_STATE, N_HEADS, DT_RANK = (128, 16, 16, 64)
        D_HEAD = D_MODEL // N_HEADS
        B, L = (2, 256)

        def _mhssm(x, A_log, Wx, Wdt, bdt, Wout, bout):
            b, l, d = x.shape
            xh = x.reshape(b, l, N_HEADS, D_HEAD)
            xp = jnp.einsum('blhd,ed->blhe', xh, Wx)
            dt_x = xp[..., :DT_RANK]
            B_x = xp[..., DT_RANK:DT_RANK + D_STATE]
            C_x = xp[..., DT_RANK + D_STATE:]
            dt = jax.nn.softplus(jnp.einsum('blhr,dr->blhd', dt_x, Wdt) + bdt)
            A = -jnp.exp(A_log)

            def step(h, inp):
                dt_t, B_t, C_t, x_t = inp
                A_bar = jnp.exp(dt_t[..., None] * A[None, :, None, :])
                h = A_bar * h + (dt_t * x_t)[..., None] * B_t[:, :, None, :]
                y_t = jnp.einsum('bhdn,bhn->bhd', h, C_t)
                return (h, y_t)
            h0 = jnp.zeros((b, N_HEADS, D_HEAD, D_STATE), dtype=x.dtype)
            inps = (jnp.moveaxis(dt, 1, 0), jnp.moveaxis(B_x, 1, 0), jnp.moveaxis(C_x, 1, 0), jnp.moveaxis(xh, 1, 0))
            _, ys = jax.lax.scan(step, h0, inps)
            y = jnp.moveaxis(ys, 0, 1).reshape(b, l, d)
            return y @ Wout.T + bout
        return _mhssm(x, A_log, Wx, Wdt, bdt, Wout, bout)

    def _L1_ffn_ref(x, gate_w, gate_b, w1, b1, w2, b2, ln_g, ln_b):
        import jax, jax.numpy as jnp
        import numpy as np
        TOP_K = 2
        TEMP = 0.9
        EPS = 1e-05
        B, S, D, F, E = (2, 256, 128, 512, 8)

        def _moe_forward(x, gate_w, gate_b, w1, b1, w2, b2, ln_g, ln_b):
            logits = (x @ gate_w + gate_b) / TEMP
            topk_vals, topk_idx = jax.lax.top_k(logits, TOP_K)
            keep = jax.nn.one_hot(topk_idx, E, dtype=jnp.bool_).any(-2)
            masked = jnp.where(keep, logits, -jnp.inf)
            gate_probs = jax.nn.softmax(masked, axis=-1)
            h = jnp.einsum('bsd,edf->bsef', x, w1) + b1
            h = jax.nn.gelu(h, approximate=False)
            expert_out = jnp.einsum('bsef,efd->bsed', h, w2) + b2
            out = jnp.einsum('bse,bsed->bsd', gate_probs, expert_out)
            mu = out.mean(-1, keepdims=True)
            var = out.var(-1, keepdims=True)
            out = (out - mu) / jnp.sqrt(var + EPS) * ln_g + ln_b
            return out
        return _moe_forward(x, gate_w, gate_b, w1, b1, w2, b2, ln_g, ln_b)
    x = L0_attn_x
    xn = _layernorm(x, axis=-1)
    s = _L0_attn_ref(xn, L0_attn_time_decay, L0_attn_time_mix_k, L0_attn_time_mix_v, L0_attn_time_mix_r, L0_attn_Wk, L0_attn_Wv, L0_attn_Wr, L0_attn_Wo)
    g = _silu(_L0_ffn_ref(xn, L0_ffn_norm_weight, L0_ffn_router_w, L0_ffn_sw1, L0_ffn_sb1, L0_ffn_sw2, L0_ffn_sb2, L0_ffn_ew1, L0_ffn_eb1, L0_ffn_ew2, L0_ffn_eb2))
    x = x + s * g
    xn = _layernorm(x, axis=-1)
    s = _L1_attn_ref(xn, L1_attn_A_log, L1_attn_Wx, L1_attn_Wdt, L1_attn_bdt, L1_attn_Wout, L1_attn_bout)
    g = _silu(_L1_ffn_ref(xn, L1_ffn_gate_w, L1_ffn_gate_b, L1_ffn_w1, L1_ffn_b1, L1_ffn_w2, L1_ffn_b2, L1_ffn_ln_g, L1_ffn_ln_b))
    x = x + s * g
    return x

_drawn_inputs = setup_inputs


def setup_inputs(seed=0):
    import zlib

    import numpy as np

    out = dict(_drawn_inputs(seed))
    spreads = {'L0_attn_time_mix_k': (0.5, 0.2),
     'L0_attn_time_mix_v': (0.5, 0.6),
     'L0_attn_time_mix_r': (0.5, 0.6),
     'L0_ffn_norm_weight': (1.0, 0.6),
     'L0_ffn_sb1': (0.0, 0.8),
     'L0_ffn_sb2': (0.0, 0.8),
     'L0_ffn_eb1': (0.0, 0.8),
     'L0_ffn_eb2': (0.0, 0.8),
     'L1_ffn_gate_b': (0.0, 0.532),
     'L1_ffn_b1': (0.0, 0.8),
     'L1_ffn_b2': (0.0, 0.717),
     'L1_ffn_ln_g': (1.0, 0.6),
     'L1_ffn_ln_b': (0.0, 0.8)}
    factors = {'L0_attn_time_decay': 24.532, 'L0_attn_Wr': 4.02, 'L1_attn_Wdt': 3.644}
    for name, (base, spread) in spreads.items():
        noise = np.random.default_rng([zlib.crc32(name.encode()), seed]).standard_normal(out[name].shape)
        drawn = base * np.exp(spread * noise) if base else spread * noise
        out[name] = jnp.asarray(drawn.astype(out[name].dtype))
    for name, factor in factors.items():
        out[name] = (out[name] * factor).astype(out[name].dtype)
    return out
```

```python
def run_layer0(nc, ctx, shared, dram):
    from concourse import mybir

    F32, F32R, U32 = mybir.dt.float32, mybir.dt.float32r, mybir.dt.uint32
    ALU, ACT, AX = mybir.AluOpType, mybir.ActivationFunctionType, mybir.AxisListType

    def sb(name, shape, dt=F32):
        return ctx.enter_context(nc.sbuf_tensor("l0_" + name, shape, dt))

    def sem(name):
        return ctx.enter_context(nc.semaphore("l0_" + name))

    P = 128
    B, S = dram["x"].shape[:2]
    J = S // P
    EXPERTS = 8
    E = EXPERTS + 1
    C = 4
    N = E * C
    RING = 2 * C
    LO_ON_POOL = (1,)
    LN_EPS, RMS_EPS, SUM_EPS = 1e-5, 1e-8, 1e-6

    w1h, w1l, w2h, w2l = (shared[k] for k in ("w1h", "w1l", "w2h", "w2l"))
    hh, hl = shared["hh"], shared["hl"]
    t, acc = shared["t"], shared["acc"]
    ident, iota8 = shared["ident"], shared["iota8"]
    PH, PY, G = shared["PH"], shared["PY"], shared["G"]

    CB1, CB2 = 0, E * C
    CTD, CMV, CMR, CNW = CB2 + E, CB2 + E + 1, CB2 + E + 2, CB2 + E + 3
    cols = sb("cols", [P, CNW + 1])
    hid = [sb(f"hid{i}", [P, S]) for i in range(C)]
    gate = [sb(f"gate{i}", [P, S]) for i in range(4)]
    sw1h, sw1l = sb("sw1h", [P, C * P], F32R), sb("sw1l", [P, C * P], F32R)
    sw2h, sw2l = sb("sw2h", [P, C, P], F32R), sb("sw2l", [P, C, P], F32R)
    stage = [sb(f"stage{i}", [P, 2 * C * P]) for i in range(3)]
    wa = sb("wa", [P, 4, P])
    rw = sb("rw", [P, EXPERTS])
    woh, wol = sb("woh", [P, P], F32R), sb("wol", [P, P], F32R)
    wrh, wrl = sb("wrh", [P, P], F32R), sb("wrl", [P, P], F32R)
    decay = sb("decay", [P, 2])
    half = sb("half", [P, 2 * C])
    xin, xres, xo = sb("xin", [P, J, P]), sb("xres", [P, J, P]), sb("xo", [P, J, P])
    xn, xr, sq = sb("xn", [P, J, P]), sb("xr", [P, J, P]), sb("sq", [P, J, P])
    st, mv = sb("st", [P, J, 6]), sb("mv", [P, J, 2])
    var, rstd = sb("var", [P, 2, J]), sb("rstd", [P, 2, J])
    xT, nT = sb("xT", [P, S]), sb("nT", [P, S])
    nh = [sb(f"nh{i}", [P, S], F32R) for i in range(2)]
    nl = [sb(f"nl{i}", [P, S], F32R) for i in range(2)]
    sums = sb("sums", [P, S + 1])
    dif, vin, rin = sb("dif", [P, S]), sb("vin", [P, S]), sb("rin", [P, S])
    vh, vl, rh, rl = (sb(n, [P, S], F32R) for n in ("vh", "vl", "rh", "rl"))
    tr = sb("tr", [P, S])
    rv = [sb(f"rv{i}", [P, S]) for i in range(2)]
    z, tz, q, prod = sb("z", [P, S]), sb("tz", [P, S]), sb("q", [P, S]), sb("prod", [P, S])
    key, ex = sb("key", [P, J, EXPERTS]), sb("ex", [P, J, EXPERTS])
    prob, eq = sb("prob", [P, J, EXPERTS]), sb("eq", [P, J, 2, EXPERTS])
    top, idx = sb("top", [P, J, 8]), sb("idx", [P, J, 8], U32)
    idxf, sel = sb("idxf", [P, J, 2]), sb("sel", [P, J, EXPERTS])
    tot, comb = sb("tot", [P, 3, J]), sb("comb", [P, J, EXPERTS])
    combT = sb("combT", [EXPERTS, S])

    cols_in, wa_in = sem("cols_in"), sem("wa_in")
    stage_in = [sem(f"stage_in{i}") for i in range(3)]
    hi_made, lo_made = sem("w_hi_made"), sem("w_lo_made")
    set_step = sem("setup_step")
    wvo_done, attn_w = sem("wvo_done"), sem("attn_w_split")
    decay_step, decay_made = sem("decay_step"), sem("decay_made")
    zero_made = sem("zero_made")
    xin_in, xres_in = sem("xin_in"), sem("xres_in")
    prep, tail = sem("prep_step"), sem("tail_step")
    var_made, rstd_made = sem("var_made"), sem("rstd_made")
    xn_made, xposed = sem("xn_made"), sem("x_transposed")
    xT_made, nT_made, nl_made = sem("xT_made"), sem("nT_made"), sem("nl_made")
    logits_done, ex_made = sem("logits_done"), sem("ex_made")
    comb_made, combT_done, combT_made = sem("comb_made"), sem("combT_done"), sem("combT_made")
    comb_out = sem("comb_out")
    mixed, mixed_hi, mixed_lo = sem("mixed"), sem("mixed_hi"), sem("mixed_lo")
    attn_done, tr_made, rv_made = sem("attn_done"), sem("tr_made"), sem("rv_made")
    gate_in = [sem(f"gate_in{i}") for i in range(len(gate))]
    up_done, hid_made = sem("up_done"), sem("hid_made")
    lo_dve, lo_pool = sem("lo_dve"), sem("lo_pool")
    y_done, t_made, acc_made = sem("y_done"), sem("t_made"), sem("acc_made")
    z_made, tz_made, prod_made = sem("z_made"), sem("tz_made"), sem("prod_made")
    prodT_done, xo_made, xo_out = sem("prodT_done"), sem("xo_made"), sem("xo_out")

    dve_passed, sp_passed = sem("dve_passed"), sem("sp_passed")

    NP = len(LO_ON_POOL)
    ND = C - NP
    PREP, TAIL = 17, 1

    def first_weights(e):
        return (sw1h[:, :], sw1l[:, :]) if e == EXPERTS else (w1h[:, e, :], w1l[:, e, :])

    def second_weights(e):
        return (sw2h[:, :, :], sw2l[:, :, :]) if e == EXPERTS else (w2h[:, e * C:(e + 1) * C, :], w2l[:, e * C:(e + 1) * C, :])

    def slot_of(par, e, c):
        return (par * N + e * C + c) % RING

    x_tok = dram["x"].rearrange("b (j p) d -> b p j d", p=P)
    x1_tok = dram["x1"].rearrange("b (j p) d -> b p j d", p=P)

    def chained(eng, s, per):
        def step(b, n, ins):
            assert 1 <= n <= per
            ins.then_inc(s, 1)
            eng.wait_ge(s, b * per + n)
        return step

    def apart(eng, passed):
        eng.sem_inc(passed, 1)

    def rolled(eng, body):
        body(0, 0, True, False)
        with eng.Fori(0, (B - 2) // 2) as k:
            body(2 * k + 1, 1, False, False)
            body(2 * k + 2, 0, False, False)
        body(B - 1, 1, False, True)

    block = ctx.enter_context(nc.Block())

    @block.sync
    def _(sp):
        def load_x(b, first):
            if not first:
                sp.wait_ge(xn_made, b)
                apart(sp, sp_passed)
            sp.dma_start(xin[:, :, :], x_tok[b]).then_inc(xin_in, 16)

        def load_gate(b, e, first):
            s = e % len(gate)
            if e >= len(gate):
                sp.wait_ge(t_made, b * EXPERTS + e - len(gate) + 1)
            elif not first:
                sp.wait_ge(t_made, (b - 1) * EXPERTS + e + EXPERTS - len(gate) + 1)
            apart(sp, sp_passed)
            sp.dma_start(gate[s][:, :], dram["comb0"][b, e].partition_broadcast(P)).then_inc(gate_in[s], 16)

        def store_comb(b):
            sp.wait_ge(combT_made, b + 1)
            apart(sp, sp_passed)
            sp.dma_start(dram["comb0"][b], combT[:, :]).then_inc(comb_out, 16)

        def tail_dma(b):
            sp.wait_ge(xo_made, b + 1)
            apart(sp, sp_passed)
            sp.dma_start(xres[:, :, :], x_tok[b]).then_inc(xres_in, 16)

        def store_x1(b):
            sp.wait_ge(xo_made, b + 2)
            apart(sp, sp_passed)
            sp.dma_start(x1_tok[b], xo[:, :, :]).then_inc(xo_out, 16)

        sp.sem_inc(xo_out, 16)
        load_x(0, True)
        sp.dma_start(cols[:, :], dram["cols0"]).then_inc(cols_in, 16)
        sp.dma_start(rw[:, :], dram["rw"]).then_inc(cols_in, 16)
        sp.dma_start(ident[:, :], dram["ident"]).then_inc(cols_in, 16)
        sp.dma_start(iota8[:, :], dram["iota8"]).then_inc(cols_in, 16)
        sp.dma_start(wa[:, 0:3, :], dram["wa"].rearrange("k p n -> p k n")).then_inc(wa_in, 16)
        for e in range(E):
            s = e % 3
            if e >= 3:
                sp.wait_ge(hi_made, e - 2)
                sp.wait_ge(lo_made, e - 2)
            w1 = dram["ew1"][e] if e < EXPERTS else dram["sw1"]
            w2 = dram["ew2"][e] if e < EXPERTS else dram["sw2"]
            sp.dma_start(stage[s][:, 0:C * P], w1).then_inc(stage_in[s], 16)
            sp.dma_start(stage[s][:, C * P:].rearrange("p (c n) -> p c n", c=C),
                         w2.rearrange("(c p) n -> p c n", p=P)).then_inc(stage_in[s], 16)
        store_comb(0)

        def body(b, par, first, last):
            sp.wait_ge(comb_out, 16 * (b + 1))
            apart(sp, sp_passed)
            for e in range(len(gate)):
                load_gate(b, e, first)
            if not last:
                load_x(b + 1, False)
            if not first:
                tail_dma(b - 1)
            for e in range(len(gate), EXPERTS):
                load_gate(b, e, first)
                if e == len(gate) and not first:
                    store_x1(b - 1)
            if not last:
                store_comb(b + 1)

        rolled(sp, body)
        tail_dma(B - 1)
        store_x1(B - 1)
        sp.wait_ge(xo_out, 16 * (B + 1))

    @block.tensor
    def _(pe):
        def three_pass(out, wh, wl, h, l, start=True, stop=True):
            pe.matmul(out, wh, h, start=start, stop=False)
            pe.matmul(out, wl, h, start=False, stop=False)
            return pe.matmul(out, wh, l, start=False, stop=stop)

        def up(b, par, e, first):
            if e == 0:
                pe.wait_ge(nl_made, b + 1)
            if first:
                pe.wait_ge(hi_made, e + 1)
                pe.wait_ge(lo_made, e + 1)
            for c in range(C):
                if not (first and e == 0):
                    pe.wait_ge(hid_made, b * N + (e - 1) * C + c + 1)
                w = slice(c * P, (c + 1) * P)
                three_pass(PH[c][:, :], first_weights(e)[0][:, w], first_weights(e)[1][:, w], nh[par][:, :], nl[par][:, :]).then_inc(up_done, 1)

        def down(b, par, e, first):
            if not (first and e == 0):
                pe.wait_ge(t_made, b * EXPERTS + min(e, EXPERTS))
                if e == 0:
                    pe.wait_ge(z_made, b)
            for c in range(C):
                if c in LO_ON_POOL:
                    pe.wait_ge(lo_pool, b * E * NP + e * NP + LO_ON_POOL.index(c) + 1)
                else:
                    own = [k for k in range(C) if k not in LO_ON_POOL]
                    pe.wait_ge(lo_dve, b * E * ND + e * ND + own.index(c) + 1)
                s = slot_of(par, e, c)
                last = three_pass(PY[:, :], second_weights(e)[0][:, c, :], second_weights(e)[1][:, c, :], hh[s][:, :], hl[s][:, :],
                                  c == 0, c == C - 1)
            last.then_inc(y_done, 1)

        def transposes(dst, src):
            for j in range(J):
                last = pe.transpose(dst[:, j * P:(j + 1) * P], src[:, j, :], ident[:, :])
            return last

        def transpose_x(b, first):
            pe.wait_ge(xn_made, b + 1)
            if not first:
                pe.wait_ge(rv_made, b)
            transposes(G[0], xn)
            transposes(G[1], xr).then_inc(xposed, 1)

        def logits(b, first):
            pe.wait_ge(nT_made, b + 1)
            if not first:
                pe.wait_ge(combT_made, b)
            for j in range(J):
                last = pe.matmul(G[2][:, j * EXPERTS:(j + 1) * EXPERTS], nT[:, j * P:(j + 1) * P], rw[:, :],
                                 start=True, stop=True)
            last.then_inc(logits_done, 1)

        def transpose_comb(b):
            pe.wait_ge(comb_made, b + 1)
            for j in range(J):
                last = pe.transpose(G[2][0:EXPERTS, j * P:(j + 1) * P], comb[:, j, :], ident[:, :])
            last.then_inc(combT_done, 1)

        def attention(b):
            pe.wait_ge(mixed_lo, b + 1)
            pe.wait_ge(nT_made, b + 1)
            three_pass(G[0][:, :], woh[:, :], wol[:, :], vh[:, :], vl[:, :])
            three_pass(G[1][:, :], wrh[:, :], wrl[:, :], rh[:, :], rl[:, :]).then_inc(attn_done, 1)

        def transpose_prod(b):
            pe.wait_ge(prod_made, b + 1)
            pe.wait_ge(xo_made, b + 1)
            for j in range(J):
                last = pe.transpose(G[2][:, j * P:(j + 1) * P], prod[:, j * P:(j + 1) * P], ident[:, :])
            last.then_inc(prodT_done, 1)

        pe.wait_ge(wa_in, 16)
        pe.matmul(G[2][:, 0:P], wa[:, 0, :], wa[:, 1, :], start=True, stop=True).then_inc(wvo_done, 1)
        pe.wait_ge(cols_in, 16 * 4)
        transpose_x(0, True)
        pe.wait_ge(attn_w, 1)
        logits(0, True)
        transpose_comb(0)
        attention(0)

        def body(b, par, first, last):
            for e in range(E):
                up(b, par, e, first)
                if e == 2 and not first:
                    pe.wait_ge(combT_made, b + 1)
                    transpose_prod(b - 1)
                if e == 3 and not last:
                    transpose_x(b + 1, False)
                if e == 5 and not last:
                    if not first:
                        pe.wait_ge(xo_made, b + 1)
                    logits(b + 1, False)
                if e == 7 and not last:
                    transpose_comb(b + 1)
                if e == E - 1 and not last:
                    attention(b + 1)
                if e > 0:
                    down(b, par, e - 1, first)
            down(b, par, E - 1, first)

        rolled(pe, body)
        transpose_prod(B - 1)

    @block.scalar
    def _(act):
        def hidden(b, par, e, first):
            for c in range(C):
                act.wait_ge(up_done, b * N + e * C + c + 1)
                if not (first and e < 2):
                    act.wait_ge(y_done, b * E + e - 1)
                if not (first and e == 0):
                    if c in LO_ON_POOL:
                        act.wait_ge(lo_pool, b * E * NP + (e - 1) * NP + LO_ON_POOL.index(c) + 1)
                    else:
                        own = [k for k in range(C) if k not in LO_ON_POOL]
                        act.wait_ge(lo_dve, b * E * ND + (e - 1) * ND + own.index(c) + 1)
                bias = cols[:, CB1 + e * C + c:CB1 + e * C + c + 1]
                act.activation(hh[slot_of(par, e, c)][:, :], PH[c][:, :], ACT.Relu, bias=bias)
                act.activation(hid[c][:, :], PH[c][:, :], ACT.Relu, bias=bias).then_inc(hid_made, 1)

        def evacuate_x(b, par, first):
            act.wait_ge(xposed, b + 1)
            if not first:
                act.wait_ge(mixed, b)
                act.wait_ge(nl_made, b)
                act.wait_ge(logits_done, b)
            act.activation(xT[:, :], G[0][:, :], ACT.Identity).then_inc(xT_made, 1)
            nw = cols[:, CNW:CNW + 1]
            act.activation(nT[:, :], G[1][:, :], ACT.Identity, scale=nw)
            act.activation(nh[par][:, :], G[1][:, :], ACT.Identity, scale=nw).then_inc(nT_made, 1)

        def router_exp(b):
            act.wait_ge(logits_done, b + 1)
            act.activation(ex[:, :, :], G[2][:, 0:J * EXPERTS].rearrange("p (j e) -> p j e", j=J), ACT.Exp,
                           scale=-1.0).then_inc(ex_made, 1)

        def split_mixed(b, first):
            act.wait_ge(mixed, b + 1)
            if not first:
                act.wait_ge(attn_done, b)
            act.activation(vh[:, :], vin[:, :], ACT.Identity)
            act.activation(rh[:, :], rin[:, :], ACT.Identity).then_inc(mixed_hi, 1)

        def tanh_r(b, first):
            act.wait_ge(attn_done, b + 1)
            if not first:
                act.wait_ge(rv_made, b)
            act.activation(tr[:, :], G[1][:, :], ACT.Tanh, scale=0.5).then_inc(tr_made, 1)

        def tanh_z(b, first):
            act.wait_ge(z_made, b + 1)
            act.activation(tz[:, :], z[:, :], ACT.Tanh, scale=0.5).then_inc(tz_made, 1)

        act.wait_ge(cols_in, 16 * 4)
        act.activation(decay[:, 0:1], cols[:, CTD:CTD + 1], ACT.Exp).then_inc(decay_step, 1)
        act.wait_ge(decay_step, 1)
        act.activation(decay[:, 1:2], decay[:, 0:1], ACT.Exp, scale=-1.0).then_inc(decay_made, 1)
        act.wait_ge(wvo_done, 1)
        act.activation(wa[:, 3, :], G[2][:, 0:P], ACT.Identity)
        act.activation(woh[:, :], G[2][:, 0:P], ACT.Identity)
        act.activation(wrh[:, :], wa[:, 2, :], ACT.Identity).then_inc(set_step, 1)

        def split_weights(e):
            act.wait_ge(stage_in[e % 3], 32 * (e // 3 + 1))
            act.activation(first_weights(e)[0], stage[e % 3][:, 0:C * P], ACT.Identity)
            act.activation(second_weights(e)[0], stage[e % 3][:, C * P:].rearrange("p (c n) -> p c n", c=C),
                           ACT.Identity).then_inc(hi_made, 1)
        split_weights(0)
        evacuate_x(0, 0, True)
        split_weights(1)
        router_exp(0)
        split_weights(2)
        split_mixed(0, True)
        for e in range(3, E):
            split_weights(e)
        tanh_r(0, True)

        def body(b, par, first, last):
            for e in range(E):
                hidden(b, par, e, first)
                if e == 1 and not first:
                    tanh_z(b - 1, False)
                if e == 3 and not last:
                    evacuate_x(b + 1, 1 - par, False)
                if e == 5 and not last:
                    router_exp(b + 1)
                if e == 6 and not last:
                    split_mixed(b + 1, False)
            if not last:
                tanh_r(b + 1, False)

        rolled(act, body)
        tanh_z(B - 1, False)

    @block.gpsimd
    def _(pool):
        def power(b, k):
            pool.wait_ge(var_made, 2 * b + k)
            pool.tensor_tensor(rstd[:, k - 1, :], var[:, k - 1, :], half[:, 0:J], ALU.pow).then_inc(rstd_made, 1)

        def low_part(b, par, e, first):
            for c in LO_ON_POOL:
                s = slot_of(par, e, c)
                pool.wait_ge(hid_made, b * N + e * C + c + 1)
                pool.tensor_tensor(hl[s][:, :], hid[c][:, :], hh[s][:, :].bitcast(F32), ALU.subtract).then_inc(lo_pool, 1)

        def accumulate(b, e):
            pool.wait_ge(t_made, b * EXPERTS + e + 1)
            if e >= 2:
                pool.wait_ge(acc_made, b * (EXPERTS - 1) + e - 1)
            pool.tensor_tensor(acc[:, :], acc[:, :], t[e % 2][:, :], ALU.add).then_inc(acc_made, 1)

        pool.memset(half[:, :], -0.5).then_inc(zero_made, 1)
        pool.memset(sums[:, 0:1], 0.0).then_inc(zero_made, 1)
        pool.wait_ge(zero_made, 2)
        power(0, 1)
        power(0, 2)
        for e in range(E):
            pool.wait_ge(hi_made, e + 1)
            st_ = stage[e % 3]
            pool.tensor_tensor(first_weights(e)[1], st_[:, 0:C * P], first_weights(e)[0].bitcast(F32), ALU.subtract)
            pool.tensor_tensor(second_weights(e)[1], st_[:, C * P:].rearrange("p (c n) -> p c n", c=C),
                               second_weights(e)[0].bitcast(F32), ALU.subtract).then_inc(lo_made, 1)
        
        def body(b, par, first, last):
            for e in range(E):
                if e == 0 and not last:
                    power(b + 1, 1)
                if e == 2 and not last:
                    power(b + 1, 2)
                low_part(b, par, e, first)
                if 2 <= e:
                    accumulate(b, e - 1)

        rolled(pool, body)

    @block.vector
    def _(dve):
        chain, tchain = chained(dve, prep, PREP), chained(dve, tail, TAIL)
        own = [c for c in range(C) if c not in LO_ON_POOL]

        def low_part(b, par, e, first):
            for c in own:
                s = slot_of(par, e, c)
                dve.wait_ge(hid_made, b * N + e * C + c + 1)
                dve.tensor_tensor(hl[s][:, :], hid[c][:, :], hh[s][:, :].bitcast(F32), ALU.subtract).then_inc(lo_dve, 1)

        def weigh(b, e, first):
            dve.wait_ge(y_done, b * E + e + 1)
            b2 = cols[:, CB2 + e:CB2 + e + 1]
            if e == EXPERTS:
                dve.wait_ge(acc_made, (b + 1) * (EXPERTS - 1))
                dve.scalar_tensor_tensor(z[:, :], PY[:, :], b2, acc[:, :], ALU.add, ALU.add).then_inc(z_made, 1)
                return
            s = e % len(gate)
            dve.wait_ge(gate_in[s], 16 * (b * (EXPERTS // len(gate)) + e // len(gate) + 1))
            if e == 0:
                out = acc
                if not first:
                    dve.wait_ge(z_made, b)
            else:
                out = t[e % 2]
                if e >= 3:
                    dve.wait_ge(acc_made, b * (EXPERTS - 1) + e - 2)
            dve.scalar_tensor_tensor(out[:, :], PY[:, :], b2, gate[s][:, :], ALU.add, ALU.mult).then_inc(t_made, 1)

        def normalise(b, first):
            dve.wait_ge(xin_in, 16 * (b + 1))
            if not first:
                dve.wait_ge(xposed, b)
            for j in range(J):
                i = dve.bn_stats(st[:, j, :], xin[:, j, :])
            chain(b, 1, i)
            apart(dve, dve_passed)
            for j in range(J):
                i = dve.bn_aggr(mv[:, j, :], st[:, j, :])
            chain(b, 2, i)
            dve.tensor_scalar(var[:, 0, :], mv[:, :, 1], LN_EPS, None, ALU.add).then_inc(var_made, 1)
            dve.wait_ge(rstd_made, 2 * b + 1)
            for j in range(J):
                i = dve.tensor_scalar(xn[:, j, :], xin[:, j, :], mv[:, j, 0:1], rstd[:, 0, j:j + 1],
                                      ALU.subtract, ALU.mult)
            chain(b, 3, i)

        def rms(b):
            chain(b, 4, dve.tensor_tensor(sq[:, :, :], xn[:, :, :], xn[:, :, :], ALU.mult))
            chain(b, 5, dve.tensor_reduce(tot[:, 2, :], sq[:, :, :], AX.X, ALU.add))
            dve.tensor_scalar(var[:, 1, :], tot[:, 2, :], 1.0 / P, RMS_EPS, ALU.mult, ALU.add).then_inc(var_made, 1)
            dve.wait_ge(rstd_made, 2 * b + 2)
            for j in range(J):
                i = dve.tensor_scalar(xr[:, j, :], xn[:, j, :], rstd[:, 1, j:j + 1], None, ALU.mult)
            i.then_inc(xn_made, 1)

        def split_normed(b, par):
            dve.wait_ge(nT_made, b + 1)
            dve.tensor_tensor(nl[par][:, :], nT[:, :], nh[par][:, :].bitcast(F32), ALU.subtract).then_inc(nl_made, 1)

        def mix(b):
            dve.wait_ge(xT_made, b + 1)
            chain(b, 6, dve.tensor_tensor_scan(sums[:, 1:S + 1], decay[:, 1:2].to_broadcast([P, S]), xT[:, :], 0.0,
                                               ALU.mult, ALU.add))
            prev = sums[:, 0:S]
            chain(b, 7, dve.tensor_tensor(dif[:, :], xT[:, :], prev, ALU.subtract))
            dve.scalar_tensor_tensor(vin[:, :], dif[:, :], cols[:, CMV:CMV + 1], prev, ALU.mult, ALU.add)
            dve.scalar_tensor_tensor(rin[:, :], dif[:, :], cols[:, CMR:CMR + 1], prev, ALU.mult,
                                     ALU.add).then_inc(mixed, 1)

        def split_mixed(b):
            dve.wait_ge(mixed_hi, b + 1)
            dve.tensor_tensor(vl[:, :], vin[:, :], vh[:, :].bitcast(F32), ALU.subtract)
            dve.tensor_tensor(rl[:, :], rin[:, :], rh[:, :].bitcast(F32), ALU.subtract).then_inc(mixed_lo, 1)

        def route_keys(b):
            dve.wait_ge(ex_made, b + 1)
            chain(b, 8, dve.tensor_scalar(key[:, :, :], G[2][:, 0:J * EXPERTS].rearrange("p (j e) -> p j e", j=J),
                                          17.0, -88.0, ALU.min, ALU.max))
            apart(dve, dve_passed)
            for j in range(J):
                i = dve.max(top[:, j, :], key[:, j, :])
            chain(b, 9, i)
            apart(dve, dve_passed)
            for j in range(J):
                i = dve.max_index(idx[:, j, :], top[:, j, :], key[:, j, :])
            chain(b, 10, i)
            chain(b, 11, dve.tensor_copy(idxf[:, :, :], idx[:, :, 0:2]))

        def route(b):
            for k in range(2):
                dve.tensor_tensor(eq[:, :, k, :], iota8[:, :].rearrange("p (j e) -> p j e", j=J),
                                  idxf[:, :, k:k + 1].to_broadcast([P, J, EXPERTS]), ALU.is_equal)
            chain(b, 12, dve.tensor_scalar(ex[:, :, :], ex[:, :, :], 1.0, None, ALU.add))
            dve.tensor_tensor(sel[:, :, :], eq[:, :, 0, :], eq[:, :, 1, :], ALU.add)
            chain(b, 13, dve.reciprocal(prob[:, :, :], ex[:, :, :]))
            chain(b, 14, dve.tensor_tensor(sel[:, :, :], sel[:, :, :], prob[:, :, :], ALU.mult))
            chain(b, 15, dve.tensor_reduce(tot[:, 0, :], sel[:, :, :], AX.X, ALU.add))
            chain(b, 16, dve.tensor_scalar(tot[:, 0, :], tot[:, 0, :], SUM_EPS, None, ALU.add))
            chain(b, 17, dve.reciprocal(tot[:, 1, :], tot[:, 0, :]))
            dve.tensor_tensor(comb[:, :, :], sel[:, :, :], tot[:, 1:2, :].rearrange("p k j -> p j k").to_broadcast([P, J, EXPERTS]),
                              ALU.mult).then_inc(comb_made, 1)

        def keep_comb(b, first):
            dve.wait_ge(combT_done, b + 1)
            if not first:
                dve.wait_ge(comb_out, 16 * b)
            dve.tensor_copy(combT[:, :], G[2][0:EXPERTS, :]).then_inc(combT_made, 1)

        def gated(b, par):
            dve.wait_ge(tr_made, b + 1)
            dve.scalar_tensor_tensor(rv[par][:, :], tr[:, :], 1.0, G[0][:, :], ALU.add, ALU.mult).then_inc(rv_made, 1)

        def product(b, par):
            dve.wait_ge(tz_made, b + 1)
            tchain(b, 1, dve.scalar_tensor_tensor(q[:, :], tz[:, :], 1.0, z[:, :], ALU.add, ALU.mult))
            dve.scalar_tensor_tensor(prod[:, :], q[:, :], 0.25, rv[par][:, :], ALU.mult, ALU.mult).then_inc(prod_made, 1)

        def add_residual(b):
            dve.wait_ge(prodT_done, b + 1)
            dve.wait_ge(xres_in, 16 * (b + 1))
            dve.wait_ge(xo_out, 16 * (b + 1))
            dve.tensor_tensor(xo[:, :, :].rearrange("p j d -> p (j d)"), G[2][:, :],
                              xres[:, :, :].rearrange("p j d -> p (j d)"), ALU.add).then_inc(xo_made, 1)

        dve.sem_inc(xo_made, 1)
        dve.wait_ge(zero_made, 2)
        dve.wait_ge(cols_in, 16 * 4)
        normalise(0, True)
        rms(0)
        dve.wait_ge(set_step, 1)
        dve.tensor_tensor(wol[:, :], wa[:, 3, :], woh[:, :].bitcast(F32), ALU.subtract)
        dve.tensor_tensor(wrl[:, :], wa[:, 2, :], wrh[:, :].bitcast(F32), ALU.subtract).then_inc(attn_w, 1)
        dve.wait_ge(decay_made, 1)
        split_normed(0, 0)
        mix(0)
        route_keys(0)
        route(0)
        keep_comb(0, True)
        split_mixed(0)
        gated(0, 0)

        def body(b, par, first, last):
            for e in range(E):
                low_part(b, par, e, first)
                if e > 0:
                    weigh(b, e - 1, first)
                if e == 0 and not last:
                    normalise(b + 1, False)
                if e == 1:
                    if not first:
                        product(b - 1, 1 - par)
                if e == 2 and not last:
                    rms(b + 1)
                if e == 3 and not first:
                    add_residual(b - 1)
                if e == 4 and not last:
                    split_normed(b + 1, 1 - par)
                    mix(b + 1)
                if e == 5 and not last:
                    route_keys(b + 1)
                if e == 6 and not last:
                    route(b + 1)
                    split_mixed(b + 1)
                if e == 7 and not last:
                    keep_comb(b + 1, False)
            if not last:
                gated(b + 1, 1 - par)
            weigh(b, E - 1, first)

        rolled(dve, body)
        product(B - 1, 1)
        add_residual(B - 1)


def run_layer1(nc, ctx, shared, dram):
    from concourse import mybir

    F32, F32R, U32 = mybir.dt.float32, mybir.dt.float32r, mybir.dt.uint32
    ALU, ACT, AX = mybir.AluOpType, mybir.ActivationFunctionType, mybir.AxisListType

    def sb(name, shape, dt=F32):
        return ctx.enter_context(nc.sbuf_tensor("l1_" + name, shape, dt))

    def sem(name):
        return ctx.enter_context(nc.semaphore("l1_" + name))

    P = 128
    B, S = dram["x"].shape[:2]
    J = S // P
    E = 8
    C = 4
    N = E * C
    RING = 2 * C
    HID = 2
    BANKS = 3
    NS = 16
    PER = NS // E
    HALF = 8
    RX = 3
    R = dram["wxr"].shape[0]
    LO_ON_POOL = (0, 2, 3)
    LN_EPS, TEMP = 1e-5, 0.9

    w1h, w1l, w2h, w2l = (shared[k] for k in ("w1h", "w1l", "w2h", "w2l"))
    hh, hl = shared["hh"], shared["hl"]
    t, acc = shared["t"], shared["acc"]
    ident, iota8 = shared["ident"], shared["iota8"]
    PH, PY, G = shared["PH"][0:3], shared["PY"], shared["G"][0:2]
    PB, PC = shared["PH"][3], shared["G"][2]

    CB1, CB2 = 0, E * C
    CBDT, CBOUT, CA = CB2 + E, CB2 + E + 1, CB2 + E + 2
    cols = sb("cols", [P, CA + NS])
    aneg = sb("aneg", [P, NS])
    gb = sb("gb", [P, J, E])
    lng, lnb = sb("lng", [P, P]), sb("lnb", [P, P])
    gw = sb("gw", [P, E])
    half = sb("half", [P, J])
    hid = [sb(f"hid{i}", [P, S]) for i in range(HID)]
    gate = [sb(f"gate{i}", [P, S]) for i in range(2)]
    wth, wtl = sb("wth", [P, P], F32R), sb("wtl", [P, P], F32R)
    woh, wol = sb("woh", [P, P], F32R), sb("wol", [P, P], F32R)
    wsh, wsl = sb("wsh", [P, 4, P], F32R), sb("wsl", [P, 4, P], F32R)
    pick = sb("pick", [P, HALF, P], F32R)
    nh = [sb(f"nh{i}", [P, S], F32R) for i in range(2)]
    nl = [sb(f"nl{i}", [P, S], F32R) for i in range(2)]
    xn, xT = sb("xn", [P, J, P]), sb("xT", [P, S])
    dt, u = sb("dt", [P, S]), sb("u", [P, S])
    soft = sb("soft", [P, S])
    abar = sb("abar", [P, NS, S])
    bch, bcl = sb("bch", [P, 4, S], F32R), sb("bcl", [P, 4, S], F32R)
    bx = [sb(f"bx{i}", [P, S]) for i in range(RX)]
    y = sb("y", [P, S])
    yh, yl = sb("yh", [P, S], F32R), sb("yl", [P, S], F32R)
    s1 = sb("s1", [P, S])
    z, tz = sb("z", [P, J, P]), sb("tz", [P, J, P])
    xres = sb("xres", [P, J, P])
    st, mv = sb("st", [P, J, 6]), sb("mv", [P, J, 2])
    st2, mv2 = sb("st2", [P, J, 6]), sb("mv2", [P, J, 2])
    var, rstd = sb("var", [P, 2, J]), sb("rstd", [P, 2, J])
    lg, eq = sb("lg", [P, J, E]), sb("eq", [P, J, 2, E])
    top, idx = sb("top", [P, J, 8]), sb("idx", [P, J, 8], U32)
    idxf, gap, th = sb("idxf", [P, J, 2]), sb("gap", [P, J, 1]), sb("th", [P, J, 2])
    comb = sb("comb", [P, J, E])
    combT = xn[0:E, :, :].rearrange("p j d -> p (j d)")
    stage = [abar[:, 2 * i:2 * i + 2, :].rearrange("p k n -> p (k n)") for i in range(3)]
    wtmp = abar[:, 6:9, :].rearrange("p k (m n) -> p (k m) n", n=P)
    wset = abar[:, 9:10, :].rearrange("p k (m n) -> p (k m) n", n=P)
    wx64 = abar[0:R, 10:11, 0:2 * P].rearrange("p k (m n) -> p (k m) n", n=P)
    picks = abar[:, 12:14, :].rearrange("p k (m n) -> p (k m) n", n=P)

    cols_in, w_in = sem("cols_in"), sem("w_in")
    stage_in = [sem(f"stage_in{i}") for i in range(3)]
    hi_made, lo_made = sem("w_hi_made"), sem("w_lo_made")
    half_made = sem("half_made")
    wt_done, small_made = sem("wt_done"), sem("small_made")
    small_hi, small_lo = sem("small_hi"), sem("small_lo")
    a_made = sem("a_made")
    xin_in, xres_in = sem("xin_in"), sem("xres_in")
    prep, tail = sem("prep_step"), sem("tail_step")
    var_made, rstd_made = sem("var_made"), sem("rstd_made")
    tvar_made, trstd_made = sem("tail_var_made"), sem("tail_rstd_made")
    xn_made, xposed, nT_made, nl_made = sem("xn_made"), sem("x_transposed"), sem("nT_made"), sem("nl_made")
    logits_done, gap_made, th_made = sem("logits_done"), sem("gap_made"), sem("th_made")
    comb_made, combT_done, combT_made, comb_out = sem("comb_made"), sem("combT_done"), sem("combT_made"), sem("comb_out")
    dt_done, v_made, e_made, e1_made, ln_made = sem("dt_done"), sem("v_made"), sem("e_made"), sem("e1_made"), sem("ln_made")
    left_out, log_made = sem("left_out"), sem("log_made")
    dt_made, u_made, abar_made = sem("dt_made"), sem("u_made"), sem("abar_made")
    set_done, set_hi, set_lo = sem("set_done"), sem("set_hi"), sem("set_lo")
    b_done, c_done, bx_made, scan_made, m_made, y_made = (
        sem("b_done"), sem("c_done"), sem("bx_made"), sem("scan_made"), sem("m_made"), sem("y_made"))
    yh_made, yl_made, wout_done, s1_made = sem("yh_made"), sem("yl_made"), sem("wout_done"), sem("s1_made")
    gate_in = [sem(f"gate_in{i}") for i in range(len(gate))]
    up_done, hid_made, lo_dve, lo_pool = sem("up_done"), sem("hid_made"), sem("lo_dve"), sem("lo_pool")
    y2_done, t_made, acc_made = sem("expert_done"), sem("t_made"), sem("acc_made")
    accT_done, s1T_done, z_made, tz_made = sem("accT_done"), sem("s1T_done"), sem("z_made"), sem("tz_made")
    xo_made, xo_out = sem("xo_made"), sem("xo_out")

    dve_passed, sp_passed = sem("dve_passed"), sem("sp_passed")

    NP = len(LO_ON_POOL)
    ND = C - NP
    PREP, TAIL = 9, 6
    OWN = [c for c in range(C) if c not in LO_ON_POOL]

    def slot_of(e, c):
        return (e * C + c) % RING

    def lo_ready(eng, b, e, c):
        if c in LO_ON_POOL:
            eng.wait_ge(lo_pool, (b * E + e) * NP + LO_ON_POOL.index(c) + 1)
        else:
            eng.wait_ge(lo_dve, (b * E + e) * ND + OWN.index(c) + 1)

    x1_tok = dram["x1"].rearrange("b (j p) d -> b p j d", p=P)
    out_tok = dram["out"].rearrange("b (j p) d -> b p j d", p=P)

    def chained(eng, s, per):
        def step(b, n, ins):
            assert 1 <= n <= per
            ins.then_inc(s, 1)
            eng.wait_ge(s, b * per + n)
        return step

    def apart(eng, passed):
        eng.sem_inc(passed, 1)

    def rolled(eng, body):
        body(0, 0, True, False)
        with eng.Fori(0, (B - 2) // 2) as k:
            body(2 * k + 1, 1, False, False)
            body(2 * k + 2, 0, False, False)
        body(B - 1, 1, False, True)

    block = ctx.enter_context(nc.Block())

    @block.sync
    def _(sp):
        def load_x(b, first):
            if not first:
                sp.wait_ge(xposed, b)
                apart(sp, sp_passed)
            sp.dma_start(xn[:, :, :], x1_tok[b]).then_inc(xin_in, 16)

        def load_gate(b, e, first):
            s = e % len(gate)
            if e >= len(gate) or not first:
                sp.wait_ge(t_made, b * E + e - len(gate) + 1)
            apart(sp, sp_passed)
            sp.dma_start(gate[s][:, :], dram["comb1"][b, e].partition_broadcast(P)).then_inc(gate_in[s], 16)

        def store_comb(b):
            sp.wait_ge(combT_made, b + 1)
            apart(sp, sp_passed)
            sp.dma_start(dram["comb1"][b], combT).then_inc(comb_out, 16)

        def load_residual(b):
            sp.wait_ge(xo_out, 16 * (b + 1))
            apart(sp, sp_passed)
            sp.dma_start(xres[:, :, :], x1_tok[b]).then_inc(xres_in, 16)

        def store_out(b):
            sp.wait_ge(xo_made, b + 1)
            apart(sp, sp_passed)
            sp.dma_start(out_tok[b], xres[:, :, :]).then_inc(xo_out, 16)

        sp.sem_inc(xo_out, 16)
        load_x(0, True)
        for dst, name in ((cols[:, :], "cols1"), (gb[:, :, :].rearrange("p j e -> p (j e)"), "gb"), (lng[:, :], "lng"),
                          (lnb[:, :], "lnb"), (gw[:, :], "gw")):
            sp.dma_start(dst, dram[name]).then_inc(cols_in, 16)
        sp.dma_start(wtmp[:, 0, :], dram["mask"]).then_inc(w_in, 16)
        sp.dma_start(wtmp[:, 1, :], dram["wout"]).then_inc(w_in, 16)
        sp.dma_start(wset[:, :, :], dram["ws"].rearrange("k p n -> p k n")).then_inc(w_in, 16)
        sp.dma_start(wx64[:, 0, :], dram["wxr"]).then_inc(w_in, 16)
        sp.dma_start(wx64[:, 1, :], dram["wdt"]).then_inc(w_in, 16)
        sp.dma_start(picks[:, :, :], dram["pick"].rearrange("k p n -> p k n")).then_inc(w_in, 16)
        for e in range(E):
            s = e % 3
            if e >= 3:
                sp.wait_ge(hi_made, e - 2)
                sp.wait_ge(lo_made, e - 2)
            sp.dma_start(stage[s][:, 0:C * P], dram["w1"][e]).then_inc(stage_in[s], 16)
            sp.dma_start(stage[s][:, C * P:].rearrange("p (c n) -> p c n", c=C),
                         dram["w2"][e].rearrange("(c p) n -> p c n", p=P)).then_inc(stage_in[s], 16)
        store_comb(0)

        def body(b, par, first, last):
            sp.wait_ge(comb_out, 16 * (b + 1))
            apart(sp, sp_passed)
            for e in range(E):
                load_gate(b, e, first)
                if e == 1:
                    if not last:
                        load_x(b + 1, False)
                    if not first:
                        load_residual(b - 1)
                if e == 4 and not first:
                    store_out(b - 1)
            if not last:
                store_comb(b + 1)

        rolled(sp, body)
        load_residual(B - 1)
        store_out(B - 1)
        sp.wait_ge(xo_out, 16 * (B + 1))

    @block.tensor
    def _(pe):
        def three_pass(out, wh, wl, h, l, start=True, stop=True):
            pe.matmul(out, wh, h, start=start, stop=False)
            pe.matmul(out, wl, h, start=False, stop=False)
            return pe.matmul(out, wh, l, start=False, stop=stop)

        def up(b, par, e, c, first):
            k = e * C + c
            if k == 0:
                pe.wait_ge(nl_made, b + 1)
            if first and c == 0:
                pe.wait_ge(hi_made, e + 1)
                pe.wait_ge(lo_made, e + 1)
            if k >= BANKS:
                pe.wait_ge(hid_made, b * N + k - BANKS + 1)
            elif not first:
                before = max(n for n in range(N) if n % BANKS == k)
                pe.wait_ge(hid_made, (b - 1) * N + before + 1)
            w = slice(c * P, (c + 1) * P)
            three_pass(PH[k % BANKS][:, :], w1h[:, e, w], w1l[:, e, w], nh[par][:, :], nl[par][:, :]).then_inc(up_done, 1)

        def down(b, e, first):
            if not (first and e == 0):
                pe.wait_ge(t_made, b * E + e)
            for c in range(C):
                lo_ready(pe, b, e, c)
                s = slot_of(e, c)
                last = three_pass(PY[:, :], w2h[:, e * C + c, :], w2l[:, e * C + c, :], hh[s][:, :], hl[s][:, :],
                                  c == 0, c == C - 1)
            last.then_inc(y2_done, 1)

        def spread(b, n, k, bank, done, read):
            if n == 0:
                pe.wait_ge(set_lo, 4 * (b + 1))
            else:
                pe.wait_ge(read, b * NS + n)
            s = 2 * k + n // HALF
            pe.matmul(bank[:, :], pick[:, n % HALF, :], bch[:, s, :], start=True, stop=False)
            pe.matmul(bank[:, :], pick[:, n % HALF, :], bcl[:, s, :], start=False, stop=True).then_inc(done, 1)

        def spread_b(b, n):
            spread(b, n, 0, PB, b_done, bx_made)

        def spread_c(b, n):
            spread(b, n, 1, PC, c_done, m_made)

        def compact(b, par, first):
            if not first:
                pe.wait_ge(bx_made, b * NS)
                pe.wait_ge(m_made, b * NS)
            for s, bank in enumerate((PB, PC, G[0], G[1])):
                if s == 2:
                    pe.wait_ge(gap_made, b + 1)
                if s == 3:
                    pe.wait_ge(v_made, b + 1)
                three_pass(bank[:, :], wsh[:, s, :], wsl[:, s, :], nh[par][:, :], nl[par][:, :]).then_inc(set_done, 1)

        def step_sizes(b, par):
            pe.wait_ge(nl_made, b + 1)
            three_pass(G[1][:, :], wth[:, :], wtl[:, :], nh[par][:, :], nl[par][:, :]).then_inc(dt_done, 1)

        def transposes(dst, src, s):
            for j in range(J):
                last = pe.transpose(dst[:, j * P:(j + 1) * P], src[:, j * P:(j + 1) * P], ident[:, :])
            last.then_inc(s, 1)

        def transpose_x(b, first):
            pe.wait_ge(xn_made, b + 1)
            if not first:
                pe.wait_ge(z_made, b - 1)
            transposes(G[1], xn[:, :, :].rearrange("p j d -> p (j d)"), xposed)

        def logits(b, first):
            pe.wait_ge(nT_made, b + 1)
            if not first:
                pe.wait_ge(xo_made, b - 1)
            for j in range(J):
                last = pe.matmul(G[0][:, j * E:(j + 1) * E], xT[:, j * P:(j + 1) * P], gw[:, :], start=True, stop=True)
            last.then_inc(logits_done, 1)

        def transpose_comb(b):
            pe.wait_ge(comb_made, b + 1)
            pe.wait_ge(set_hi, 4 * (b + 1))
            for j in range(J):
                last = pe.transpose(G[0][0:E, j * P:(j + 1) * P], comb[:, j, :], ident[:, :])
            last.then_inc(combT_done, 1)

        def project(b):
            pe.wait_ge(yl_made, b + 1)
            pe.wait_ge(combT_made, b + 1)
            three_pass(G[0][:, :], woh[:, :], wol[:, :], yh[:, :], yl[:, :]).then_inc(wout_done, 1)

        def transpose_acc(b):
            pe.wait_ge(acc_made, (b + 1) * (E - 1))
            transposes(G[1], acc, accT_done)

        def transpose_s1(b):
            pe.wait_ge(s1_made, b + 1)
            transposes(G[0], s1, s1T_done)

        pe.sem_inc(s1T_done, 1)
        pe.wait_ge(w_in, 16 * 6)
        pe.matmul(G[0][:, 0:P], wx64[:, 0, :], wx64[:, 1, :], start=True, stop=True).then_inc(wt_done, 1)
        pe.wait_ge(cols_in, 16 * 5)
        transpose_x(0, True)
        pe.wait_ge(small_lo, 1)
        logits(0, True)
        step_sizes(0, 0)
        compact(0, 0, True)
        transpose_comb(0)

        def body(b, par, first, last):
            for e in range(E):
                for c in range(C):
                    up(b, par, e, c, first)
                    n = e * PER + c // 2
                    (spread_b, spread_c)[c % 2](b, n)
                if e == 0 and not first:
                    pe.wait_ge(combT_made, b + 1)
                    project(b - 1)
                if e == 1 and not first:
                    pe.wait_ge(set_hi, 4 * (b + 1))
                    transpose_acc(b - 1)
                if e == 2 and not first:
                    transpose_s1(b - 1)
                if e == 3 and not last:
                    if first:
                        pe.wait_ge(set_hi, 4 * (b + 1))
                    else:
                        pe.wait_ge(z_made, b)
                    transpose_x(b + 1, False)
                if e == 5 and not last:
                    if not first:
                        pe.wait_ge(xo_made, b)
                    else:
                        pe.wait_ge(combT_made, b + 1)
                    logits(b + 1, False)
                    step_sizes(b + 1, 1 - par)
                if e > 0:
                    down(b, e - 1, first)
            if not last:
                compact(b + 1, 1 - par, False)
            down(b, E - 1, first)
            if not last:
                transpose_comb(b + 1)

        rolled(pe, body)
        pe.wait_ge(yl_made, B)
        three_pass(G[0][:, :], woh[:, :], wol[:, :], yh[:, :], yl[:, :]).then_inc(wout_done, 1)
        transpose_acc(B - 1)
        transpose_s1(B - 1)

    @block.scalar
    def _(act):
        def hidden(b, e, first):
            for c in range(C):
                k = e * C + c
                act.wait_ge(up_done, b * N + k + 1)
                if not (first and e < 2):
                    act.wait_ge(y2_done, b * E + e - 1)
                if k >= HID:
                    lo_ready(act, b, (k - HID) // C, (k - HID) % C)
                elif not first:
                    lo_ready(act, b - 1, E - 1, C - HID + k)
                bias = cols[:, CB1 + k:CB1 + k + 1]
                act.activation(hh[slot_of(e, c)][:, :], PH[k % BANKS][:, :], ACT.Gelu, bias=bias)
                act.activation(hid[c % HID][:, :], PH[k % BANKS][:, :], ACT.Gelu, bias=bias).then_inc(hid_made, 1)

        def evacuate_x(b, par, first):
            act.wait_ge(xposed, b + 1)
            if not first:
                act.wait_ge(u_made, b)
                act.wait_ge(logits_done, b)
            act.activation(xT[:, :], G[1][:, :], ACT.Identity)
            act.activation(nh[par][:, :], G[1][:, :], ACT.Identity).then_inc(nT_made, 1)

        def gate_tanh(b):
            act.wait_ge(gap_made, b + 1)
            act.activation(th[:, :, 0:1], gap[:, :, :], ACT.Tanh, scale=0.5 / TEMP).then_inc(th_made, 1)

        def window(b, first):
            act.wait_ge(v_made, b + 1)
            act.activation(soft[:, :], soft[:, :], ACT.Exp).then_inc(e_made, 1)
            for s, bank in enumerate((PB, PC)):
                evacuate_set(b, s, bank, first)
            act.wait_ge(e1_made, b + 1)
            if not first:
                act.wait_ge(s1T_done, b)
            act.activation(s1[:, :], u[:, :], ACT.Ln).then_inc(ln_made, 1)
            evacuate_set(b, 2, G[0], first)
            act.wait_ge(dt_made, b + 1)
            if first:
                act.wait_ge(lo_made, E)
            for n in range(NS):
                if not first:
                    act.wait_ge(scan_made, (b - 1) * NS + n + 1)
                act.activation(abar[:, n, :], dt[:, :], ACT.Exp, scale=aneg[:, n:n + 1]).then_inc(abar_made, 1)
                if n == 3:
                    evacuate_set(b, 3, G[1], first)

        def evacuate_set(b, s, bank, first):
            act.wait_ge(set_done, 4 * b + s + 1)
            if not first and s % 2 == 0:
                act.wait_ge(c_done, b * NS)
            if s > 0 or not first:
                act.wait_ge(set_lo, 4 * b + s)
            act.activation(bch[:, s, :], bank[:, :], ACT.Identity)
            act.activation(tz[:, :, :].rearrange("p j d -> p (j d)"), bank[:, :], ACT.Identity).then_inc(set_hi, 1)

        def split_y(b, first):
            act.wait_ge(y_made, (b + 1) * (NS - 1))
            if not first:
                act.wait_ge(wout_done, b)
            act.activation(yh[:, :], y[:, :], ACT.Identity).then_inc(yh_made, 1)

        def evacuate_s1(b, first):
            act.wait_ge(wout_done, b + 1)
            if not first:
                act.wait_ge(s1T_done, b + 1)
            act.activation(s1[:, :], G[0][:, :], ACT.Identity, bias=cols[:, CBOUT:CBOUT + 1]).then_inc(s1_made, 1)

        def tanh_z(b):
            act.wait_ge(z_made, b + 1)
            act.activation(tz[:, :, :], z[:, :, :], ACT.Tanh, scale=0.5).then_inc(tz_made, 1)

        act.wait_ge(cols_in, 16 * 5)
        act.activation(aneg[:, :], cols[:, CA:CA + NS], ACT.Exp).then_inc(a_made, 1)
        act.wait_ge(small_made, 1)
        act.activation(wth[:, :], wtmp[:, 2, :], ACT.Identity)
        act.activation(woh[:, :], wtmp[:, 1, :], ACT.Identity)
        act.activation(wsh[:, :, :], wset[:, :, :], ACT.Identity)
        act.activation(pick[:, :, :], picks[:, :, :], ACT.Identity).then_inc(small_hi, 1)
        evacuate_x(0, 0, True)
        for e in range(E):
            act.wait_ge(stage_in[e % 3], 32 * (e // 3 + 1))
            act.activation(w1h[:, e, :], stage[e % 3][:, 0:C * P], ACT.Identity)
            act.activation(w2h[:, e * C:(e + 1) * C, :], stage[e % 3][:, C * P:].rearrange("p (c n) -> p c n", c=C),
                           ACT.Identity).then_inc(hi_made, 1)
        gate_tanh(0)
        window(0, True)

        def body(b, par, first, last):
            for e in range(E):
                hidden(b, e, first)
                if e == 0 and not first:
                    evacuate_s1(b - 1, False)
                if e == 2 and not first:
                    tanh_z(b - 1)
                if e == 3 and not last:
                    evacuate_x(b + 1, 1 - par, False)
                if e == 6 and not last:
                    gate_tanh(b + 1)
            if not last:
                window(b + 1, False)
            split_y(b, first)

        rolled(act, body)
        evacuate_s1(B - 1, False)
        tanh_z(B - 1)

    @block.gpsimd
    def _(pool):
        def power(b, k, made, done):
            pool.wait_ge(made, b + 1)
            pool.tensor_tensor(rstd[:, k, :], var[:, k, :], half[:, :], ALU.pow).then_inc(done, 1)

        def low_part(b, e):
            for c in LO_ON_POOL:
                s = slot_of(e, c)
                pool.wait_ge(hid_made, b * N + e * C + c + 1)
                pool.tensor_tensor(hl[s][:, :], hid[c % HID][:, :], hh[s][:, :].bitcast(F32), ALU.subtract).then_inc(lo_pool, 1)

        def accumulate(b, e):
            pool.wait_ge(t_made, b * E + e + 1)
            if e >= 2:
                pool.wait_ge(acc_made, b * (E - 1) + e - 1)
            pool.tensor_tensor(acc[:, :], acc[:, :], t[e % 2][:, :], ALU.add).then_inc(acc_made, 1)

        def sum_states(b, n):
            if n == 0:
                return
            pool.wait_ge(m_made, b * NS + n + 1)
            if n >= 2:
                pool.wait_ge(y_made, b * (NS - 1) + n - 1)
            pool.tensor_tensor(y[:, :], y[:, :], bx[n % RX][:, :], ALU.add).then_inc(y_made, 1)

        pool.memset(half[:, :], -0.5).then_inc(half_made, 1)
        pool.wait_ge(half_made, 1)
        power(0, 0, var_made, rstd_made)
        for e in range(E):
            pool.wait_ge(hi_made, e + 1)
            pool.tensor_tensor(w1l[:, e, :], stage[e % 3][:, 0:C * P], w1h[:, e, :].bitcast(F32), ALU.subtract)
            pool.tensor_tensor(w2l[:, e * C:(e + 1) * C, :], stage[e % 3][:, C * P:].rearrange("p (c n) -> p c n", c=C),
                               w2h[:, e * C:(e + 1) * C, :].bitcast(F32), ALU.subtract).then_inc(lo_made, 1)

        def body(b, par, first, last):
            for e in range(E):
                low_part(b, e)
                sum_states(b, PER * e)
                sum_states(b, PER * e + 1)
                if e >= 2:
                    accumulate(b, e - 1)
                if e == 1 and not first:
                    power(b - 1, 1, tvar_made, trstd_made)
                if e == 1 and not last:
                    power(b + 1, 0, var_made, rstd_made)
            accumulate(b, E - 1)

        rolled(pool, body)
        power(B - 1, 1, tvar_made, trstd_made)

    @block.vector
    def _(dve):
        chain, tchain = chained(dve, prep, PREP), chained(dve, tail, TAIL)

        def low_part(b, e):
            for c in OWN:
                s = slot_of(e, c)
                dve.wait_ge(hid_made, b * N + e * C + c + 1)
                dve.tensor_tensor(hl[s][:, :], hid[c % HID][:, :], hh[s][:, :].bitcast(F32), ALU.subtract).then_inc(lo_dve, 1)

        def weigh(b, e, first):
            dve.wait_ge(y2_done, b * E + e + 1)
            s = e % len(gate)
            dve.wait_ge(gate_in[s], 16 * (b * (E // len(gate)) + e // len(gate) + 1))
            if e == 0:
                out = acc
                if not first:
                    dve.wait_ge(accT_done, b)
            else:
                out = t[e % 2]
                if e >= 3:
                    dve.wait_ge(acc_made, b * (E - 1) + e - 2)
                elif not first:
                    dve.wait_ge(acc_made, b * (E - 1))
            dve.scalar_tensor_tensor(out[:, :], PY[:, :], cols[:, CB2 + e:CB2 + e + 1], gate[s][:, :],
                                     ALU.add, ALU.mult).then_inc(t_made, 1)

        def states_in(b, n, first):
            dve.wait_ge(b_done, b * NS + n + 1)
            if n == 0:
                dve.wait_ge(u_made, b + 1)
            if n > RX:
                dve.wait_ge(y_made, b * (NS - 1) + n - RX)
            elif not first:
                dve.wait_ge(y_made, b * (NS - 1))
            dve.tensor_tensor(bx[n % RX][:, :], u[:, :], PB[:, :], ALU.mult).then_inc(bx_made, 1)

        def state_scan(b, n):
            dve.wait_ge(bx_made, b * NS + n + 1)
            dve.wait_ge(abar_made, b * NS + n + 1)
            dve.tensor_tensor_scan(bx[n % RX][:, :], abar[:, n, :], bx[n % RX][:, :], 0.0,
                                   ALU.mult, ALU.add).then_inc(scan_made, 1)

        def states_out(b, n, first):
            dve.wait_ge(scan_made, b * NS + n + 1)
            dve.wait_ge(c_done, b * NS + n + 1)
            out = y if n == 0 else bx[n % RX]
            if n == 0 and not first:
                dve.wait_ge(yl_made, b)
            dve.tensor_tensor(out[:, :], bx[n % RX][:, :], PC[:, :], ALU.mult).then_inc(m_made, 1)

        def normalise(b):
            dve.wait_ge(xin_in, 16 * (b + 1))
            for j in range(J):
                i = dve.bn_stats(st[:, j, :], xn[:, j, :])
            chain(b, 1, i)
            apart(dve, dve_passed)
            for j in range(J):
                i = dve.bn_aggr(mv[:, j, :], st[:, j, :])
            chain(b, 2, i)
            dve.tensor_scalar(var[:, 0, :], mv[:, :, 1], LN_EPS, None, ALU.add).then_inc(var_made, 1)

        def normalise2(b):
            dve.wait_ge(rstd_made, b + 1)
            for j in range(J):
                i = dve.tensor_scalar(xn[:, j, :], xn[:, j, :], mv[:, j, 0:1], rstd[:, 0, j:j + 1],
                                      ALU.subtract, ALU.mult)
            i.then_inc(xn_made, 1)

        def split_normed(b, par):
            dve.wait_ge(nT_made, b + 1)
            dve.tensor_tensor(nl[par][:, :], xT[:, :], nh[par][:, :].bitcast(F32), ALU.subtract).then_inc(nl_made, 1)

        def route(b):
            dve.wait_ge(logits_done, b + 1)
            chain(b, 3, dve.tensor_tensor(lg[:, :, :], G[0][:, 0:J * E].rearrange("p (j e) -> p j e", j=J), gb[:, :, :],
                                          ALU.add))
            apart(dve, dve_passed)
            for j in range(J):
                i = dve.max(top[:, j, :], lg[:, j, :])
            chain(b, 4, i)
            dve.tensor_tensor(gap[:, :, :], top[:, :, 0:1], top[:, :, 1:2], ALU.subtract).then_inc(gap_made, 1)
            apart(dve, dve_passed)
            for j in range(J):
                i = dve.max_index(idx[:, j, :], top[:, j, :], lg[:, j, :])
            chain(b, 5, i)
            chain(b, 6, dve.tensor_copy(idxf[:, :, :], idx[:, :, 0:2]))

        def softmax_of_two(b):
            dve.wait_ge(th_made, b + 1)
            for k in range(2):
                dve.tensor_tensor(eq[:, :, k, :], iota8[:, :].rearrange("p (j e) -> p j e", j=J),
                                  idxf[:, :, k:k + 1].to_broadcast([P, J, E]), ALU.is_equal)
            dve.tensor_scalar(th[:, :, 1:2], th[:, :, 0:1], -0.5, 0.5, ALU.mult, ALU.add)
            chain(b, 8, dve.tensor_scalar(gap[:, :, :], th[:, :, 0:1], 0.5, 0.5, ALU.mult, ALU.add))
            dve.tensor_tensor(eq[:, :, 1, :], eq[:, :, 1, :], th[:, :, 1:2].to_broadcast([P, J, E]), ALU.mult)
            chain(b, 9, dve.tensor_tensor(eq[:, :, 0, :], eq[:, :, 0, :], gap[:, :, :].to_broadcast([P, J, E]), ALU.mult))
            dve.tensor_tensor(comb[:, :, :], eq[:, :, 0, :], eq[:, :, 1, :], ALU.add).then_inc(comb_made, 1)

        def keep_comb(b, first):
            dve.wait_ge(combT_done, b + 1)
            if not first:
                dve.wait_ge(comb_out, 16 * b)
            dve.tensor_copy(combT, G[0][0:E, :]).then_inc(combT_made, 1)

        def step_in(b, first):
            dve.wait_ge(dt_done, b + 1)
            if not first:
                dve.wait_ge(abar_made, b * NS)
            chain(b, 7, dve.tensor_scalar(dt[:, :], G[1][:, :], cols[:, CBDT:CBDT + 1], None, ALU.add))
            dve.scalar_tensor_tensor(soft[:, :], dt[:, :], -1.0, dt[:, :], ALU.mult, ALU.min).then_inc(v_made, 1)

        def split_set(b, s):
            dve.wait_ge(set_hi, 4 * b + s + 1)
            dve.tensor_tensor(bcl[:, s, :], tz[:, :, :].rearrange("p j d -> p (j d)"), bch[:, s, :].bitcast(F32),
                              ALU.subtract).then_inc(set_lo, 1)

        def softplus(b, first):
            dve.wait_ge(e_made, b + 1)
            if not first:
                dve.wait_ge(bx_made, b * NS)
            dve.tensor_scalar(u[:, :], soft[:, :], 1.0, None, ALU.add).then_inc(e1_made, 1)
            split_set(b, 0)
            split_set(b, 1)
            dve.wait_ge(e1_made, b + 1)
            dve.scalar_tensor_tensor(soft[:, :], u[:, :], 1.0, soft[:, :], ALU.subtract,
                                     ALU.subtract).then_inc(left_out, 1)
            dve.wait_ge(left_out, b + 1)
            dve.wait_ge(ln_made, b + 1)
            dve.tensor_tensor(soft[:, :], s1[:, :], soft[:, :], ALU.subtract).then_inc(log_made, 1)
            dve.wait_ge(log_made, b + 1)
            dve.scalar_tensor_tensor(dt[:, :], dt[:, :], 0.0, soft[:, :], ALU.max, ALU.add).then_inc(dt_made, 1)
            dve.wait_ge(dt_made, b + 1)
            dve.tensor_tensor(u[:, :], dt[:, :], xT[:, :], ALU.mult).then_inc(u_made, 1)
            split_set(b, 2)
            split_set(b, 3)

        def split_y(b):
            dve.wait_ge(yh_made, b + 1)
            dve.tensor_tensor(yl[:, :], y[:, :], yh[:, :].bitcast(F32), ALU.subtract).then_inc(yl_made, 1)

        def norm_experts(b):
            dve.wait_ge(accT_done, b + 1)
            for j in range(J):
                i = dve.bn_stats(st2[:, j, :], G[1][:, j * P:(j + 1) * P])
            tchain(b, 1, i)
            apart(dve, dve_passed)
            for j in range(J):
                i = dve.bn_aggr(mv2[:, j, :], st2[:, j, :])
            tchain(b, 2, i)
            dve.tensor_scalar(var[:, 1, :], mv2[:, :, 1], LN_EPS, None, ALU.add).then_inc(tvar_made, 1)

        def norm_experts2(b):
            dve.wait_ge(trstd_made, b + 1)
            for j in range(J):
                i = dve.tensor_scalar(z[:, j, :], G[1][:, j * P:(j + 1) * P], mv2[:, j, 0:1], rstd[:, 1, j:j + 1],
                                      ALU.subtract, ALU.mult)
            tchain(b, 3, i)
            tchain(b, 4, dve.tensor_tensor(z[:, :, :], z[:, :, :], lng[:, None, :].to_broadcast([P, J, P]), ALU.mult))
            dve.tensor_tensor(z[:, :, :], z[:, :, :], lnb[:, None, :].to_broadcast([P, J, P]), ALU.add).then_inc(z_made, 1)

        def finish(b):
            dve.wait_ge(tz_made, b + 1)
            tchain(b, 5, dve.scalar_tensor_tensor(z[:, :, :], tz[:, :, :], 1.0, z[:, :, :], ALU.add, ALU.mult))
            dve.wait_ge(s1T_done, b + 2)
            tchain(b, 6, dve.scalar_tensor_tensor(z[:, :, :], z[:, :, :], 0.5,
                                                  G[0][:, :].rearrange("p (j d) -> p j d", j=J), ALU.mult, ALU.mult))
            dve.wait_ge(xres_in, 16 * (b + 1))
            dve.tensor_tensor(xres[:, :, :], xres[:, :, :], z[:, :, :], ALU.add).then_inc(xo_made, 1)

        dve.wait_ge(cols_in, 16 * 5)
        dve.wait_ge(half_made, 1)
        normalise(0)
        normalise2(0)
        dve.wait_ge(a_made, 1)
        dve.tensor_scalar(aneg[:, :], aneg[:, :], -1.0, None, ALU.mult)
        dve.wait_ge(w_in, 16 * 6)
        dve.wait_ge(wt_done, 1)
        dve.tensor_tensor(wtmp[:, 2, :], G[0][:, 0:P], wtmp[:, 0, :], ALU.mult)
        dve.tensor_tensor(wset[:, :, :], wset[:, :, :], wtmp[:, 0:1, :].to_broadcast([P, 4, P]),
                          ALU.mult).then_inc(small_made, 1)
        dve.wait_ge(small_hi, 1)
        dve.tensor_tensor(wtl[:, :], wtmp[:, 2, :], wth[:, :].bitcast(F32), ALU.subtract)
        dve.tensor_tensor(wol[:, :], wtmp[:, 1, :], woh[:, :].bitcast(F32), ALU.subtract)
        dve.tensor_tensor(wsl[:, :, :], wset[:, :, :], wsh[:, :, :].bitcast(F32), ALU.subtract).then_inc(small_lo, 1)
        split_normed(0, 0)
        route(0)
        step_in(0, True)
        softmax_of_two(0)
        softplus(0, True)
        keep_comb(0, True)

        def body(b, par, first, last):
            for e in range(E):
                for n in (PER * e, PER * e + 1):
                    states_in(b, n, first)
                    state_scan(b, n)
                    states_out(b, n, first)
                low_part(b, e)
                if e > 0:
                    weigh(b, e - 1, first)
                if e == 0 and not last:
                    normalise(b + 1)
                if e == 1 and not first:
                    norm_experts(b - 1)
                if e == 2:
                    if not last:
                        normalise2(b + 1)
                    if not first:
                        norm_experts2(b - 1)
                if e == 3 and not first:
                    finish(b - 1)
                if e == 4 and not last:
                    split_normed(b + 1, 1 - par)
                if e == 5 and not last:
                    route(b + 1)
                    step_in(b + 1, False)
                if e == 6 and not last:
                    softmax_of_two(b + 1)
            if not last:
                softplus(b + 1, False)
            weigh(b, E - 1, first)
            if not last:
                keep_comb(b + 1, False)
            split_y(b)

        rolled(dve, body)
        norm_experts(B - 1)
        norm_experts2(B - 1)
        finish(B - 1)


def build_program(nc, dram):
    from contextlib import ExitStack

    from concourse import mybir

    F32, F32R = mybir.dt.float32, mybir.dt.float32r
    P, C = 128, 4
    EXPERTS = dram["ew1"].shape[0]
    S = dram["x"].shape[1]

    with ExitStack() as ctx:
        def sb(name, shape, dt=F32):
            return ctx.enter_context(nc.sbuf_tensor(name, shape, dt))

        def psum(name):
            return ctx.enter_context(nc.psum_tensor(name, [P, 512], F32))

        shared = {
            "w1h": sb("w1h", [P, EXPERTS, C * P], F32R), "w1l": sb("w1l", [P, EXPERTS, C * P], F32R),
            "w2h": sb("w2h", [P, EXPERTS * C, P], F32R), "w2l": sb("w2l", [P, EXPERTS * C, P], F32R),
            "hh": [sb(f"hh{i}", [P, S], F32R) for i in range(2 * C)],
            "hl": [sb(f"hl{i}", [P, S], F32R) for i in range(2 * C)],
            "t": [sb(f"t{i}", [P, S]) for i in range(2)],
            "acc": sb("acc", [P, S]),
            "ident": sb("ident", [P, P]), "iota8": sb("iota8", [P, 4 * EXPERTS]),
            "PH": [psum(f"PH{i}") for i in range(4)], "PY": psum("PY"), "G": [psum(f"G{i}") for i in range(3)],
        }
        with ExitStack() as own:
            run_layer0(nc, own, shared, dram)
        with ExitStack() as own:
            run_layer1(nc, own, shared, dram)


def lay_out(i):
    import numpy as np

    P, HEADS = 128, 16
    E = i["L0_ffn_eb1"].shape[0]
    D_HEAD = P // HEADS
    NS, R = i["L1_attn_A_log"].shape[1], i["L1_attn_Wdt"].shape[1]

    def columns(a):
        return np.asarray(a).reshape(-1, P).T

    def chunks(b):
        return np.asarray(b).reshape(-1, P).T

    wx = np.asarray(i["L1_attn_Wx"])
    head = np.repeat(np.arange(HEADS), D_HEAD)
    place = np.tile(np.arange(D_HEAD), HEADS)
    same_head = head[:, None] == head[None, :]
    out = {
        "x": i["L0_attn_x"],
        "cols0": np.concatenate([chunks(i["L0_ffn_eb1"]), columns(i["L0_ffn_sb1"]), chunks(i["L0_ffn_eb2"]),
                                 columns(i["L0_ffn_sb2"]), columns(i["L0_attn_time_decay"]),
                                 columns(i["L0_attn_time_mix_v"]), columns(i["L0_attn_time_mix_r"]),
                                 columns(i["L0_ffn_norm_weight"])], axis=1),
        "rw": np.asarray(i["L0_ffn_router_w"]).T,
        "ident": np.eye(P, dtype=np.float32),
        "iota8": np.tile(np.arange(E, dtype=np.float32), (P, 4)),
        "wa": np.stack([np.asarray(i["L0_attn_Wv"]), np.asarray(i["L0_attn_Wo"]).T, np.asarray(i["L0_attn_Wr"]).T]),
        "ew1": i["L0_ffn_ew1"], "ew2": i["L0_ffn_ew2"], "sw1": i["L0_ffn_sw1"], "sw2": i["L0_ffn_sw2"],
        "cols1": np.concatenate([chunks(i["L1_ffn_b1"]), chunks(i["L1_ffn_b2"]),
                                 np.tile(np.asarray(i["L1_attn_bdt"]), HEADS)[:, None], columns(i["L1_attn_bout"]),
                                 np.repeat(np.asarray(i["L1_attn_A_log"]), D_HEAD, axis=0)], axis=1),
        "gb": np.tile(np.asarray(i["L1_ffn_gate_b"]), (P, 4)),
        "lng": np.tile(np.asarray(i["L1_ffn_ln_g"]), (P, 1)),
        "lnb": np.tile(np.asarray(i["L1_ffn_ln_b"]), (P, 1)),
        "gw": i["L1_ffn_gate_w"],
        "mask": same_head.astype(np.float32),
        "wout": np.asarray(i["L1_attn_Wout"]).T,
        "ws": np.stack([np.tile(wx[R + k * D_HEAD:R + (k + 1) * D_HEAD].T, (HEADS, HEADS))
                        for k in range(2 * NS // D_HEAD)]),
        "wxr": np.tile(wx[:R], (1, HEADS)),
        "wdt": np.tile(np.asarray(i["L1_attn_Wdt"]).T, (1, HEADS)),
        "pick": np.stack([same_head & (place == n)[:, None] for n in range(D_HEAD)]).astype(np.float32),
        "w1": i["L1_ffn_w1"], "w2": i["L1_ffn_w2"],
    }
    return {name: np.ascontiguousarray(a) for name, a in out.items()}




def kernel(**inputs):
    import concourse.bacc as bacc
    from concourse import mybir
    from concourse.bass_utils import run_bass_kernel_spmd

    nc = bacc.Bacc("TRN2", target_bir_lowering=False, num_devices=1, dynamic_dma_scratch_size=4096)
    arrays = lay_out(inputs)
    dram = {name: nc.dram_tensor("in_" + name, a.shape, mybir.dt.from_np(a.dtype), kind="ExternalInput").ap()
            for name, a in arrays.items()}
    B, S, D = arrays["x"].shape
    E = arrays["ew1"].shape[0]
    f32 = mybir.dt.float32
    dram["x1"] = nc.dram_tensor("x1", (B, S, D), f32, kind="Internal").ap()
    dram["comb0"] = nc.dram_tensor("comb0", (B, E, S), f32, kind="Internal").ap()
    dram["comb1"] = nc.dram_tensor("comb1", (B, E, S), f32, kind="Internal").ap()
    dram["out"] = nc.dram_tensor("out", (B, S, D), f32, kind="ExternalOutput").ap()
    build_program(nc, dram)
    result = run_bass_kernel_spmd(nc, [{"in_" + name: a for name, a in arrays.items()}], core_ids=[0])
    return result.results[0]["out"]
```

```python
def run_layer0(nc, ctx, shared, dram):
    from concourse import mybir

    F32, F32R, U32 = mybir.dt.float32, mybir.dt.float32r, mybir.dt.uint32
    ALU, ACT, AX = mybir.AluOpType, mybir.ActivationFunctionType, mybir.AxisListType

    def sb(name, shape, dt=F32):
        return ctx.enter_context(nc.sbuf_tensor("l0_" + name, shape, dt))

    def sem(name):
        return ctx.enter_context(nc.semaphore("l0_" + name))

    P = 128
    B, S = dram["x"].shape[:2]
    J = S // P
    EXPERTS = 8
    E = EXPERTS + 1
    C = 4
    N = E * C
    RING = 2 * C
    LO_ON_POOL = (1,)
    LN_EPS, RMS_EPS, SUM_EPS = 1e-5, 1e-8, 1e-6

    w1h, w1l, w2h, w2l = (shared[k] for k in ("w1h", "w1l", "w2h", "w2l"))
    hh, hl = shared["hh"], shared["hl"]
    t, acc = shared["t"], shared["acc"]
    ident, iota8 = shared["ident"], shared["iota8"]
    PH, PY, G = shared["PH"], shared["PY"], shared["G"]

    CB1, CB2 = 0, E * C
    CTD, CMV, CMR, CNW = CB2 + E, CB2 + E + 1, CB2 + E + 2, CB2 + E + 3
    cols = sb("cols", [P, CNW + 1])
    hid = [sb(f"hid{i}", [P, S]) for i in range(C)]
    gate = [sb(f"gate{i}", [P, S]) for i in range(4)]
    sw1h, sw1l = sb("sw1h", [P, C * P], F32R), sb("sw1l", [P, C * P], F32R)
    sw2h, sw2l = sb("sw2h", [P, C, P], F32R), sb("sw2l", [P, C, P], F32R)
    stage = [sb(f"stage{i}", [P, 2 * C * P]) for i in range(3)]
    wa = sb("wa", [P, 4, P])
    rw = sb("rw", [P, EXPERTS])
    woh, wol = sb("woh", [P, P], F32R), sb("wol", [P, P], F32R)
    wrh, wrl = sb("wrh", [P, P], F32R), sb("wrl", [P, P], F32R)
    decay = sb("decay", [P, 2])
    half = sb("half", [P, 2 * C])
    xin, xres, xo = sb("xin", [P, J, P]), sb("xres", [P, J, P]), sb("xo", [P, J, P])
    xn, xr, sq = sb("xn", [P, J, P]), sb("xr", [P, J, P]), sb("sq", [P, J, P])
    st, mv = sb("st", [P, J, 6]), sb("mv", [P, J, 2])
    var, rstd = sb("var", [P, 2, J]), sb("rstd", [P, 2, J])
    xT, nT = sb("xT", [P, S]), sb("nT", [P, S])
    nh = [sb(f"nh{i}", [P, S], F32R) for i in range(2)]
    nl = [sb(f"nl{i}", [P, S], F32R) for i in range(2)]
    sums = sb("sums", [P, S + 1])
    dif, vin, rin = sb("dif", [P, S]), sb("vin", [P, S]), sb("rin", [P, S])
    vh, vl, rh, rl = (sb(n, [P, S], F32R) for n in ("vh", "vl", "rh", "rl"))
    tr = sb("tr", [P, S])
    rv = [sb(f"rv{i}", [P, S]) for i in range(2)]
    z, tz, q, prod = sb("z", [P, S]), sb("tz", [P, S]), sb("q", [P, S]), sb("prod", [P, S])
    key, ex = sb("key", [P, J, EXPERTS]), sb("ex", [P, J, EXPERTS])
    prob, eq = sb("prob", [P, J, EXPERTS]), sb("eq", [P, J, 2, EXPERTS])
    top, idx = sb("top", [P, J, 8]), sb("idx", [P, J, 8], U32)
    idxf, sel = sb("idxf", [P, J, 2]), sb("sel", [P, J, EXPERTS])
    tot, comb = sb("tot", [P, 3, J]), sb("comb", [P, J, EXPERTS])
    combT = sb("combT", [EXPERTS, S])

    cols_in, wa_in = sem("cols_in"), sem("wa_in")
    stage_in = [sem(f"stage_in{i}") for i in range(3)]
    hi_made, lo_made = sem("w_hi_made"), sem("w_lo_made")
    set_step = sem("setup_step")
    wvo_done, attn_w = sem("wvo_done"), sem("attn_w_split")
    decay_step, decay_made = sem("decay_step"), sem("decay_made")
    zero_made = sem("zero_made")
    xin_in, xres_in = sem("xin_in"), sem("xres_in")
    prep, tail = sem("prep_step"), sem("tail_step")
    var_made, rstd_made = sem("var_made"), sem("rstd_made")
    xn_made, xposed = sem("xn_made"), sem("x_transposed")
    xT_made, nT_made, nl_made = sem("xT_made"), sem("nT_made"), sem("nl_made")
    logits_done, ex_made = sem("logits_done"), sem("ex_made")
    comb_made, combT_done, combT_made = sem("comb_made"), sem("combT_done"), sem("combT_made")
    comb_out = sem("comb_out")
    mixed, mixed_hi, mixed_lo = sem("mixed"), sem("mixed_hi"), sem("mixed_lo")
    attn_done, tr_made, rv_made = sem("attn_done"), sem("tr_made"), sem("rv_made")
    gate_in = [sem(f"gate_in{i}") for i in range(len(gate))]
    up_done, hid_made = sem("up_done"), sem("hid_made")
    lo_dve, lo_pool = sem("lo_dve"), sem("lo_pool")
    y_done, t_made, acc_made = sem("y_done"), sem("t_made"), sem("acc_made")
    z_made, tz_made, prod_made = sem("z_made"), sem("tz_made"), sem("prod_made")
    prodT_done, xo_made, xo_out = sem("prodT_done"), sem("xo_made"), sem("xo_out")

    dve_passed, sp_passed = sem("dve_passed"), sem("sp_passed")

    NP = len(LO_ON_POOL)
    ND = C - NP
    PREP, TAIL = 17, 1

    def first_weights(e):
        return (sw1h[:, :], sw1l[:, :]) if e == EXPERTS else (w1h[:, e, :], w1l[:, e, :])

    def second_weights(e):
        return (sw2h[:, :, :], sw2l[:, :, :]) if e == EXPERTS else (w2h[:, e * C:(e + 1) * C, :], w2l[:, e * C:(e + 1) * C, :])

    def slot_of(par, e, c):
        return (par * N + e * C + c) % RING

    x_tok = dram["x"].rearrange("b (j p) d -> b p j d", p=P)
    x1_tok = dram["x1"].rearrange("b (j p) d -> b p j d", p=P)

    def chained(eng, s, per):
        def step(b, n, ins):
            assert 1 <= n <= per
            ins.then_inc(s, 1)
            eng.wait_ge(s, b * per + n)
        return step

    def apart(eng, passed):
        eng.sem_inc(passed, 1)

    def rolled(eng, body):
        body(0, 0, True, False)
        with eng.Fori(0, (B - 2) // 2) as k:
            body(2 * k + 1, 1, False, False)
            body(2 * k + 2, 0, False, False)
        body(B - 1, 1, False, True)

    block = ctx.enter_context(nc.Block())

    @block.sync
    def _(sp):
        def load_x(b, first):
            if not first:
                sp.wait_ge(xn_made, b)
                apart(sp, sp_passed)
            sp.dma_start(xin[:, :, :], x_tok[b]).then_inc(xin_in, 16)

        def load_gate(b, e, first):
            s = e % len(gate)
            if e >= len(gate):
                sp.wait_ge(t_made, b * EXPERTS + e - len(gate) + 1)
            elif not first:
                sp.wait_ge(t_made, (b - 1) * EXPERTS + e + EXPERTS - len(gate) + 1)
            apart(sp, sp_passed)
            sp.dma_start(gate[s][:, :], dram["comb0"][b, e].partition_broadcast(P)).then_inc(gate_in[s], 16)

        def store_comb(b):
            sp.wait_ge(combT_made, b + 1)
            apart(sp, sp_passed)
            sp.dma_start(dram["comb0"][b], combT[:, :]).then_inc(comb_out, 16)

        def tail_dma(b):
            sp.wait_ge(xo_made, b + 1)
            apart(sp, sp_passed)
            sp.dma_start(xres[:, :, :], x_tok[b]).then_inc(xres_in, 16)

        def store_x1(b):
            sp.wait_ge(xo_made, b + 2)
            apart(sp, sp_passed)
            sp.dma_start(x1_tok[b], xo[:, :, :]).then_inc(xo_out, 16)

        sp.sem_inc(xo_out, 16)
        load_x(0, True)
        sp.dma_start(cols[:, :], dram["cols0"]).then_inc(cols_in, 16)
        sp.dma_start(rw[:, :], dram["rw"]).then_inc(cols_in, 16)
        sp.dma_start(ident[:, :], dram["ident"]).then_inc(cols_in, 16)
        sp.dma_start(iota8[:, :], dram["iota8"]).then_inc(cols_in, 16)
        sp.dma_start(wa[:, 0:3, :], dram["wa"].rearrange("k p n -> p k n")).then_inc(wa_in, 16)
        for e in range(E):
            s = e % 3
            if e >= 3:
                sp.wait_ge(hi_made, e - 2)
                sp.wait_ge(lo_made, e - 2)
            w1 = dram["ew1"][e] if e < EXPERTS else dram["sw1"]
            w2 = dram["ew2"][e] if e < EXPERTS else dram["sw2"]
            sp.dma_start(stage[s][:, 0:C * P], w1).then_inc(stage_in[s], 16)
            sp.dma_start(stage[s][:, C * P:].rearrange("p (c n) -> p c n", c=C),
                         w2.rearrange("(c p) n -> p c n", p=P)).then_inc(stage_in[s], 16)
        store_comb(0)

        def body(b, par, first, last):
            sp.wait_ge(comb_out, 16 * (b + 1))
            apart(sp, sp_passed)
            for e in range(len(gate)):
                load_gate(b, e, first)
            if not last:
                load_x(b + 1, False)
            if not first:
                tail_dma(b - 1)
            for e in range(len(gate), EXPERTS):
                load_gate(b, e, first)
                if e == len(gate) and not first:
                    store_x1(b - 1)
            if not last:
                store_comb(b + 1)

        rolled(sp, body)
        tail_dma(B - 1)
        store_x1(B - 1)
        sp.wait_ge(xo_out, 16 * (B + 1))

    @block.tensor
    def _(pe):
        def three_pass(out, wh, wl, h, l, start=True, stop=True):
            pe.matmul(out, wh, h, start=start, stop=False)
            pe.matmul(out, wl, h, start=False, stop=False)
            return pe.matmul(out, wh, l, start=False, stop=stop)

        def up(b, par, e, first):
            if e == 0:
                pe.wait_ge(nl_made, b + 1)
            if first:
                pe.wait_ge(hi_made, e + 1)
                pe.wait_ge(lo_made, e + 1)
            for c in range(C):
                if not (first and e == 0):
                    pe.wait_ge(hid_made, b * N + (e - 1) * C + c + 1)
                w = slice(c * P, (c + 1) * P)
                three_pass(PH[c][:, :], first_weights(e)[0][:, w], first_weights(e)[1][:, w], nh[par][:, :], nl[par][:, :]).then_inc(up_done, 1)

        def down(b, par, e, first):
            if not (first and e == 0):
                pe.wait_ge(t_made, b * EXPERTS + min(e, EXPERTS))
                if e == 0:
                    pe.wait_ge(z_made, b)
            for c in range(C):
                if c in LO_ON_POOL:
                    pe.wait_ge(lo_pool, b * E * NP + e * NP + LO_ON_POOL.index(c) + 1)
                else:
                    own = [k for k in range(C) if k not in LO_ON_POOL]
                    pe.wait_ge(lo_dve, b * E * ND + e * ND + own.index(c) + 1)
                s = slot_of(par, e, c)
                last = three_pass(PY[:, :], second_weights(e)[0][:, c, :], second_weights(e)[1][:, c, :], hh[s][:, :], hl[s][:, :],
                                  c == 0, c == C - 1)
            last.then_inc(y_done, 1)

        def transposes(dst, src):
            for j in range(J):
                last = pe.transpose(dst[:, j * P:(j + 1) * P], src[:, j, :], ident[:, :])
            return last

        def transpose_x(b, first):
            pe.wait_ge(xn_made, b + 1)
            if not first:
                pe.wait_ge(rv_made, b)
            transposes(G[0], xn)
            transposes(G[1], xr).then_inc(xposed, 1)

        def logits(b, first):
            pe.wait_ge(nT_made, b + 1)
            if not first:
                pe.wait_ge(combT_made, b)
            for j in range(J):
                last = pe.matmul(G[2][:, j * EXPERTS:(j + 1) * EXPERTS], nT[:, j * P:(j + 1) * P], rw[:, :],
                                 start=True, stop=True)
            last.then_inc(logits_done, 1)

        def transpose_comb(b):
            pe.wait_ge(comb_made, b + 1)
            for j in range(J):
                last = pe.transpose(G[2][0:EXPERTS, j * P:(j + 1) * P], comb[:, j, :], ident[:, :])
            last.then_inc(combT_done, 1)

        def attention(b):
            pe.wait_ge(mixed_lo, b + 1)
            pe.wait_ge(nT_made, b + 1)
            three_pass(G[0][:, :], woh[:, :], wol[:, :], vh[:, :], vl[:, :])
            three_pass(G[1][:, :], wrh[:, :], wrl[:, :], rh[:, :], rl[:, :]).then_inc(attn_done, 1)

        def transpose_prod(b):
            pe.wait_ge(prod_made, b + 1)
            pe.wait_ge(xo_made, b + 1)
            for j in range(J):
                last = pe.transpose(G[2][:, j * P:(j + 1) * P], prod[:, j * P:(j + 1) * P], ident[:, :])
            last.then_inc(prodT_done, 1)

        pe.wait_ge(wa_in, 16)
        pe.matmul(G[2][:, 0:P], wa[:, 0, :], wa[:, 1, :], start=True, stop=True).then_inc(wvo_done, 1)
        pe.wait_ge(cols_in, 16 * 4)
        transpose_x(0, True)
        pe.wait_ge(attn_w, 1)
        logits(0, True)
        transpose_comb(0)
        attention(0)

        def body(b, par, first, last):
            for e in range(E):
                up(b, par, e, first)
                if e == 2 and not first:
                    pe.wait_ge(combT_made, b + 1)
                    transpose_prod(b - 1)
                if e == 3 and not last:
                    transpose_x(b + 1, False)
                if e == 5 and not last:
                    if not first:
                        pe.wait_ge(xo_made, b + 1)
                    logits(b + 1, False)
                if e == 7 and not last:
                    transpose_comb(b + 1)
                if e == E - 1 and not last:
                    attention(b + 1)
                if e > 0:
                    down(b, par, e - 1, first)
            down(b, par, E - 1, first)

        rolled(pe, body)
        transpose_prod(B - 1)

    @block.scalar
    def _(act):
        def hidden(b, par, e, first):
            for c in range(C):
                act.wait_ge(up_done, b * N + e * C + c + 1)
                if not (first and e < 2):
                    act.wait_ge(y_done, b * E + e - 1)
                if not (first and e == 0):
                    if c in LO_ON_POOL:
                        act.wait_ge(lo_pool, b * E * NP + (e - 1) * NP + LO_ON_POOL.index(c) + 1)
                    else:
                        own = [k for k in range(C) if k not in LO_ON_POOL]
                        act.wait_ge(lo_dve, b * E * ND + (e - 1) * ND + own.index(c) + 1)
                bias = cols[:, CB1 + e * C + c:CB1 + e * C + c + 1]
                act.activation(hh[slot_of(par, e, c)][:, :], PH[c][:, :], ACT.Relu, bias=bias)
                act.activation(hid[c][:, :], PH[c][:, :], ACT.Relu, bias=bias).then_inc(hid_made, 1)

        def evacuate_x(b, par, first):
            act.wait_ge(xposed, b + 1)
            if not first:
                act.wait_ge(mixed, b)
                act.wait_ge(nl_made, b)
                act.wait_ge(logits_done, b)
            act.activation(xT[:, :], G[0][:, :], ACT.Identity).then_inc(xT_made, 1)
            nw = cols[:, CNW:CNW + 1]
            act.activation(nT[:, :], G[1][:, :], ACT.Identity, scale=nw)
            act.activation(nh[par][:, :], G[1][:, :], ACT.Identity, scale=nw).then_inc(nT_made, 1)

        def router_exp(b):
            act.wait_ge(logits_done, b + 1)
            act.activation(ex[:, :, :], G[2][:, 0:J * EXPERTS].rearrange("p (j e) -> p j e", j=J), ACT.Exp,
                           scale=-1.0).then_inc(ex_made, 1)

        def split_mixed(b, first):
            act.wait_ge(mixed, b + 1)
            if not first:
                act.wait_ge(attn_done, b)
            act.activation(vh[:, :], vin[:, :], ACT.Identity)
            act.activation(rh[:, :], rin[:, :], ACT.Identity).then_inc(mixed_hi, 1)

        def tanh_r(b, first):
            act.wait_ge(attn_done, b + 1)
            if not first:
                act.wait_ge(rv_made, b)
            act.activation(tr[:, :], G[1][:, :], ACT.Tanh, scale=0.5).then_inc(tr_made, 1)

        def tanh_z(b, first):
            act.wait_ge(z_made, b + 1)
            act.activation(tz[:, :], z[:, :], ACT.Tanh, scale=0.5).then_inc(tz_made, 1)

        act.wait_ge(cols_in, 16 * 4)
        act.activation(decay[:, 0:1], cols[:, CTD:CTD + 1], ACT.Exp).then_inc(decay_step, 1)
        act.wait_ge(decay_step, 1)
        act.activation(decay[:, 1:2], decay[:, 0:1], ACT.Exp, scale=-1.0).then_inc(decay_made, 1)
        act.wait_ge(wvo_done, 1)
        act.activation(wa[:, 3, :], G[2][:, 0:P], ACT.Identity)
        act.activation(woh[:, :], G[2][:, 0:P], ACT.Identity)
        act.activation(wrh[:, :], wa[:, 2, :], ACT.Identity).then_inc(set_step, 1)

        def split_weights(e):
            act.wait_ge(stage_in[e % 3], 32 * (e // 3 + 1))
            act.activation(first_weights(e)[0], stage[e % 3][:, 0:C * P], ACT.Identity)
            act.activation(second_weights(e)[0], stage[e % 3][:, C * P:].rearrange("p (c n) -> p c n", c=C),
                           ACT.Identity).then_inc(hi_made, 1)
        split_weights(0)
        evacuate_x(0, 0, True)
        split_weights(1)
        router_exp(0)
        split_weights(2)
        split_mixed(0, True)
        for e in range(3, E):
            split_weights(e)
        tanh_r(0, True)

        def body(b, par, first, last):
            for e in range(E):
                hidden(b, par, e, first)
                if e == 1 and not first:
                    tanh_z(b - 1, False)
                if e == 3 and not last:
                    evacuate_x(b + 1, 1 - par, False)
                if e == 5 and not last:
                    router_exp(b + 1)
                if e == 6 and not last:
                    split_mixed(b + 1, False)
            if not last:
                tanh_r(b + 1, False)

        rolled(act, body)
        tanh_z(B - 1, False)

    @block.gpsimd
    def _(pool):
        def power(b, k):
            pool.wait_ge(var_made, 2 * b + k)
            pool.tensor_tensor(rstd[:, k - 1, :], var[:, k - 1, :], half[:, 0:J], ALU.pow).then_inc(rstd_made, 1)

        def low_part(b, par, e, first):
            for c in LO_ON_POOL:
                s = slot_of(par, e, c)
                pool.wait_ge(hid_made, b * N + e * C + c + 1)
                pool.tensor_tensor(hl[s][:, :], hid[c][:, :], hh[s][:, :].bitcast(F32), ALU.subtract).then_inc(lo_pool, 1)

        def accumulate(b, e):
            pool.wait_ge(t_made, b * EXPERTS + e + 1)
            if e >= 2:
                pool.wait_ge(acc_made, b * (EXPERTS - 1) + e - 1)
            pool.tensor_tensor(acc[:, :], acc[:, :], t[e % 2][:, :], ALU.add).then_inc(acc_made, 1)

        pool.memset(half[:, :], -0.5).then_inc(zero_made, 1)
        pool.memset(sums[:, 0:1], 0.0).then_inc(zero_made, 1)
        pool.wait_ge(zero_made, 2)
        power(0, 1)
        power(0, 2)
        for e in range(E):
            pool.wait_ge(hi_made, e + 1)
            st_ = stage[e % 3]
            pool.tensor_tensor(first_weights(e)[1], st_[:, 0:C * P], first_weights(e)[0].bitcast(F32), ALU.subtract)
            pool.tensor_tensor(second_weights(e)[1], st_[:, C * P:].rearrange("p (c n) -> p c n", c=C),
                               second_weights(e)[0].bitcast(F32), ALU.subtract).then_inc(lo_made, 1)
        
        def body(b, par, first, last):
            for e in range(E):
                if e == 0 and not last:
                    power(b + 1, 1)
                if e == 2 and not last:
                    power(b + 1, 2)
                low_part(b, par, e, first)
                if 2 <= e:
                    accumulate(b, e - 1)

        rolled(pool, body)

    @block.vector
    def _(dve):
        chain, tchain = chained(dve, prep, PREP), chained(dve, tail, TAIL)
        own = [c for c in range(C) if c not in LO_ON_POOL]

        def low_part(b, par, e, first):
            for c in own:
                s = slot_of(par, e, c)
                dve.wait_ge(hid_made, b * N + e * C + c + 1)
                dve.tensor_tensor(hl[s][:, :], hid[c][:, :], hh[s][:, :].bitcast(F32), ALU.subtract).then_inc(lo_dve, 1)

        def weigh(b, e, first):
            dve.wait_ge(y_done, b * E + e + 1)
            b2 = cols[:, CB2 + e:CB2 + e + 1]
            if e == EXPERTS:
                dve.wait_ge(acc_made, (b + 1) * (EXPERTS - 1))
                dve.scalar_tensor_tensor(z[:, :], PY[:, :], b2, acc[:, :], ALU.add, ALU.add).then_inc(z_made, 1)
                return
            s = e % len(gate)
            dve.wait_ge(gate_in[s], 16 * (b * (EXPERTS // len(gate)) + e // len(gate) + 1))
            if e == 0:
                out = acc
                if not first:
                    dve.wait_ge(z_made, b)
            else:
                out = t[e % 2]
                if e >= 3:
                    dve.wait_ge(acc_made, b * (EXPERTS - 1) + e - 2)
            dve.scalar_tensor_tensor(out[:, :], PY[:, :], b2, gate[s][:, :], ALU.add, ALU.mult).then_inc(t_made, 1)

        def normalise(b, first):
            dve.wait_ge(xin_in, 16 * (b + 1))
            if not first:
                dve.wait_ge(xposed, b)
            for j in range(J):
                i = dve.bn_stats(st[:, j, :], xin[:, j, :])
            chain(b, 1, i)
            apart(dve, dve_passed)
            for j in range(J):
                i = dve.bn_aggr(mv[:, j, :], st[:, j, :])
            chain(b, 2, i)
            dve.tensor_scalar(var[:, 0, :], mv[:, :, 1], LN_EPS, None, ALU.add).then_inc(var_made, 1)
            dve.wait_ge(rstd_made, 2 * b + 1)
            for j in range(J):
                i = dve.tensor_scalar(xn[:, j, :], xin[:, j, :], mv[:, j, 0:1], rstd[:, 0, j:j + 1],
                                      ALU.subtract, ALU.mult)
            chain(b, 3, i)

        def rms(b):
            chain(b, 4, dve.tensor_tensor(sq[:, :, :], xn[:, :, :], xn[:, :, :], ALU.mult))
            chain(b, 5, dve.tensor_reduce(tot[:, 2, :], sq[:, :, :], AX.X, ALU.add))
            dve.tensor_scalar(var[:, 1, :], tot[:, 2, :], 1.0 / P, RMS_EPS, ALU.mult, ALU.add).then_inc(var_made, 1)
            dve.wait_ge(rstd_made, 2 * b + 2)
            for j in range(J):
                i = dve.tensor_scalar(xr[:, j, :], xn[:, j, :], rstd[:, 1, j:j + 1], None, ALU.mult)
            i.then_inc(xn_made, 1)

        def split_normed(b, par):
            dve.wait_ge(nT_made, b + 1)
            dve.tensor_tensor(nl[par][:, :], nT[:, :], nh[par][:, :].bitcast(F32), ALU.subtract).then_inc(nl_made, 1)

        def mix(b):
            dve.wait_ge(xT_made, b + 1)
            chain(b, 6, dve.tensor_tensor_scan(sums[:, 1:S + 1], decay[:, 1:2].to_broadcast([P, S]), xT[:, :], 0.0,
                                               ALU.mult, ALU.add))
            prev = sums[:, 0:S]
            chain(b, 7, dve.tensor_tensor(dif[:, :], xT[:, :], prev, ALU.subtract))
            dve.scalar_tensor_tensor(vin[:, :], dif[:, :], cols[:, CMV:CMV + 1], prev, ALU.mult, ALU.add)
            dve.scalar_tensor_tensor(rin[:, :], dif[:, :], cols[:, CMR:CMR + 1], prev, ALU.mult,
                                     ALU.add).then_inc(mixed, 1)

        def split_mixed(b):
            dve.wait_ge(mixed_hi, b + 1)
            dve.tensor_tensor(vl[:, :], vin[:, :], vh[:, :].bitcast(F32), ALU.subtract)
            dve.tensor_tensor(rl[:, :], rin[:, :], rh[:, :].bitcast(F32), ALU.subtract).then_inc(mixed_lo, 1)

        def route_keys(b):
            dve.wait_ge(ex_made, b + 1)
            chain(b, 8, dve.tensor_scalar(key[:, :, :], G[2][:, 0:J * EXPERTS].rearrange("p (j e) -> p j e", j=J),
                                          17.0, -88.0, ALU.min, ALU.max))
            apart(dve, dve_passed)
            for j in range(J):
                i = dve.max(top[:, j, :], key[:, j, :])
            chain(b, 9, i)
            apart(dve, dve_passed)
            for j in range(J):
                i = dve.max_index(idx[:, j, :], top[:, j, :], key[:, j, :])
            chain(b, 10, i)
            chain(b, 11, dve.tensor_copy(idxf[:, :, :], idx[:, :, 0:2]))

        def route(b):
            for k in range(2):
                dve.tensor_tensor(eq[:, :, k, :], iota8[:, :].rearrange("p (j e) -> p j e", j=J),
                                  idxf[:, :, k:k + 1].to_broadcast([P, J, EXPERTS]), ALU.is_equal)
            chain(b, 12, dve.tensor_scalar(ex[:, :, :], ex[:, :, :], 1.0, None, ALU.add))
            dve.tensor_tensor(sel[:, :, :], eq[:, :, 0, :], eq[:, :, 1, :], ALU.add)
            chain(b, 13, dve.reciprocal(prob[:, :, :], ex[:, :, :]))
            chain(b, 14, dve.tensor_tensor(sel[:, :, :], sel[:, :, :], prob[:, :, :], ALU.mult))
            chain(b, 15, dve.tensor_reduce(tot[:, 0, :], sel[:, :, :], AX.X, ALU.add))
            chain(b, 16, dve.tensor_scalar(tot[:, 0, :], tot[:, 0, :], SUM_EPS, None, ALU.add))
            chain(b, 17, dve.reciprocal(tot[:, 1, :], tot[:, 0, :]))
            dve.tensor_tensor(comb[:, :, :], sel[:, :, :], tot[:, 1:2, :].rearrange("p k j -> p j k").to_broadcast([P, J, EXPERTS]),
                              ALU.mult).then_inc(comb_made, 1)

        def keep_comb(b, first):
            dve.wait_ge(combT_done, b + 1)
            if not first:
                dve.wait_ge(comb_out, 16 * b)
            dve.tensor_copy(combT[:, :], G[2][0:EXPERTS, :]).then_inc(combT_made, 1)

        def gated(b, par):
            dve.wait_ge(tr_made, b + 1)
            dve.scalar_tensor_tensor(rv[par][:, :], tr[:, :], 1.0, G[0][:, :], ALU.add, ALU.mult).then_inc(rv_made, 1)

        def product(b, par):
            dve.wait_ge(tz_made, b + 1)
            tchain(b, 1, dve.scalar_tensor_tensor(q[:, :], tz[:, :], 1.0, z[:, :], ALU.add, ALU.mult))
            dve.scalar_tensor_tensor(prod[:, :], q[:, :], 0.25, rv[par][:, :], ALU.mult, ALU.mult).then_inc(prod_made, 1)

        def add_residual(b):
            dve.wait_ge(prodT_done, b + 1)
            dve.wait_ge(xres_in, 16 * (b + 1))
            dve.wait_ge(xo_out, 16 * (b + 1))
            dve.tensor_tensor(xo[:, :, :].rearrange("p j d -> p (j d)"), G[2][:, :],
                              xres[:, :, :].rearrange("p j d -> p (j d)"), ALU.add).then_inc(xo_made, 1)

        dve.sem_inc(xo_made, 1)
        dve.wait_ge(zero_made, 2)
        dve.wait_ge(cols_in, 16 * 4)
        normalise(0, True)
        rms(0)
        dve.wait_ge(set_step, 1)
        dve.tensor_tensor(wol[:, :], wa[:, 3, :], woh[:, :].bitcast(F32), ALU.subtract)
        dve.tensor_tensor(wrl[:, :], wa[:, 2, :], wrh[:, :].bitcast(F32), ALU.subtract).then_inc(attn_w, 1)
        dve.wait_ge(decay_made, 1)
        split_normed(0, 0)
        mix(0)
        route_keys(0)
        route(0)
        keep_comb(0, True)
        split_mixed(0)
        gated(0, 0)

        def body(b, par, first, last):
            for e in range(E):
                low_part(b, par, e, first)
                if e > 0:
                    weigh(b, e - 1, first)
                if e == 0 and not last:
                    normalise(b + 1, False)
                if e == 1:
                    if not first:
                        product(b - 1, 1 - par)
                if e == 2 and not last:
                    rms(b + 1)
                if e == 3 and not first:
                    add_residual(b - 1)
                if e == 4 and not last:
                    split_normed(b + 1, 1 - par)
                    mix(b + 1)
                if e == 5 and not last:
                    route_keys(b + 1)
                if e == 6 and not last:
                    route(b + 1)
                    split_mixed(b + 1)
                if e == 7 and not last:
                    keep_comb(b + 1, False)
            if not last:
                gated(b + 1, 1 - par)
            weigh(b, E - 1, first)

        rolled(dve, body)
        product(B - 1, 1)
        add_residual(B - 1)


def run_layer1(nc, ctx, shared, dram):
    from concourse import mybir

    F32, F32R, U32 = mybir.dt.float32, mybir.dt.float32r, mybir.dt.uint32
    ALU, ACT, AX = mybir.AluOpType, mybir.ActivationFunctionType, mybir.AxisListType

    def sb(name, shape, dt=F32):
        return ctx.enter_context(nc.sbuf_tensor("l1_" + name, shape, dt))

    def sem(name):
        return ctx.enter_context(nc.semaphore("l1_" + name))

    P = 128
    B, S = dram["x"].shape[:2]
    J = S // P
    E = 8
    C = 4
    N = E * C
    RING = 2 * C
    HID = C
    BANKS = 3
    NS = 16
    PER = NS // E
    HALF = 8
    SOON, LATE = 8, 0
    RX = 4
    R = dram["wxr"].shape[0]
    LO_ON_DVE = [(2, 3) if e in (1, 3, 7) else (3,) for e in range(E)]
    LN_EPS, TEMP = 1e-5, 0.9

    w1h, w1l, w2h, w2l = (shared[k] for k in ("w1h", "w1l", "w2h", "w2l"))
    hh, hl = shared["hh"], shared["hl"]
    t, acc = shared["t"], [shared["acc"], sb("acc1", [P, S])]
    ident, iota8 = shared["ident"], shared["iota8"]
    PH, PY, G = shared["PH"][0:3], shared["PY"], shared["G"][0:2]
    PB, PC = shared["PH"][3], shared["G"][2]

    CB1, CB2 = 0, E * C
    CBDT, CA = CB2 + E, CB2 + E + 1
    cols = sb("cols", [P, CA + NS])
    aneg = sb("aneg", [P, NS])
    gb = sb("gb", [P, J, E])
    lng, lnb = sb("lng", [P, P]), sb("lnb", [P, P])
    gw = sb("gw", [P, E])
    half = sb("half", [P, J])
    hid = [sb(f"hid{i}", [P, S]) for i in range(HID)]
    gate = [sb(f"gate{i}", [P, S]) for i in range(2)]
    wth, wtl = sb("wth", [P, P], F32R), sb("wtl", [P, P], F32R)
    wo = sb("wo", [P, P])
    wsh, wsl = sb("wsh", [P, 4, P], F32R), sb("wsl", [P, 4, P], F32R)
    pick = sb("pick", [P, HALF, P], F32R)
    nh = [sb(f"nh{i}", [P, S], F32R) for i in range(2)]
    nl = [sb(f"nl{i}", [P, S], F32R) for i in range(2)]
    xn, xT = sb("xn", [P, J, P]), sb("xT", [P, S])
    dt, u = sb("dt", [P, S]), sb("u", [P, S])
    soft = sb("soft", [P, S])
    abar = sb("abar", [P, NS, S])
    bch, bcl = sb("bch", [P, 4, S], F32R), sb("bcl", [P, 4, S], F32R)
    bx = [sb(f"bx{i}", [P, S]) for i in range(RX)]
    y = [sb(f"y{i}", [P, S]) for i in range(2)]
    s1 = sb("s1", [P, J, P])
    ones, bout = sb("ones", [1, P]), sb("bout", [1, S])
    ln = sb("ln", [P, S])
    z = sb("z", [P, J, P])
    tz = xn
    xres = sb("xres", [P, J, P])
    st, mv = sb("st", [P, J, 6]), sb("mv", [P, J, 2])
    st2, mv2 = sb("st2", [P, J, 6]), sb("mv2", [P, J, 2])
    var, rstd = sb("var", [P, 2, J]), sb("rstd", [P, 2, J])
    lg, eq = sb("lg", [P, J, E]), sb("eq", [P, J, 2, E])
    top, idx = sb("top", [P, J, 8]), sb("idx", [P, J, 8], U32)
    idxf, gap, th = sb("idxf", [P, J, 2]), sb("gap", [P, J, 1]), sb("th", [P, J, 2])
    comb = sb("comb", [P, J, E])
    combT = xn[0:E, :, :].rearrange("p j d -> p (j d)")
    stage = [abar[:, 2 * i:2 * i + 2, :].rearrange("p k n -> p (k n)") for i in range(3)]
    wtmp = abar[:, 6:9, :].rearrange("p k (m n) -> p (k m) n", n=P)
    wset = abar[:, 9:10, :].rearrange("p k (m n) -> p (k m) n", n=P)
    wx64 = abar[0:R, 10:11, 0:2 * P].rearrange("p k (m n) -> p (k m) n", n=P)
    picks = abar[:, 12:14, :].rearrange("p k (m n) -> p (k m) n", n=P)

    cols_in, w_in = sem("cols_in"), sem("w_in")
    stage_in = [sem(f"stage_in{i}") for i in range(3)]
    hi_made, lo_made = sem("w_hi_made"), sem("w_lo_made")
    half_made = sem("half_made")
    wt_done, small_made = sem("wt_done"), sem("small_made")
    small_hi, small_lo = sem("small_hi"), sem("small_lo")
    a_made = sem("a_made")
    xin_in, xres_in = sem("xin_in"), sem("xres_in")
    prep, tail = sem("prep_step"), sem("tail_step")
    var_made, rstd_made = sem("var_made"), sem("rstd_made")
    tvar_made, trstd_made = sem("tail_var_made"), sem("tail_rstd_made")
    xn_made, xposed, nT_made, nl_made = sem("xn_made"), sem("x_transposed"), sem("nT_made"), sem("nl_made")
    logits_done, gap_made, th_made = sem("logits_done"), sem("gap_made"), sem("th_made")
    comb_made, combT_done, combT_made, comb_out = sem("comb_made"), sem("combT_done"), sem("combT_made"), sem("comb_out")
    dt_done, v_made, e_made, e1_made, ln_made = sem("dt_done"), sem("v_made"), sem("e_made"), sem("e1_made"), sem("ln_made")
    left_out, kept_made = sem("left_out"), sem("kept_made")
    dt_made, u_made, abar_made = sem("dt_made"), sem("u_made"), sem("abar_made")
    set_done, set_hi, set_lo = sem("set_done"), sem("set_hi"), sem("set_lo")
    b_done, c_done, bx_made, scan_made, m_made, y_made = (
        sem("b_done"), sem("c_done"), sem("bx_made"), sem("scan_made"), sem("m_made"), sem("y_made"))
    wout_done, s1_made = sem("wout_done"), sem("s1_made")
    gate_in = [sem(f"gate_in{i}") for i in range(len(gate))]
    up_done, hid_made, lo_dve, lo_pool = sem("up_done"), sem("hid_made"), sem("lo_dve"), sem("lo_pool")
    y2_done, t_made, acc_made = sem("expert_done"), sem("t_made"), sem("acc_made")
    accT_done, accT_made, z_made, tz_made = sem("accT_done"), sem("accT_made"), sem("z_made"), sem("tz_made")
    xo_made, xo_out = sem("xo_made"), sem("xo_out")

    dve_passed, sp_passed = sem("dve_passed"), sem("sp_passed")

    PREP, TAIL = 9, 6
    BY_DVE = [(e, c) for e in range(E) for c in LO_ON_DVE[e]]
    BY_POOL = [(e, c) for e in range(E) for c in range(C) if c not in LO_ON_DVE[e]]

    def slot_of(e, c):
        return (e * C + c) % RING

    def lo_ready(eng, b, e, c):
        for made, by in ((lo_pool, BY_POOL), (lo_dve, BY_DVE)):
            if (e, c) in by:
                eng.wait_ge(made, b * len(by) + by.index((e, c)) + 1)

    x1_tok = dram["x1"].rearrange("b (j p) d -> b p j d", p=P)
    out_tok = dram["out"].rearrange("b (j p) d -> b p j d", p=P)

    def chained(eng, s, per):
        def step(b, n, ins):
            assert 1 <= n <= per
            ins.then_inc(s, 1)
            eng.wait_ge(s, b * per + n)
        return step

    def apart(eng, passed):
        eng.sem_inc(passed, 1)

    def rolled(eng, body):
        body(0, 0, True, False)
        with eng.Fori(0, (B - 2) // 2) as k:
            body(2 * k + 1, 1, False, False)
            body(2 * k + 2, 0, False, False)
        body(B - 1, 1, False, True)

    block = ctx.enter_context(nc.Block())

    @block.sync
    def _(sp):
        def load_x(b, first):
            if not first:
                sp.wait_ge(xposed, b)
                apart(sp, sp_passed)
            sp.dma_start(xn[:, :, :], x1_tok[b]).then_inc(xin_in, 16)

        def load_gate(b, e, first):
            s = e % len(gate)
            if e >= len(gate) or not first:
                sp.wait_ge(t_made, b * E + e - len(gate) + 1)
            apart(sp, sp_passed)
            sp.dma_start(gate[s][:, :], dram["comb1"][b, e].partition_broadcast(P)).then_inc(gate_in[s], 16)

        def store_comb(b):
            sp.wait_ge(combT_made, b + 1)
            apart(sp, sp_passed)
            sp.dma_start(dram["comb1"][b], combT).then_inc(comb_out, 16)

        def load_residual(b):
            sp.wait_ge(xo_out, 16 * (b + 1))
            apart(sp, sp_passed)
            sp.dma_start(xres[:, :, :], x1_tok[b]).then_inc(xres_in, 16)

        def store_out(b):
            sp.wait_ge(xo_made, b + 2)
            apart(sp, sp_passed)
            sp.dma_start(out_tok[b], xres[:, :, :]).then_inc(xo_out, 16)

        sp.sem_inc(xo_out, 16)
        load_x(0, True)
        for dst, name in ((cols[:, :], "cols1"), (gb[:, :, :].rearrange("p j e -> p (j e)"), "gb"), (lng[:, :], "lng"),
                          (lnb[:, :], "lnb"), (gw[:, :], "gw")):
            sp.dma_start(dst, dram[name]).then_inc(cols_in, 16)
        sp.dma_start(wtmp[:, 0, :], dram["mask"]).then_inc(w_in, 16)
        sp.dma_start(wo[:, :], dram["wout"]).then_inc(w_in, 16)
        sp.dma_start(bout[:, :], dram["bout"]).then_inc(w_in, 16)
        sp.dma_start(wset[:, :, :], dram["ws"].rearrange("k p n -> p k n")).then_inc(w_in, 16)
        sp.dma_start(wx64[:, 0, :], dram["wxr"]).then_inc(w_in, 16)
        sp.dma_start(wx64[:, 1, :], dram["wdt"]).then_inc(w_in, 16)
        sp.dma_start(picks[:, :, :], dram["pick"].rearrange("k p n -> p k n")).then_inc(w_in, 16)
        for e in range(E):
            s = e % 3
            if e >= 3:
                sp.wait_ge(hi_made, e - 2)
                sp.wait_ge(lo_made, e - 2)
            sp.dma_start(stage[s][:, 0:C * P], dram["w1"][e]).then_inc(stage_in[s], 16)
            sp.dma_start(stage[s][:, C * P:].rearrange("p (c n) -> p c n", c=C),
                         dram["w2"][e].rearrange("(c p) n -> p c n", p=P)).then_inc(stage_in[s], 16)
        store_comb(0)

        def body(b, par, first, last):
            sp.wait_ge(comb_out, 16 * (b + 1))
            apart(sp, sp_passed)
            if not last:
                load_x(b + 1, False)
            for e in range(E):
                load_gate(b, e, first)
                if e == 1 and not first:
                    load_residual(b - 1)
            if not first:
                store_out(b - 1)
            if not last:
                store_comb(b + 1)

        rolled(sp, body)
        load_residual(B - 1)
        store_out(B - 1)
        sp.wait_ge(xo_out, 16 * (B + 1))

    @block.tensor
    def _(pe):
        def three_pass(out, wh, wl, h, l, start=True, stop=True):
            pe.matmul(out, wh, h, start=start, stop=False)
            pe.matmul(out, wl, h, start=False, stop=False)
            return pe.matmul(out, wh, l, start=False, stop=stop)

        def up(b, par, e, c, first):
            k = e * C + c
            if k == 0:
                pe.wait_ge(nl_made, b + 1)
            if first and c == 0:
                pe.wait_ge(hi_made, e + 1)
                pe.wait_ge(lo_made, e + 1)
            if k >= BANKS:
                pe.wait_ge(hid_made, b * N + k - BANKS + 1)
            elif not first:
                before = max(n for n in range(N) if n % BANKS == k)
                pe.wait_ge(hid_made, (b - 1) * N + before + 1)
            w = slice(c * P, (c + 1) * P)
            three_pass(PH[k % BANKS][:, :], w1h[:, e, w], w1l[:, e, w], nh[par][:, :], nl[par][:, :]).then_inc(up_done, 1)

        def down(b, e, c):
            lo_ready(pe, b, e, c)
            s = slot_of(e, c)
            last = three_pass(PY[:, :], w2h[:, e * C + c, :], w2l[:, e * C + c, :], hh[s][:, :], hl[s][:, :],
                              c == 0, c == C - 1)
            if c == C - 1:
                last.then_inc(y2_done, 1)

        def spread(b, n, k, bank, done, read, first):
            if n % HALF == 0:
                pe.wait_ge(set_lo, 4 * b + 2 * (n // HALF + 1))
            if not (first and n == 0):
                pe.wait_ge(read, b * NS + n)
            s = 2 * k + n // HALF
            pe.matmul(bank[:, :], pick[:, n % HALF, :], bch[:, s, :], start=True, stop=False)
            pe.matmul(bank[:, :], pick[:, n % HALF, :], bcl[:, s, :], start=False, stop=True).then_inc(done, 1)

        def spread_b(b, n, first):
            spread(b, n, 0, PB, b_done, bx_made, first)

        def spread_c(b, n, first):
            spread(b, n, 1, PC, c_done, m_made, first)

        def compact(b, par, half):
            if half == 0:
                pe.wait_ge(gap_made, b + 1)
                pe.wait_ge(v_made, b + 1)
            else:
                pe.wait_ge(combT_made, b + 1)
                pe.wait_ge(set_lo, 4 * b + 2)
            for k in range(2):
                s = 2 * k + half
                three_pass(G[k][:, :], wsh[:, s, :], wsl[:, s, :], nh[par][:, :], nl[par][:, :]).then_inc(set_done, 1)

        def step_sizes(b, par):
            pe.wait_ge(nl_made, b + 1)
            three_pass(G[1][:, :], wth[:, :], wtl[:, :], nh[par][:, :], nl[par][:, :]).then_inc(dt_done, 1)

        def transposes(dst, src, s):
            for j in range(J):
                last = pe.transpose(dst[:, j * P:(j + 1) * P], src[:, j * P:(j + 1) * P], ident[:, :])
            last.then_inc(s, 1)

        def transpose_x(b, first):
            pe.wait_ge(xn_made, b + 1)
            if not first:
                pe.wait_ge(s1_made, b - 1)
            transposes(G[0], xn[:, :, :].rearrange("p j d -> p (j d)"), xposed)

        def logits(b):
            pe.wait_ge(nT_made, b + 1)
            for j in range(J):
                last = pe.matmul(G[0][:, j * E:(j + 1) * E], xT[:, j * P:(j + 1) * P], gw[:, :], start=True, stop=True)
            last.then_inc(logits_done, 1)

        def transpose_comb(b):
            pe.wait_ge(comb_made, b + 1)
            pe.wait_ge(set_lo, 4 * b + 1)
            for j in range(J):
                last = pe.transpose(G[0][0:E, j * P:(j + 1) * P], comb[:, j, :], ident[:, :])
            last.then_inc(combT_done, 1)

        def project(b, par):
            pe.wait_ge(y_made, (b + 1) * (NS - 1))
            pe.matmul(G[0][:, :], ones[:, :], bout[:, :], start=True, stop=False)
            for j in range(J):
                tok = slice(j * P, (j + 1) * P)
                last = pe.matmul(G[0][:, tok], y[par][:, tok], wo[:, :], start=False, stop=j == J - 1)
            last.then_inc(wout_done, 1)

        def transpose_acc(b, par):
            pe.wait_ge(acc_made, (b + 1) * (E - 1))
            transposes(G[1], acc[par], accT_done)

        pe.wait_ge(w_in, 16 * 7)
        pe.matmul(G[1][:, 0:P], wx64[:, 0, :], wx64[:, 1, :], start=True, stop=True).then_inc(wt_done, 1)
        pe.wait_ge(cols_in, 16 * 5)
        transpose_x(0, True)
        pe.wait_ge(small_lo, 1)
        logits(0)
        step_sizes(0, 0)
        compact(0, 0, 0)
        transpose_comb(0)

        def body(b, par, first, last):
            if first:
                spread_b(b, 0, first)
                spread_c(b, 0, first)
            for e in range(E):
                before = (b, e - 1) if e > 0 else None if first else (b - 1, E - 1)
                n = PER * e + 1
                following = None if last and e == E - 1 else (b + 1, 0, False) if e == E - 1 else (b, n + 1, first)

                def down_before(c):
                    if before and c == 0 and not (first and e == 1):
                        pe.wait_ge(t_made, before[0] * E + before[1])
                    if before:
                        down(*before, c)

                if e == 0:
                    spread_b(b, n, first)
                up(b, par, e, 0, first)
                up(b, par, e, 1, first)
                down_before(0)
                up(b, par, e, 2, first)
                down_before(1)
                spread_c(b, n, first)
                down_before(2)
                if following:
                    spread_b(*following)
                if e == 0:
                    compact(b, par, 1)
                if e == 1 and not first:
                    pe.wait_ge(set_lo, 4 * (b + 1))
                    project(b - 1, 1 - par)
                if e == 2:
                    if not last:
                        if first:
                            pe.wait_ge(set_lo, 4 * (b + 1))
                        transpose_x(b + 1, first)
                    if not first:
                        transpose_acc(b - 1, 1 - par)
                if e == 3 and not last:
                    logits(b + 1)
                if e == 4 and not last:
                    if not first:
                        pe.wait_ge(accT_made, b)
                    step_sizes(b + 1, 1 - par)
                if e == 6 and not last:
                    compact(b + 1, 1 - par, 0)
                if e == 7 and not last:
                    transpose_comb(b + 1)
                down_before(3)
                if following:
                    spread_c(*following)
                up(b, par, e, 3, first)
                if e < E - 1:
                    spread_b(b, n + PER, first)

        rolled(pe, body)
        pe.wait_ge(t_made, B * E - 1)
        for c in range(C):
            down(B - 1, E - 1, c)
        project(B - 1, (B - 1) % 2)
        transpose_acc(B - 1, (B - 1) % 2)

    @block.scalar
    def _(act):
        def hidden(b, e, first):
            for c in range(C):
                k = e * C + c
                act.wait_ge(up_done, b * N + k + 1)
                if not (first and e < 2):
                    act.wait_ge(y2_done, b * E + e - 1)
                if k >= HID:
                    lo_ready(act, b, (k - HID) // C, (k - HID) % C)
                elif not first:
                    lo_ready(act, b - 1, E - 1, C - HID + k)
                bias = cols[:, CB1 + k:CB1 + k + 1]
                act.activation(hh[slot_of(e, c)][:, :], PH[k % BANKS][:, :], ACT.Gelu, bias=bias)
                act.activation(hid[c % HID][:, :], PH[k % BANKS][:, :], ACT.Gelu, bias=bias).then_inc(hid_made, 1)

        def evacuate_x(b, par, first):
            act.wait_ge(xposed, b + 1)
            if not first:
                act.wait_ge(u_made, b)
                act.wait_ge(logits_done, b)
            act.activation(xT[:, :], G[0][:, :], ACT.Identity)
            act.activation(nh[par][:, :], G[0][:, :], ACT.Identity).then_inc(nT_made, 1)

        def gate_tanh(b):
            act.wait_ge(gap_made, b + 1)
            act.activation(th[:, :, 0:1], gap[:, :, :], ACT.Tanh, scale=0.5 / TEMP).then_inc(th_made, 1)

        def softplus(b, par):
            act.preload_act_table_set("natural_log_exp_and_others")
            act.wait_ge(v_made, b + 1)
            act.activation(soft[:, :], soft[:, :], ACT.Exp).then_inc(e_made, 1)
            act.wait_ge(e1_made, b + 1)
            act.activation(ln[:, :], y[par][:, :], ACT.Ln).then_inc(ln_made, 1)

        def decays(b, states, first):
            act.preload_act_table_set("natural_log_exp_and_others")
            act.wait_ge(dt_made, b + 1)
            if first:
                act.wait_ge(lo_made, E)
            for n in states:
                decay(b, n, first)

        def decay(b, n, first):
            if not first:
                act.wait_ge(scan_made, (b - 1) * NS + n + 1)
            act.activation(abar[:, n, :], dt[:, :], ACT.Exp, scale=aneg[:, n:n + 1]).then_inc(abar_made, 1)

        def evacuate_sets(b, half, first):
            for k in range(2):
                act.wait_ge(set_done, 4 * b + 2 * half + k + 1)
                if not first:
                    act.wait_ge(b_done, (b - 1) * NS + HALF * (half + 1))
                    act.wait_ge(c_done, (b - 1) * NS + HALF * (half + 1))
                act.activation(bch[:, 2 * k + half, :], G[k][:, :], ACT.Identity).then_inc(set_hi, 1)

        def evacuate_s1(b):
            act.wait_ge(wout_done, b + 1)
            act.wait_ge(xo_made, b + 1)
            act.activation(s1[:, :, :], G[0][:, :].rearrange("p (j d) -> p j d", j=J), ACT.Identity).then_inc(s1_made, 1)

        def evacuate_acc(b):
            act.wait_ge(accT_done, b + 1)
            act.activation(z[:, :, :], G[1][:, :].rearrange("p (j d) -> p j d", j=J), ACT.Identity).then_inc(accT_made, 1)

        def tanh_z(b):
            act.wait_ge(z_made, b + 1)
            act.activation(tz[:, :, :], z[:, :, :], ACT.Tanh, scale=0.5).then_inc(tz_made, 1)

        act.wait_ge(cols_in, 16 * 5)
        act.activation(aneg[:, :], cols[:, CA:CA + NS], ACT.Exp).then_inc(a_made, 1)
        act.wait_ge(small_made, 1)
        act.activation(wth[:, :], wtmp[:, 2, :], ACT.Identity)
        act.activation(wsh[:, :, :], wset[:, :, :], ACT.Identity)
        act.activation(pick[:, :, :], picks[:, :, :], ACT.Identity).then_inc(small_hi, 1)
        evacuate_x(0, 0, True)
        for e in range(E):
            act.wait_ge(stage_in[e % 3], 32 * (e // 3 + 1))
            act.activation(w1h[:, e, :], stage[e % 3][:, 0:C * P], ACT.Identity)
            act.activation(w2h[:, e * C:(e + 1) * C, :], stage[e % 3][:, C * P:].rearrange("p (c n) -> p c n", c=C),
                           ACT.Identity).then_inc(hi_made, 1)
        gate_tanh(0)
        softplus(0, 0)
        evacuate_sets(0, 0, True)
        decays(0, range(NS - LATE), True)

        def body(b, par, first, last):
            for e in range(E):
                hidden(b, e, first)
                if e == 0:
                    evacuate_sets(b, 1, first)
                    if LATE:
                        decays(b, range(NS - LATE, NS), first)
                if e == 1 and not first:
                    evacuate_s1(b - 1)
                if e == 2:
                    if not last:
                        evacuate_x(b + 1, 1 - par, False)
                    if not first:
                        evacuate_acc(b - 1)
                if e == 4 and not last:
                    gate_tanh(b + 1)
                if e == 5 and not last:
                    softplus(b + 1, 1 - par)
                if e == 6 and not first:
                    tanh_z(b - 1)
                if e == 6 and not last:
                    evacuate_sets(b + 1, 0, False)
                    decays(b + 1, range(SOON), False)
            if not last:
                decays(b + 1, range(SOON, NS - LATE), False)

        rolled(act, body)
        evacuate_s1(B - 1)
        evacuate_acc(B - 1)
        tanh_z(B - 1)

    @block.gpsimd
    def _(pool):
        def power(b, k, made, done):
            pool.wait_ge(made, b + 1)
            pool.tensor_tensor(rstd[:, k, :], var[:, k, :], half[:, :], ALU.pow).then_inc(done, 1)

        def low_part(b, e, c):
            s = slot_of(e, c)
            pool.wait_ge(hid_made, b * N + e * C + c + 1)
            pool.tensor_tensor(hl[s][:, :], hid[c % HID][:, :], hh[s][:, :].bitcast(F32), ALU.subtract).then_inc(lo_pool, 1)

        def accumulate(b, par, e):
            pool.wait_ge(t_made, b * E + e + 1)
            if e >= 2:
                pool.wait_ge(acc_made, b * (E - 1) + e - 1)
            pool.tensor_tensor(acc[par][:, :], acc[par][:, :], t[e % 2][:, :], ALU.add).then_inc(acc_made, 1)

        def sum_states(b, par, n):
            if n == 0:
                return
            pool.wait_ge(m_made, b * NS + n + 1)
            if n >= 2:
                pool.wait_ge(y_made, b * (NS - 1) + n - 1)
            pool.tensor_tensor(y[par][:, :], y[par][:, :], bx[n % RX][:, :], ALU.add).then_inc(y_made, 1)

        pool.memset(ones[:, :], 1.0).then_inc(half_made, 1)
        pool.memset(half[:, :], -0.5).then_inc(half_made, 1)
        pool.wait_ge(half_made, 2)
        power(0, 0, var_made, rstd_made)
        for e in range(E):
            pool.wait_ge(hi_made, e + 1)
            pool.tensor_tensor(w1l[:, e, :], stage[e % 3][:, 0:C * P], w1h[:, e, :].bitcast(F32), ALU.subtract)
            pool.tensor_tensor(w2l[:, e * C:(e + 1) * C, :], stage[e % 3][:, C * P:].rearrange("p (c n) -> p c n", c=C),
                               w2h[:, e * C:(e + 1) * C, :].bitcast(F32), ALU.subtract).then_inc(lo_made, 1)

        def body(b, par, first, last):
            for e in range(E):
                if e > 0:
                    sum_states(b, par, PER * e - 1)
                elif not first:
                    sum_states(b - 1, 1 - par, NS - 1)
                if e < 2 and not first:
                    accumulate(b - 1, 1 - par, E - 2 + e)
                if e >= 3:
                    accumulate(b, par, e - 2)
                low_part(b, e, 0)
                sum_states(b, par, PER * e)
                low_part(b, e, 1)
                if 2 not in LO_ON_DVE[e]:
                    low_part(b, e, 2)
                if e == 3 and not first:
                    power(b - 1, 1, tvar_made, trstd_made)
                if e == 0 and not last:
                    power(b + 1, 0, var_made, rstd_made)
        rolled(pool, body)
        sum_states(B - 1, (B - 1) % 2, NS - 1)
        accumulate(B - 1, (B - 1) % 2, E - 2)
        accumulate(B - 1, (B - 1) % 2, E - 1)
        power(B - 1, 1, tvar_made, trstd_made)

    @block.vector
    def _(dve):
        chain, tchain = chained(dve, prep, PREP), chained(dve, tail, TAIL)

        def low_part(b, e):
            for c in LO_ON_DVE[e]:
                s = slot_of(e, c)
                dve.wait_ge(hid_made, b * N + e * C + c + 1)
                dve.tensor_tensor(hl[s][:, :], hid[c % HID][:, :], hh[s][:, :].bitcast(F32), ALU.subtract).then_inc(lo_dve, 1)

        def weigh(b, par, e, first):
            dve.wait_ge(y2_done, b * E + e + 1)
            s = e % len(gate)
            dve.wait_ge(gate_in[s], 16 * (b * (E // len(gate)) + e // len(gate) + 1))
            if e == 0:
                out = acc[par]
            else:
                out = t[e % 2]
                if e >= 3:
                    dve.wait_ge(acc_made, b * (E - 1) + e - 2)
                elif not first:
                    dve.wait_ge(acc_made, b * (E - 1))
            dve.scalar_tensor_tensor(out[:, :], PY[:, :], cols[:, CB2 + e:CB2 + e + 1], gate[s][:, :],
                                     ALU.add, ALU.mult).then_inc(t_made, 1)

        def states_in(b, n, first):
            dve.wait_ge(b_done, b * NS + n + 1)
            if n == 0:
                dve.wait_ge(u_made, b + 1)
            if n > RX:
                dve.wait_ge(y_made, b * (NS - 1) + n - RX)
            elif n < RX and not first:
                dve.wait_ge(y_made, (b - 1) * (NS - 1) + NS - RX + n)
            dve.tensor_tensor(bx[n % RX][:, :], u[:, :], PB[:, :], ALU.mult).then_inc(bx_made, 1)

        def state_scan(b, n):
            dve.wait_ge(bx_made, b * NS + n + 1)
            dve.wait_ge(abar_made, b * NS + n + 1)
            dve.tensor_tensor_scan(bx[n % RX][:, :], abar[:, n, :], bx[n % RX][:, :], 0.0,
                                   ALU.mult, ALU.add).then_inc(scan_made, 1)

        def states_out(b, par, n, first):
            dve.wait_ge(scan_made, b * NS + n + 1)
            dve.wait_ge(c_done, b * NS + n + 1)
            out = y[par] if n == 0 else bx[n % RX]
            dve.tensor_tensor(out[:, :], bx[n % RX][:, :], PC[:, :], ALU.mult).then_inc(m_made, 1)

        def normalise(b):
            dve.wait_ge(xin_in, 16 * (b + 1))
            for j in range(J):
                i = dve.bn_stats(st[:, j, :], xn[:, j, :])
            chain(b, 1, i)
            apart(dve, dve_passed)
            for j in range(J):
                i = dve.bn_aggr(mv[:, j, :], st[:, j, :])
            chain(b, 2, i)
            dve.tensor_scalar(var[:, 0, :], mv[:, :, 1], LN_EPS, None, ALU.add).then_inc(var_made, 1)

        def normalise2(b):
            dve.wait_ge(rstd_made, b + 1)
            for j in range(J):
                i = dve.tensor_scalar(xn[:, j, :], xn[:, j, :], mv[:, j, 0:1], rstd[:, 0, j:j + 1],
                                      ALU.subtract, ALU.mult)
            i.then_inc(xn_made, 1)

        def split_normed(b, par):
            dve.wait_ge(nT_made, b + 1)
            dve.tensor_tensor(nl[par][:, :], xT[:, :], nh[par][:, :].bitcast(F32), ALU.subtract).then_inc(nl_made, 1)

        def route(b):
            dve.wait_ge(logits_done, b + 1)
            chain(b, 3, dve.tensor_tensor(lg[:, :, :], G[0][:, 0:J * E].rearrange("p (j e) -> p j e", j=J), gb[:, :, :],
                                          ALU.add))
            apart(dve, dve_passed)
            for j in range(J):
                i = dve.max(top[:, j, :], lg[:, j, :])
            chain(b, 4, i)
            dve.tensor_tensor(gap[:, :, :], top[:, :, 0:1], top[:, :, 1:2], ALU.subtract).then_inc(gap_made, 1)

        def route2(b):
            for j in range(J):
                i = dve.max_index(idx[:, j, :], top[:, j, :], lg[:, j, :])
            chain(b, 5, i)
            chain(b, 6, dve.tensor_copy(idxf[:, :, :], idx[:, :, 0:2]))

        def softmax_of_two(b):
            dve.wait_ge(th_made, b + 1)
            for k in range(2):
                dve.tensor_tensor(eq[:, :, k, :], iota8[:, :].rearrange("p (j e) -> p j e", j=J),
                                  idxf[:, :, k:k + 1].to_broadcast([P, J, E]), ALU.is_equal)
            dve.tensor_scalar(th[:, :, 1:2], th[:, :, 0:1], -0.5, 0.5, ALU.mult, ALU.add)
            chain(b, 8, dve.tensor_scalar(gap[:, :, :], th[:, :, 0:1], 0.5, 0.5, ALU.mult, ALU.add))
            dve.tensor_tensor(eq[:, :, 1, :], eq[:, :, 1, :], th[:, :, 1:2].to_broadcast([P, J, E]), ALU.mult)
            chain(b, 9, dve.tensor_tensor(eq[:, :, 0, :], eq[:, :, 0, :], gap[:, :, :].to_broadcast([P, J, E]), ALU.mult))
            dve.tensor_tensor(comb[:, :, :], eq[:, :, 0, :], eq[:, :, 1, :], ALU.add).then_inc(comb_made, 1)

        def keep_comb(b, first):
            dve.wait_ge(combT_done, b + 1)
            if not first:
                dve.wait_ge(comb_out, 16 * b)
            dve.tensor_copy(combT, G[0][0:E, :]).then_inc(combT_made, 1)

        def step_in(b, first):
            dve.wait_ge(dt_done, b + 1)
            if not first:
                dve.wait_ge(abar_made, b * NS)
            chain(b, 7, dve.tensor_scalar(dt[:, :], G[1][:, :], cols[:, CBDT:CBDT + 1], None, ALU.add))
            dve.scalar_tensor_tensor(soft[:, :], dt[:, :], -1.0, dt[:, :], ALU.mult, ALU.min).then_inc(v_made, 1)

        def split_sets(b, half):
            for k in range(2):
                s = 2 * k + half
                dve.wait_ge(set_hi, 4 * b + 2 * half + k + 1)
                dve.tensor_tensor(bcl[:, s, :], G[k][:, :], bch[:, s, :].bitcast(F32), ALU.subtract).then_inc(set_lo, 1)

        def one_plus(b, par):
            dve.wait_ge(e_made, b + 1)
            e1 = y[par]
            dve.tensor_scalar(e1[:, :], soft[:, :], 1.0, None, ALU.add).then_inc(e1_made, 1)
            dve.wait_ge(e1_made, b + 1)
            dve.scalar_tensor_tensor(soft[:, :], e1[:, :], 1.0, soft[:, :], ALU.subtract, ALU.subtract).then_inc(left_out, 1)

        def softplus(b):
            dve.wait_ge(left_out, b + 1)
            dve.scalar_tensor_tensor(dt[:, :], dt[:, :], 0.0, soft[:, :], ALU.max, ALU.subtract).then_inc(kept_made, 1)
            dve.wait_ge(kept_made, b + 1)
            dve.wait_ge(ln_made, b + 1)
            dve.tensor_tensor(dt[:, :], dt[:, :], ln[:, :], ALU.add).then_inc(dt_made, 1)

        def states_input(b, first):
            dve.wait_ge(dt_made, b + 1)
            if not first:
                dve.wait_ge(bx_made, b * NS)
            dve.tensor_tensor(u[:, :], dt[:, :], xT[:, :], ALU.mult).then_inc(u_made, 1)

        def norm_experts(b):
            dve.wait_ge(accT_made, b + 1)
            for j in range(J):
                i = dve.bn_stats(st2[:, j, :], z[:, j, :])
            tchain(b, 1, i)
            apart(dve, dve_passed)
            for j in range(J):
                i = dve.bn_aggr(mv2[:, j, :], st2[:, j, :])
            tchain(b, 2, i)
            dve.tensor_scalar(var[:, 1, :], mv2[:, :, 1], LN_EPS, None, ALU.add).then_inc(tvar_made, 1)

        def norm_experts2(b):
            dve.wait_ge(trstd_made, b + 1)
            for j in range(J):
                i = dve.tensor_scalar(z[:, j, :], z[:, j, :], mv2[:, j, 0:1], rstd[:, 1, j:j + 1],
                                      ALU.subtract, ALU.mult)
            tchain(b, 3, i)

        def scale_experts(b):
            tchain(b, 4, dve.tensor_tensor(z[:, :, :], z[:, :, :], lng[:, None, :].to_broadcast([P, J, P]), ALU.mult))
            dve.tensor_tensor(z[:, :, :], z[:, :, :], lnb[:, None, :].to_broadcast([P, J, P]), ALU.add).then_inc(z_made, 1)

        def finish(b):
            dve.wait_ge(tz_made, b + 1)
            tchain(b, 5, dve.scalar_tensor_tensor(z[:, :, :], tz[:, :, :], 1.0, z[:, :, :], ALU.add, ALU.mult))
            dve.wait_ge(s1_made, b + 1)
            tchain(b, 6, dve.scalar_tensor_tensor(z[:, :, :], z[:, :, :], 0.5, s1[:, :, :], ALU.mult, ALU.mult))
            dve.wait_ge(xres_in, 16 * (b + 1))
            dve.tensor_tensor(xres[:, :, :], xres[:, :, :], z[:, :, :], ALU.add).then_inc(xo_made, 1)

        dve.sem_inc(xo_made, 1)
        dve.wait_ge(cols_in, 16 * 5)
        dve.wait_ge(half_made, 2)
        normalise(0)
        normalise2(0)
        dve.wait_ge(a_made, 1)
        dve.tensor_scalar(aneg[:, :], aneg[:, :], -1.0, None, ALU.mult)
        dve.wait_ge(w_in, 16 * 7)
        dve.wait_ge(wt_done, 1)
        dve.tensor_tensor(wtmp[:, 2, :], G[1][:, 0:P], wtmp[:, 0, :], ALU.mult)
        dve.tensor_tensor(wset[:, :, :], wset[:, :, :], wtmp[:, 0:1, :].to_broadcast([P, 4, P]),
                          ALU.mult).then_inc(small_made, 1)
        dve.wait_ge(small_hi, 1)
        dve.tensor_tensor(wtl[:, :], wtmp[:, 2, :], wth[:, :].bitcast(F32), ALU.subtract)
        dve.tensor_tensor(wsl[:, :, :], wset[:, :, :], wsh[:, :, :].bitcast(F32), ALU.subtract).then_inc(small_lo, 1)
        split_normed(0, 0)
        route(0)
        route2(0)
        step_in(0, True)
        softmax_of_two(0)
        one_plus(0, 0)
        softplus(0)
        states_input(0, True)
        split_sets(0, 0)
        keep_comb(0, True)

        def body(b, par, first, last):
            for e in range(E):
                n = PER * e
                states_in(b, n, first)
                if e < 2 and not first:
                    weigh(b - 1, 1 - par, E - 2 + e, False)
                if e > 1:
                    weigh(b, par, e - 2, first)
                state_scan(b, n)
                states_in(b, n + 1, first)
                if e == 3 and not last:
                    split_normed(b + 1, 1 - par)
                if e == 7 and not last:
                    split_sets(b + 1, 0)
                states_out(b, par, n, first)
                if e == 6 and not last:
                    one_plus(b + 1, 1 - par)
                if e > 0:
                    low_part(b, e - 1)
                elif not first:
                    low_part(b - 1, E - 1)
                state_scan(b, n + 1)
                if e == 0 and not last:
                    normalise(b + 1)
                if e == 1:
                    split_sets(b, 1)
                    if not last:
                        normalise2(b + 1)
                if e == 3 and not first:
                    norm_experts(b - 1)
                if e == 4:
                    if not first:
                        norm_experts2(b - 1)
                    if not last:
                        route(b + 1)
                if e == 5 and not last:
                    step_in(b + 1, False)
                states_out(b, par, n + 1, first)
                if e == 4 and not last:
                    route2(b + 1)
                if e == 5 and not first:
                    scale_experts(b - 1)
                if e == 6 and not last:
                    softplus(b + 1)
                    softmax_of_two(b + 1)
                if e == 7:
                    if not first:
                        finish(b - 1)
                    if not last:
                        states_input(b + 1, False)
                        keep_comb(b + 1, False)

        rolled(dve, body)
        low_part(B - 1, E - 1)
        weigh(B - 1, (B - 1) % 2, E - 2, False)
        weigh(B - 1, (B - 1) % 2, E - 1, False)
        norm_experts(B - 1)
        norm_experts2(B - 1)
        scale_experts(B - 1)
        finish(B - 1)


def build_program(nc, dram):
    from contextlib import ExitStack

    from concourse import mybir

    F32, F32R = mybir.dt.float32, mybir.dt.float32r
    P, C = 128, 4
    EXPERTS = dram["ew1"].shape[0]
    S = dram["x"].shape[1]

    with ExitStack() as ctx:
        def sb(name, shape, dt=F32):
            return ctx.enter_context(nc.sbuf_tensor(name, shape, dt))

        def psum(name):
            return ctx.enter_context(nc.psum_tensor(name, [P, 512], F32))

        shared = {
            "w1h": sb("w1h", [P, EXPERTS, C * P], F32R), "w1l": sb("w1l", [P, EXPERTS, C * P], F32R),
            "w2h": sb("w2h", [P, EXPERTS * C, P], F32R), "w2l": sb("w2l", [P, EXPERTS * C, P], F32R),
            "hh": [sb(f"hh{i}", [P, S], F32R) for i in range(2 * C)],
            "hl": [sb(f"hl{i}", [P, S], F32R) for i in range(2 * C)],
            "t": [sb(f"t{i}", [P, S]) for i in range(2)],
            "acc": sb("acc", [P, S]),
            "ident": sb("ident", [P, P]), "iota8": sb("iota8", [P, 4 * EXPERTS]),
            "PH": [psum(f"PH{i}") for i in range(4)], "PY": psum("PY"), "G": [psum(f"G{i}") for i in range(3)],
        }
        with ExitStack() as own:
            run_layer0(nc, own, shared, dram)
        with ExitStack() as own:
            run_layer1(nc, own, shared, dram)


def lay_out(i):
    import numpy as np

    P, HEADS = 128, 16
    E = i["L0_ffn_eb1"].shape[0]
    D_HEAD = P // HEADS
    NS, R = i["L1_attn_A_log"].shape[1], i["L1_attn_Wdt"].shape[1]

    def columns(a):
        return np.asarray(a).reshape(-1, P).T

    def chunks(b):
        return np.asarray(b).reshape(-1, P).T

    wx = np.asarray(i["L1_attn_Wx"])
    head = np.repeat(np.arange(HEADS), D_HEAD)
    place = np.tile(np.arange(D_HEAD), HEADS)
    same_head = head[:, None] == head[None, :]
    out = {
        "x": i["L0_attn_x"],
        "cols0": np.concatenate([chunks(i["L0_ffn_eb1"]), columns(i["L0_ffn_sb1"]), chunks(i["L0_ffn_eb2"]),
                                 columns(i["L0_ffn_sb2"]), columns(i["L0_attn_time_decay"]),
                                 columns(i["L0_attn_time_mix_v"]), columns(i["L0_attn_time_mix_r"]),
                                 columns(i["L0_ffn_norm_weight"])], axis=1),
        "rw": np.asarray(i["L0_ffn_router_w"]).T,
        "ident": np.eye(P, dtype=np.float32),
        "iota8": np.tile(np.arange(E, dtype=np.float32), (P, 4)),
        "wa": np.stack([np.asarray(i["L0_attn_Wv"]), np.asarray(i["L0_attn_Wo"]).T, np.asarray(i["L0_attn_Wr"]).T]),
        "ew1": i["L0_ffn_ew1"], "ew2": i["L0_ffn_ew2"], "sw1": i["L0_ffn_sw1"], "sw2": i["L0_ffn_sw2"],
        "cols1": np.concatenate([chunks(i["L1_ffn_b1"]), chunks(i["L1_ffn_b2"]),
                                 np.tile(np.asarray(i["L1_attn_bdt"]), HEADS)[:, None],
                                 np.repeat(np.asarray(i["L1_attn_A_log"]), D_HEAD, axis=0)], axis=1),
        "gb": np.tile(np.asarray(i["L1_ffn_gate_b"]), (P, 4)),
        "lng": np.tile(np.asarray(i["L1_ffn_ln_g"]), (P, 1)),
        "lnb": np.tile(np.asarray(i["L1_ffn_ln_b"]), (P, 1)),
        "gw": i["L1_ffn_gate_w"],
        "mask": same_head.astype(np.float32),
        "wout": np.asarray(i["L1_attn_Wout"]).T,
        "bout": np.tile(np.asarray(i["L1_attn_bout"]), (1, 4)),
        "ws": np.stack([np.tile(wx[R + k * D_HEAD:R + (k + 1) * D_HEAD].T, (HEADS, HEADS))
                        for k in range(2 * NS // D_HEAD)]),
        "wxr": np.tile(wx[:R], (1, HEADS)),
        "wdt": np.tile(np.asarray(i["L1_attn_Wdt"]).T, (1, HEADS)),
        "pick": np.stack([same_head & (place == n)[:, None] for n in range(D_HEAD)]).astype(np.float32),
        "w1": i["L1_ffn_w1"], "w2": i["L1_ffn_w2"],
    }
    return {name: np.ascontiguousarray(a) for name, a in out.items()}




def kernel(**inputs):
    import concourse.bacc as bacc
    from concourse import mybir
    from concourse.bass_utils import run_bass_kernel_spmd

    nc = bacc.Bacc("TRN2", target_bir_lowering=False, num_devices=1, dynamic_dma_scratch_size=1024)
    arrays = lay_out(inputs)
    dram = {name: nc.dram_tensor("in_" + name, a.shape, mybir.dt.from_np(a.dtype), kind="ExternalInput").ap()
            for name, a in arrays.items()}
    B, S, D = arrays["x"].shape
    E = arrays["ew1"].shape[0]
    f32 = mybir.dt.float32
    dram["x1"] = nc.dram_tensor("x1", (B, S, D), f32, kind="Internal").ap()
    dram["comb0"] = nc.dram_tensor("comb0", (B, E, S), f32, kind="Internal").ap()
    dram["comb1"] = nc.dram_tensor("comb1", (B, E, S), f32, kind="Internal").ap()
    dram["out"] = nc.dram_tensor("out", (B, S, D), f32, kind="ExternalOutput").ap()
    build_program(nc, dram)
    result = run_bass_kernel_spmd(nc, [{"in_" + name: a for name, a in arrays.items()}], core_ids=[0])
    return result.results[0]["out"]
```

```python
def run_layer0(nc, ctx, shared, dram):
    from concourse import mybir

    F32, F32R, U32 = mybir.dt.float32, mybir.dt.float32r, mybir.dt.uint32
    ALU, ACT, AX = mybir.AluOpType, mybir.ActivationFunctionType, mybir.AxisListType

    def sb(name, shape, dt=F32):
        return ctx.enter_context(nc.sbuf_tensor("l0_" + name, shape, dt))

    def sem(name):
        return ctx.enter_context(nc.semaphore("l0_" + name))

    P = 128
    B, S = dram["x"].shape[:2]
    J = S // P
    EXPERTS = 8
    E = EXPERTS + 1
    C = 4
    N = E * C
    RING = 2 * C
    EARLY = 3
    LO_ON_POOL = (1, 2)
    LN_EPS, RMS_EPS, SUM_EPS = 1e-5, 1e-8, 1e-6

    w1h, w1l, w2h, w2l = (shared[k] for k in ("w1h", "w1l", "w2h", "w2l"))
    hh, hl = shared["hh"], shared["hl"]
    t, acc = shared["t"], shared["acc"]
    ident, iota8 = shared["ident"], shared["iota8"]
    PH, PY, G = shared["PH"], shared["PY"], shared["G"]

    CB1, CB2 = 0, E * C
    CTD, CMV, CMR, CNW = CB2 + E, CB2 + E + 1, CB2 + E + 2, CB2 + E + 3
    cols = sb("cols", [P, CNW + 1])
    hid = [sb(f"hid{i}", [P, S]) for i in range(C)]
    gate = [sb(f"gate{i}", [P, S]) for i in range(4)]
    sw1h, sw1l = sb("sw1h", [P, C * P], F32R), sb("sw1l", [P, C * P], F32R)
    sw2h, sw2l = sb("sw2h", [P, C, P], F32R), sb("sw2l", [P, C, P], F32R)
    stage = [sb(f"stage{i}", [P, 2 * C * P]) for i in range(3)]
    wa = sb("wa", [P, 4, P])
    rw = sb("rw", [P, EXPERTS])
    woh, wol = sb("woh", [P, P], F32R), sb("wol", [P, P], F32R)
    wrh, wrl = sb("wrh", [P, P], F32R), sb("wrl", [P, P], F32R)
    decay = sb("decay", [P, 2])
    half = sb("half", [P, 2 * C])
    xin, xres, xo = sb("xin", [P, J, P]), sb("xres", [P, J, P]), shared["xo"]
    xn, xr, sq = sb("xn", [P, J, P]), sb("xr", [P, J, P]), sb("sq", [P, J, P])
    st, mv = sb("st", [P, J, 6]), sb("mv", [P, J, 2])
    var, rstd = sb("var", [P, 2, J]), sb("rstd", [P, 2, J])
    xT, nT = sb("xT", [P, S]), sb("nT", [P, S])
    nh = [sb(f"nh{i}", [P, S], F32R) for i in range(2)]
    nl = [sb(f"nl{i}", [P, S], F32R) for i in range(2)]
    sums = sb("sums", [P, S + 1])
    dif, vin, rin = sb("dif", [P, S]), sb("vin", [P, S]), sb("rin", [P, S])
    vh, vl, rh, rl = (sb(n, [P, S], F32R) for n in ("vh", "vl", "rh", "rl"))
    tr = sb("tr", [P, S])
    rv = [sb(f"rv{i}", [P, S]) for i in range(2)]
    z, tz, q, prod = sb("z", [P, S]), sb("tz", [P, S]), sb("q", [P, S]), sb("prod", [P, S])
    key, ex = sb("key", [P, J, EXPERTS]), sb("ex", [P, J, EXPERTS])
    prob, eq = sb("prob", [P, J, EXPERTS]), sb("eq", [P, J, 2, EXPERTS])
    top, idx = sb("top", [P, J, 8]), sb("idx", [P, J, 8], U32)
    idxf, sel = sb("idxf", [P, J, 2]), sb("sel", [P, J, EXPERTS])
    tot, comb = sb("tot", [P, 3, J]), sb("comb", [P, J, EXPERTS])
    combT = sb("combT", [EXPERTS, S])

    cols_in, wa_in = sem("cols_in"), sem("wa_in")
    stage_in = [sem(f"stage_in{i}") for i in range(3)]
    hi_made, lo_made = sem("w_hi_made"), sem("w_lo_made")
    set_step = sem("setup_step")
    wvo_done, attn_w = sem("wvo_done"), sem("attn_w_split")
    decay_step, decay_made = sem("decay_step"), sem("decay_made")
    zero_made = sem("zero_made")
    xin_in, xres_in = sem("xin_in"), sem("xres_in")
    prep, tail = sem("prep_step"), sem("tail_step")
    var_made, rstd_made = sem("var_made"), sem("rstd_made")
    xn_made, xposed = sem("xn_made"), sem("x_transposed")
    xT_made, nT_made, nl_made = sem("xT_made"), sem("nT_made"), sem("nl_made")
    logits_done, ex_made = sem("logits_done"), sem("ex_made")
    comb_made, combT_done, combT_made = sem("comb_made"), sem("combT_done"), sem("combT_made")
    comb_out = sem("comb_out")
    mixed, mixed_hi, mixed_lo = sem("mixed"), sem("mixed_hi"), sem("mixed_lo")
    attn_done, tr_made, rv_made = sem("attn_done"), sem("tr_made"), sem("rv_made")
    gate_in = [sem(f"gate_in{i}") for i in range(len(gate))]
    up_done, hid_made = sem("up_done"), sem("hid_made")
    lo_dve, lo_pool = sem("lo_dve"), sem("lo_pool")
    y_done, t_made, acc_made = sem("y_done"), sem("t_made"), sem("acc_made")
    z_made, tz_made, prod_made = sem("z_made"), sem("tz_made"), sem("prod_made")
    prodT_done, xo_made, xo_out = sem("prodT_done"), sem("xo_made"), shared["x1_out"]

    dve_passed, sp_passed = sem("dve_passed"), sem("sp_passed")

    NP = len(LO_ON_POOL)
    ND = C - NP
    PREP, TAIL = 17, 1

    def first_weights(e):
        return (sw1h[:, :], sw1l[:, :]) if e == EXPERTS else (w1h[:, e, :], w1l[:, e, :])

    def second_weights(e):
        return (sw2h[:, :, :], sw2l[:, :, :]) if e == EXPERTS else (w2h[:, e * C:(e + 1) * C, :], w2l[:, e * C:(e + 1) * C, :])

    def slot_of(par, e, c):
        return (par * N + e * C + c) % RING

    x_tok = dram["x"].rearrange("b (j p) d -> b p j d", p=P)
    x1_tok = dram["x1"].rearrange("b (j p) d -> b p j d", p=P)

    def chained(eng, s, per):
        def step(b, n, ins):
            assert 1 <= n <= per
            ins.then_inc(s, 1)
            eng.wait_ge(s, b * per + n)
        return step

    def apart(eng, passed):
        eng.sem_inc(passed, 1)

    def rolled(eng, body):
        body(0, 0, True, False)
        with eng.Fori(0, (B - 2) // 2) as k:
            body(2 * k + 1, 1, False, False)
            body(2 * k + 2, 0, False, False)
        body(B - 1, 1, False, True)

    block = ctx.enter_context(nc.Block())

    @block.sync
    def _(sp):
        def load_x(b, first):
            if not first:
                sp.wait_ge(xn_made, b)
                apart(sp, sp_passed)
            sp.dma_start(xin[:, :, :], x_tok[b]).then_inc(xin_in, 16)

        def load_gate(b, e, first):
            s = e % len(gate)
            if e >= len(gate):
                sp.wait_ge(t_made, b * EXPERTS + e - len(gate) + 1)
            elif not first:
                sp.wait_ge(t_made, (b - 1) * EXPERTS + e + EXPERTS - len(gate) + 1)
            apart(sp, sp_passed)
            sp.dma_start(gate[s][:, :], dram["comb0"][b, e].partition_broadcast(P)).then_inc(gate_in[s], 16)

        def store_comb(b):
            sp.wait_ge(combT_made, b + 1)
            apart(sp, sp_passed)
            sp.dma_start(dram["comb0"][b], combT[:, :]).then_inc(comb_out, 16)

        def tail_dma(b):
            sp.wait_ge(xo_made, b + 1)
            apart(sp, sp_passed)
            sp.dma_start(xres[:, :, :], x_tok[b]).then_inc(xres_in, 16)

        def store_x1(b):
            sp.wait_ge(xo_made, b + 2)
            apart(sp, sp_passed)
            sp.dma_start(x1_tok[b], xo[:, :, :]).then_inc(xo_out, 16)

        def load_weights(i):
            s = i % 3
            if i >= 3:
                sp.wait_ge(hi_made, i - 2)
                sp.wait_ge(lo_made, i - 2)
            if i < EXPERTS:
                w1, w2 = dram["ew1"][i], dram["ew2"][i]
            elif i == EXPERTS:
                w1, w2 = dram["sw1"], dram["sw2"]
            else:
                w1, w2 = dram["w1"][i - E], dram["w2"][i - E]
            sp.dma_start(stage[s][:, 0:C * P], w1).then_inc(stage_in[s], 16)
            sp.dma_start(stage[s][:, C * P:].rearrange("p (c n) -> p c n", c=C),
                         w2.rearrange("(c p) n -> p c n", p=P)).then_inc(stage_in[s], 16)

        sp.sem_inc(xo_out, 16)
        load_x(0, True)
        sp.dma_start(wa[:, 0:3, :], dram["wa"].rearrange("k p n -> p k n")).then_inc(wa_in, 16)
        for i in range(EARLY + 3):
            load_weights(i)

        def body(b, par, first, last):
            if not last:
                load_x(b + 1, False)
            store_comb(b)
            sp.wait_ge(comb_out, 16 * (b + 1))
            apart(sp, sp_passed)
            if last:
                for e in range(3):
                    load_weights(E + e)
            for e in range(EXPERTS):
                load_gate(b, e, first)
                if first and 3 <= e < E - EARLY:
                    load_weights(EARLY + e)
                if last and e >= EXPERTS - 2:
                    load_weights(E + e - 3)
                if e == 0 and not first:
                    tail_dma(b - 1)
                if e == EXPERTS - 2 and not first:
                    store_x1(b - 1)

        rolled(sp, body)
        for e in range(EXPERTS - 3, EXPERTS):
            load_weights(E + e)
        tail_dma(B - 1)
        store_x1(B - 1)
        sp.wait_ge(xo_out, 16 * B)

    @block.tensor
    def _(pe):
        def three_pass(out, wh, wl, h, l, start=True, stop=True):
            pe.matmul(out, wh, h, start=start, stop=False)
            pe.matmul(out, wl, h, start=False, stop=False)
            return pe.matmul(out, wh, l, start=False, stop=stop)

        def up(b, par, e, c, first):
            if e == 0 and c == 0:
                pe.wait_ge(nl_made, b + 1)
            if first and c == 0:
                pe.wait_ge(hi_made, e + 1)
                pe.wait_ge(lo_made, e + 1)
            if not (first and e == 0):
                pe.wait_ge(hid_made, b * N + (e - 1) * C + c + 1)
            w = slice(c * P, (c + 1) * P)
            three_pass(PH[c][:, :], first_weights(e)[0][:, w], first_weights(e)[1][:, w], nh[par][:, :],
                       nl[par][:, :]).then_inc(up_done, 1)

        def down(b, par, e, c, first):
            if c == 0 and not (first and e == 0):
                if e == 0:
                    pe.wait_ge(z_made, b)
                else:
                    pe.wait_ge(t_made, b * EXPERTS + e)
            if c in LO_ON_POOL:
                pe.wait_ge(lo_pool, b * E * NP + e * NP + LO_ON_POOL.index(c) + 1)
            else:
                own = [k for k in range(C) if k not in LO_ON_POOL]
                pe.wait_ge(lo_dve, b * E * ND + e * ND + own.index(c) + 1)
            s = slot_of(par, e, c)
            last = three_pass(PY[:, :], second_weights(e)[0][:, c, :], second_weights(e)[1][:, c, :], hh[s][:, :],
                              hl[s][:, :], c == 0, c == C - 1)
            if c == C - 1:
                last.then_inc(y_done, 1)

        def transposes(dst, src):
            for j in range(J):
                last = pe.transpose(dst[:, j * P:(j + 1) * P], src[:, j, :], ident[:, :])
            return last

        def transpose_x(b, first):
            pe.wait_ge(xn_made, b + 1)
            if not first:
                pe.wait_ge(rv_made, b)
            transposes(G[0], xn)
            transposes(G[1], xr).then_inc(xposed, 1)

        def logits(b, first):
            pe.wait_ge(nT_made, b + 1)
            if not first:
                pe.wait_ge(combT_made, b)
            for j in range(J):
                last = pe.matmul(G[2][:, j * EXPERTS:(j + 1) * EXPERTS], nT[:, j * P:(j + 1) * P], rw[:, :],
                                 start=True, stop=True)
            last.then_inc(logits_done, 1)

        def transpose_comb(b):
            pe.wait_ge(comb_made, b + 1)
            for j in range(J):
                last = pe.transpose(G[2][0:EXPERTS, j * P:(j + 1) * P], comb[:, j, :], ident[:, :])
            last.then_inc(combT_done, 1)

        def attention(b):
            pe.wait_ge(mixed_lo, b + 1)
            pe.wait_ge(nT_made, b + 1)
            three_pass(G[0][:, :], woh[:, :], wol[:, :], vh[:, :], vl[:, :])
            three_pass(G[1][:, :], wrh[:, :], wrl[:, :], rh[:, :], rl[:, :]).then_inc(attn_done, 1)

        def transpose_prod(b):
            pe.wait_ge(prod_made, b + 1)
            pe.wait_ge(xo_made, b + 1)
            for j in range(J):
                last = pe.transpose(G[2][:, j * P:(j + 1) * P], prod[:, j * P:(j + 1) * P], ident[:, :])
            last.then_inc(prodT_done, 1)

        pe.wait_ge(wa_in, 16)
        pe.matmul(G[2][:, 0:P], wa[:, 0, :], wa[:, 1, :], start=True, stop=True).then_inc(wvo_done, 1)
        pe.wait_ge(cols_in, 16 * 4)
        transpose_x(0, True)
        pe.wait_ge(attn_w, 1)
        logits(0, True)

        def body(b, par, first, last):
            for e in range(E):
                def down_before(c):
                    if e > 0:
                        down(b, par, e - 1, c, first)
                    elif not first:
                        down(b - 1, 1 - par, E - 1, c, False)

                up(b, par, e, 0, first)
                up(b, par, e, 1, first)
                up(b, par, e, 2, first)
                down_before(0)
                down_before(1)
                up(b, par, e, 3, first)
                down_before(2)
                if e == 0 and first:
                    transpose_comb(0)
                    attention(0)
                if e == 3 and not first:
                    pe.wait_ge(combT_made, b + 1)
                    transpose_prod(b - 1)
                if e == 4 and not last:
                    transpose_x(b + 1, False)
                if e == 5 and not last:
                    if not first:
                        pe.wait_ge(xo_made, b + 1)
                    logits(b + 1, False)
                if e == 8 and not last:
                    transpose_comb(b + 1)
                    attention(b + 1)
                down_before(3)

        rolled(pe, body)
        for c in range(C):
            down(B - 1, (B - 1) % 2, E - 1, c, False)
        transpose_prod(B - 1)

    @block.scalar
    def _(act):
        def hidden(b, par, e, first):
            for c in range(C):
                act.wait_ge(up_done, b * N + e * C + c + 1)
                if not (first and e < 2):
                    act.wait_ge(y_done, b * E + e - 1)
                if not (first and e == 0):
                    if c in LO_ON_POOL:
                        act.wait_ge(lo_pool, b * E * NP + (e - 1) * NP + LO_ON_POOL.index(c) + 1)
                    else:
                        own = [k for k in range(C) if k not in LO_ON_POOL]
                        act.wait_ge(lo_dve, b * E * ND + (e - 1) * ND + own.index(c) + 1)
                bias = cols[:, CB1 + e * C + c:CB1 + e * C + c + 1]
                act.activation(hh[slot_of(par, e, c)][:, :], PH[c][:, :], ACT.Relu, bias=bias)
                act.activation(hid[c][:, :], PH[c][:, :], ACT.Relu, bias=bias).then_inc(hid_made, 1)

        def evacuate_x(b, par, first):
            act.wait_ge(xposed, b + 1)
            if not first:
                act.wait_ge(mixed, b)
                act.wait_ge(nl_made, b)
                act.wait_ge(logits_done, b)
            act.activation(xT[:, :], G[0][:, :], ACT.Identity).then_inc(xT_made, 1)
            nw = cols[:, CNW:CNW + 1]
            act.activation(nT[:, :], G[1][:, :], ACT.Identity, scale=nw)
            act.activation(nh[par][:, :], G[1][:, :], ACT.Identity, scale=nw).then_inc(nT_made, 1)

        def router_exp(b):
            act.wait_ge(logits_done, b + 1)
            act.activation(ex[:, :, :], G[2][:, 0:J * EXPERTS].rearrange("p (j e) -> p j e", j=J), ACT.Exp,
                           scale=-1.0).then_inc(ex_made, 1)

        def split_mixed(b, first):
            act.wait_ge(mixed, b + 1)
            if not first:
                act.wait_ge(attn_done, b)
            act.activation(vh[:, :], vin[:, :], ACT.Identity)
            act.activation(rh[:, :], rin[:, :], ACT.Identity).then_inc(mixed_hi, 1)

        def tanh_r(b, first):
            act.wait_ge(attn_done, b + 1)
            if not first:
                act.wait_ge(rv_made, b)
            act.activation(tr[:, :], G[1][:, :], ACT.Tanh, scale=0.5).then_inc(tr_made, 1)

        def tanh_z(b, first):
            act.wait_ge(z_made, b + 1)
            act.activation(tz[:, :], z[:, :], ACT.Tanh, scale=0.5).then_inc(tz_made, 1)

        act.dma_start(cols[:, :], dram["cols0"]).then_inc(cols_in, 16)
        act.dma_start(rw[:, :], dram["rw"]).then_inc(cols_in, 16)
        act.dma_start(ident[:, :], dram["ident"]).then_inc(cols_in, 16)
        act.dma_start(iota8[:, :], dram["iota8"]).then_inc(cols_in, 16)
        act.wait_ge(cols_in, 16 * 4)
        act.activation(decay[:, 0:1], cols[:, CTD:CTD + 1], ACT.Exp).then_inc(decay_step, 1)
        act.wait_ge(decay_step, 1)
        act.activation(decay[:, 1:2], decay[:, 0:1], ACT.Exp, scale=-1.0).then_inc(decay_made, 1)
        act.wait_ge(wvo_done, 1)
        act.activation(wa[:, 3, :], G[2][:, 0:P], ACT.Identity)
        act.activation(woh[:, :], G[2][:, 0:P], ACT.Identity)
        act.activation(wrh[:, :], wa[:, 2, :], ACT.Identity).then_inc(set_step, 1)

        def split_weights(i):
            act.wait_ge(stage_in[i % 3], 32 * (i // 3 + 1))
            if i >= E:
                act.wait_ge(y_done, (B - 1) * E + i - E + 1)
            e = i % E
            act.activation(first_weights(e)[0], stage[i % 3][:, 0:C * P], ACT.Identity)
            act.activation(second_weights(e)[0], stage[i % 3][:, C * P:].rearrange("p (c n) -> p c n", c=C),
                           ACT.Identity).then_inc(hi_made, 1)

        split_weights(0)
        evacuate_x(0, 0, True)
        split_weights(1)
        router_exp(0)
        split_weights(2)
        split_mixed(0, True)
        def body(b, par, first, last):
            for e in range(E):
                hidden(b, par, e, first)
                if first and e < E - EARLY:
                    split_weights(EARLY + e)
                if last and e >= 2:
                    split_weights(E + e - 2)
                if e == 0 and first:
                    tanh_r(0, True)
                if e == 1 and not first:
                    tanh_z(b - 1, False)
                if e == 4 and not last:
                    evacuate_x(b + 1, 1 - par, False)
                if e == 5 and not last:
                    router_exp(b + 1)
                if e == 6 and not last:
                    split_mixed(b + 1, False)
            if not last:
                tanh_r(b + 1, False)

        rolled(act, body)
        split_weights(E + EXPERTS - 1)
        tanh_z(B - 1, False)

    @block.gpsimd
    def _(pool):
        def power(b, k):
            pool.wait_ge(var_made, 2 * b + k)
            pool.tensor_tensor(rstd[:, k - 1, :], var[:, k - 1, :], half[:, 0:J], ALU.pow).then_inc(rstd_made, 1)

        def low_part(b, par, e, chunks):
            for c in chunks:
                s = slot_of(par, e, c)
                pool.wait_ge(hid_made, b * N + e * C + c + 1)
                pool.tensor_tensor(hl[s][:, :], hid[c][:, :], hh[s][:, :].bitcast(F32), ALU.subtract).then_inc(lo_pool, 1)

        def accumulate(b, e):
            pool.wait_ge(t_made, b * EXPERTS + e + 1)
            if e >= 2:
                pool.wait_ge(acc_made, b * (EXPERTS - 1) + e - 1)
            pool.tensor_tensor(acc[:, :], acc[:, :], t[e % 2][:, :], ALU.add).then_inc(acc_made, 1)

        def split_weights(i):
            pool.wait_ge(hi_made, i + 1)
            e, w = i % E, stage[i % 3]
            pool.tensor_tensor(first_weights(e)[1], w[:, 0:C * P], first_weights(e)[0].bitcast(F32), ALU.subtract)
            pool.tensor_tensor(second_weights(e)[1], w[:, C * P:].rearrange("p (c n) -> p c n", c=C),
                               second_weights(e)[0].bitcast(F32), ALU.subtract).then_inc(lo_made, 1)

        pool.memset(half[:, :], -0.5).then_inc(zero_made, 1)
        pool.memset(sums[:, 0:1], 0.0).then_inc(zero_made, 1)
        pool.wait_ge(zero_made, 2)
        power(0, 1)
        power(0, 2)
        for i in range(EARLY):
            split_weights(i)

        def body(b, par, first, last):
            for e in range(E):
                low_part(b, par, e, LO_ON_POOL[:1])
                if e == 0 and not first:
                    accumulate(b - 1, EXPERTS - 1)
                if e >= 3:
                    accumulate(b, e - 2)
                low_part(b, par, e, LO_ON_POOL[1:])
                if e == 0 and not last:
                    power(b + 1, 1)
                if e == 2 and not last:
                    power(b + 1, 2)
                if first and e < E - EARLY:
                    split_weights(EARLY + e)
                if last and e >= 2:
                    split_weights(E + e - 2)

        rolled(pool, body)
        accumulate(B - 1, EXPERTS - 1)
        split_weights(E + EXPERTS - 1)

    @block.vector
    def _(dve):
        chain, tchain = chained(dve, prep, PREP), chained(dve, tail, TAIL)
        own = [c for c in range(C) if c not in LO_ON_POOL]

        def low_part(b, par, e, chunks):
            for c in chunks:
                s = slot_of(par, e, c)
                dve.wait_ge(hid_made, b * N + e * C + c + 1)
                dve.tensor_tensor(hl[s][:, :], hid[c][:, :], hh[s][:, :].bitcast(F32), ALU.subtract).then_inc(lo_dve, 1)

        def weigh(b, e, first):
            dve.wait_ge(y_done, b * E + e + 1)
            b2 = cols[:, CB2 + e:CB2 + e + 1]
            if e == EXPERTS:
                dve.wait_ge(acc_made, (b + 1) * (EXPERTS - 1))
                dve.scalar_tensor_tensor(z[:, :], PY[:, :], b2, acc[:, :], ALU.add, ALU.add).then_inc(z_made, 1)
                return
            s = e % len(gate)
            dve.wait_ge(gate_in[s], 16 * (b * (EXPERTS // len(gate)) + e // len(gate) + 1))
            if e == 0:
                out = acc
                if not first:
                    dve.wait_ge(z_made, b)
            else:
                out = t[e % 2]
                if e >= 3:
                    dve.wait_ge(acc_made, b * (EXPERTS - 1) + e - 2)
            dve.scalar_tensor_tensor(out[:, :], PY[:, :], b2, gate[s][:, :], ALU.add, ALU.mult).then_inc(t_made, 1)

        def normalise(b, first):
            dve.wait_ge(xin_in, 16 * (b + 1))
            if not first:
                dve.wait_ge(xposed, b)
            for j in range(J):
                i = dve.bn_stats(st[:, j, :], xin[:, j, :])
            chain(b, 1, i)
            apart(dve, dve_passed)
            for j in range(J):
                i = dve.bn_aggr(mv[:, j, :], st[:, j, :])
            chain(b, 2, i)
            dve.tensor_scalar(var[:, 0, :], mv[:, :, 1], LN_EPS, None, ALU.add).then_inc(var_made, 1)

        def normalise2(b):
            dve.wait_ge(rstd_made, 2 * b + 1)
            for j in range(J):
                i = dve.tensor_scalar(xn[:, j, :], xin[:, j, :], mv[:, j, 0:1], rstd[:, 0, j:j + 1],
                                      ALU.subtract, ALU.mult)
            chain(b, 3, i)

            chain(b, 4, dve.tensor_tensor(sq[:, :, :], xn[:, :, :], xn[:, :, :], ALU.mult))

        def rms(b):
            chain(b, 5, dve.tensor_reduce(tot[:, 2, :], sq[:, :, :], AX.X, ALU.add))
            dve.tensor_scalar(var[:, 1, :], tot[:, 2, :], 1.0 / P, RMS_EPS, ALU.mult, ALU.add).then_inc(var_made, 1)

        def rms2(b):
            dve.wait_ge(rstd_made, 2 * b + 2)
            for j in range(J):
                i = dve.tensor_scalar(xr[:, j, :], xn[:, j, :], rstd[:, 1, j:j + 1], None, ALU.mult)
            i.then_inc(xn_made, 1)

        def split_normed(b, par):
            dve.wait_ge(nT_made, b + 1)
            dve.tensor_tensor(nl[par][:, :], nT[:, :], nh[par][:, :].bitcast(F32), ALU.subtract).then_inc(nl_made, 1)

        def mix(b):
            dve.wait_ge(xT_made, b + 1)
            chain(b, 6, dve.tensor_tensor_scan(sums[:, 1:S + 1], decay[:, 1:2].to_broadcast([P, S]), xT[:, :], 0.0,
                                               ALU.mult, ALU.add))
            prev = sums[:, 0:S]
            chain(b, 7, dve.tensor_tensor(dif[:, :], xT[:, :], prev, ALU.subtract))

        def mix2(b):
            prev = sums[:, 0:S]
            dve.scalar_tensor_tensor(vin[:, :], dif[:, :], cols[:, CMV:CMV + 1], prev, ALU.mult, ALU.add)
            dve.scalar_tensor_tensor(rin[:, :], dif[:, :], cols[:, CMR:CMR + 1], prev, ALU.mult,
                                     ALU.add).then_inc(mixed, 1)

        def split_mixed(b):
            dve.wait_ge(mixed_hi, b + 1)
            dve.tensor_tensor(vl[:, :], vin[:, :], vh[:, :].bitcast(F32), ALU.subtract)
            dve.tensor_tensor(rl[:, :], rin[:, :], rh[:, :].bitcast(F32), ALU.subtract).then_inc(mixed_lo, 1)

        def route_keys(b):
            dve.wait_ge(ex_made, b + 1)
            chain(b, 8, dve.tensor_scalar(key[:, :, :], G[2][:, 0:J * EXPERTS].rearrange("p (j e) -> p j e", j=J),
                                          17.0, -88.0, ALU.min, ALU.max))
            apart(dve, dve_passed)
            for j in range(J):
                i = dve.max(top[:, j, :], key[:, j, :])
            chain(b, 9, i)
            apart(dve, dve_passed)
            for j in range(J):
                i = dve.max_index(idx[:, j, :], top[:, j, :], key[:, j, :])
            chain(b, 10, i)
            chain(b, 11, dve.tensor_copy(idxf[:, :, :], idx[:, :, 0:2]))

        def route(b):
            for k in range(2):
                dve.tensor_tensor(eq[:, :, k, :], iota8[:, :].rearrange("p (j e) -> p j e", j=J),
                                  idxf[:, :, k:k + 1].to_broadcast([P, J, EXPERTS]), ALU.is_equal)
            chain(b, 12, dve.tensor_scalar(ex[:, :, :], ex[:, :, :], 1.0, None, ALU.add))
            dve.tensor_tensor(sel[:, :, :], eq[:, :, 0, :], eq[:, :, 1, :], ALU.add)
            chain(b, 13, dve.reciprocal(prob[:, :, :], ex[:, :, :]))
            chain(b, 14, dve.tensor_tensor(sel[:, :, :], sel[:, :, :], prob[:, :, :], ALU.mult))
            chain(b, 15, dve.tensor_reduce(tot[:, 0, :], sel[:, :, :], AX.X, ALU.add))
            chain(b, 16, dve.tensor_scalar(tot[:, 0, :], tot[:, 0, :], SUM_EPS, None, ALU.add))
            chain(b, 17, dve.reciprocal(tot[:, 1, :], tot[:, 0, :]))
            dve.tensor_tensor(comb[:, :, :], sel[:, :, :], tot[:, 1:2, :].rearrange("p k j -> p j k").to_broadcast([P, J, EXPERTS]),
                              ALU.mult).then_inc(comb_made, 1)

        def keep_comb(b, first):
            dve.wait_ge(combT_done, b + 1)
            if not first:
                dve.wait_ge(comb_out, 16 * b)
            dve.tensor_copy(combT[:, :], G[2][0:EXPERTS, :]).then_inc(combT_made, 1)

        def gated(b, par):
            dve.wait_ge(tr_made, b + 1)
            dve.scalar_tensor_tensor(rv[par][:, :], tr[:, :], 1.0, G[0][:, :], ALU.add, ALU.mult).then_inc(rv_made, 1)

        def product(b, par):
            dve.wait_ge(tz_made, b + 1)
            tchain(b, 1, dve.scalar_tensor_tensor(q[:, :], tz[:, :], 1.0, z[:, :], ALU.add, ALU.mult))
            dve.scalar_tensor_tensor(prod[:, :], q[:, :], 0.25, rv[par][:, :], ALU.mult, ALU.mult).then_inc(prod_made, 1)

        def add_residual(b):
            dve.wait_ge(prodT_done, b + 1)
            dve.wait_ge(xres_in, 16 * (b + 1))
            dve.wait_ge(xo_out, 16 * (b + 1))
            dve.tensor_tensor(xo[:, :, :].rearrange("p j d -> p (j d)"), G[2][:, :],
                              xres[:, :, :].rearrange("p j d -> p (j d)"), ALU.add).then_inc(xo_made, 1)

        dve.sem_inc(xo_made, 1)
        dve.wait_ge(zero_made, 2)
        normalise(0, True)
        normalise2(0)
        rms(0)
        rms2(0)
        dve.wait_ge(set_step, 1)
        dve.tensor_tensor(wol[:, :], wa[:, 3, :], woh[:, :].bitcast(F32), ALU.subtract)
        dve.tensor_tensor(wrl[:, :], wa[:, 2, :], wrh[:, :].bitcast(F32), ALU.subtract).then_inc(attn_w, 1)
        dve.wait_ge(decay_made, 1)
        dve.wait_ge(cols_in, 16 * 4)
        split_normed(0, 0)
        mix(0)
        mix2(0)
        route_keys(0)

        def body(b, par, first, last):
            for e in range(E):
                if e > 1:
                    weigh(b, e - 2, first)
                elif not first:
                    weigh(b - 1, E - 2 + e, False)
                if e > 0:
                    low_part(b, par, e - 1, own[1:])
                elif not first:
                    low_part(b - 1, 1 - par, E - 1, own[1:])
                low_part(b, par, e, own[:1])
                if e == 0 and first:
                    route(0)
                    split_mixed(0)
                if e == 1 and first:
                    keep_comb(0, True)
                    gated(0, 0)
                if e == 0:
                    if not first:
                        keep_comb(b, False)
                        gated(b, par)
                    if not last:
                        normalise(b + 1, False)
                if e == 1 and not last:
                    normalise2(b + 1)
                if e == 2:
                    if not first:
                        product(b - 1, 1 - par)
                    if not last:
                        rms(b + 1)
                if e == 3 and not last:
                    rms2(b + 1)
                if e == 4 and not first:
                    add_residual(b - 1)
                if e == 5 and not last:
                    split_normed(b + 1, 1 - par)
                    mix(b + 1)
                if e == 6 and not last:
                    mix2(b + 1)
                    route_keys(b + 1)
                if e == 7 and not last:
                    route(b + 1)
                    split_mixed(b + 1)
        rolled(dve, body)
        low_part(B - 1, (B - 1) % 2, E - 1, own[1:])
        weigh(B - 1, E - 2, False)
        weigh(B - 1, E - 1, False)
        product(B - 1, 1)
        add_residual(B - 1)


def run_layer1(nc, ctx, shared, dram):
    from concourse import mybir

    F32, F32R, U32 = mybir.dt.float32, mybir.dt.float32r, mybir.dt.uint32
    ALU, ACT, AX = mybir.AluOpType, mybir.ActivationFunctionType, mybir.AxisListType

    def sb(name, shape, dt=F32):
        return ctx.enter_context(nc.sbuf_tensor("l1_" + name, shape, dt))

    def sem(name):
        return ctx.enter_context(nc.semaphore("l1_" + name))

    P = 128
    B, S = dram["x"].shape[:2]
    J = S // P
    E = 8
    C = 4
    N = E * C
    RING = 2 * C
    HID = C
    BANKS = 3
    NS = 16
    PER = NS // E
    HALF = 8
    SOON, LATE = 4, 4
    RX = 4
    R = dram["wx"].shape[1]
    LO_ON_DVE = [(2, 3) if e in (1, 7) else (3,) for e in range(E)]
    LN_EPS, TEMP = 1e-5, 0.9

    w1h, w1l, w2h, w2l = (shared[k] for k in ("w1h", "w1l", "w2h", "w2l"))
    hh, hl = shared["hh"], shared["hl"]
    t, acc = shared["t"], [shared["acc"], sb("acc1", [P, S])]
    ident, iota8 = shared["ident"], shared["iota8"]
    PH, PY, G = shared["PH"][0:3], shared["PY"], shared["G"][0:2]
    PB, PC = shared["PH"][3], shared["G"][2]

    CB1, CB2 = 0, E * C
    CBDT, CA = CB2 + E, CB2 + E + 1
    CGW, CLG, CLB = CA + NS + J * E, CA + NS + (J + 1) * E, CA + NS + (J + 1) * E + P
    cols = sb("cols", [P, CLB + P])
    aneg = sb("aneg", [P, NS])
    gb = cols[:, CA + NS:CGW].rearrange("p (j e) -> p j e", j=J)
    gw = cols[:, CGW:CLG]
    lng, lnb = cols[:, CLG:CLB], cols[:, CLB:CLB + P]
    half = sb("half", [P, J])
    hid = [sb(f"hid{i}", [P, S]) for i in range(HID)]
    gate = [sb(f"gate{i}", [P, S]) for i in range(2)]
    wth, wtl = sb("wth", [P, P], F32R), sb("wtl", [P, P], F32R)
    wo = sb("wo", [P, P])
    wsh, wsl = sb("wsh", [P, 4, P], F32R), sb("wsl", [P, 4, P], F32R)
    pick = sb("pick", [P, HALF, P], F32R)
    nh = [sb(f"nh{i}", [P, S], F32R) for i in range(2)]
    nl = [sb(f"nl{i}", [P, S], F32R) for i in range(2)]
    xn, xT = sb("xn", [P, J, P]), sb("xT", [P, S])
    dt, u = sb("dt", [P, S]), sb("u", [P, S])
    soft = sb("soft", [P, S])
    abar = sb("abar", [P, NS, S])
    bch, bcl = sb("bch", [P, 4, S], F32R), sb("bcl", [P, 4, S], F32R)
    bx = [sb(f"bx{i}", [P, S]) for i in range(RX)]
    y = [sb(f"y{i}", [P, S]) for i in range(2)]
    s1 = sb("s1", [P, J, P])
    ones, bout = sb("ones", [1, P]), sb("bout", [1, S])
    ln = sb("ln", [P, S])
    z = sb("z", [P, J, P])
    tz = xn
    xres = sb("xres", [P, J, P])
    st, mv = sb("st", [P, J, 6]), sb("mv", [P, J, 2])
    st2, mv2 = sb("st2", [P, J, 6]), sb("mv2", [P, J, 2])
    var, rstd = sb("var", [P, 2, J]), sb("rstd", [P, 2, J])
    lg, eq = sb("lg", [P, J, E]), sb("eq", [P, J, 2, E])
    top, idx = sb("top", [P, J, 8]), sb("idx", [P, J, 8], U32)
    idxf, gap, th = sb("idxf", [P, J, 2]), sb("gap", [P, J, 1]), sb("th", [P, J, 2])
    comb = sb("comb", [P, J, E])
    combT = xn[0:E, :, :].rearrange("p j d -> p (j d)")
    wtmp = abar[:, 6:8, :].rearrange("p k (m n) -> p (k m) n", n=P)
    mask, wset, wt = wtmp[:, 0:1, :], wtmp[:, 1:5, :], wtmp[:, 5, :]
    wx64 = abar[0:R, 10:11, 0:2 * P].rearrange("p k (m n) -> p (k m) n", n=P)
    picks = abar[:, 12:14, :].rearrange("p k (m n) -> p (k m) n", n=P)

    cols_in, w_in = sem("cols_in"), sem("w_in")
    half_made = sem("half_made")
    wt_done, small_made = sem("wt_done"), sem("small_made")
    small_hi, small_lo = sem("small_hi"), sem("small_lo")
    a_made = sem("a_made")
    xin_in, xres_in = sem("xin_in"), sem("xres_in")
    prep, tail = sem("prep_step"), sem("tail_step")
    var_made, rstd_made = sem("var_made"), sem("rstd_made")
    tvar_made, trstd_made = sem("tail_var_made"), sem("tail_rstd_made")
    xn_made, xposed, nT_made, nl_made = sem("xn_made"), sem("x_transposed"), sem("nT_made"), sem("nl_made")
    logits_done, gap_made, th_made = sem("logits_done"), sem("gap_made"), sem("th_made")
    comb_made, combT_done, combT_made, comb_out = sem("comb_made"), sem("combT_done"), sem("combT_made"), sem("comb_out")
    dt_done, v_made, e_made, e1_made, ln_made = sem("dt_done"), sem("v_made"), sem("e_made"), sem("e1_made"), sem("ln_made")
    left_out, kept_made = sem("left_out"), sem("kept_made")
    dt_made, u_made, abar_made = sem("dt_made"), sem("u_made"), sem("abar_made")
    set_done, set_hi, set_lo = sem("set_done"), sem("set_hi"), sem("set_lo")
    b_done, c_done, bx_made, scan_made, m_made, y_made = (
        sem("b_done"), sem("c_done"), sem("bx_made"), sem("scan_made"), sem("m_made"), sem("y_made"))
    wout_done, s1_made = sem("wout_done"), sem("s1_made")
    gate_in = [sem(f"gate_in{i}") for i in range(len(gate))]
    up_done, hid_made, lo_dve, lo_pool = sem("up_done"), sem("hid_made"), sem("lo_dve"), sem("lo_pool")
    y2_done, t_made, acc_made = sem("expert_done"), sem("t_made"), sem("acc_made")
    accT_done, accT_made, z_made, tz_made = sem("accT_done"), sem("accT_made"), sem("z_made"), sem("tz_made")
    xo_made, xo_out = sem("xo_made"), sem("xo_out")

    dve_passed, sp_passed = sem("dve_passed"), sem("sp_passed")

    PREP, TAIL = 9, 6
    BY_DVE = [(e, c) for e in range(E) for c in LO_ON_DVE[e]]
    BY_POOL = [(e, c) for e in range(E) for c in range(C) if c not in LO_ON_DVE[e]]

    def slot_of(e, c):
        return (e * C + c) % RING

    def lo_ready(eng, b, e, c):
        for made, by in ((lo_pool, BY_POOL), (lo_dve, BY_DVE)):
            if (e, c) in by:
                eng.wait_ge(made, b * len(by) + by.index((e, c)) + 1)

    x1_tok = dram["x1"].rearrange("b (j p) d -> b p j d", p=P)
    out_tok = dram["out"].rearrange("b (j p) d -> b p j d", p=P)

    def chained(eng, s, per):
        def step(b, n, ins):
            assert 1 <= n <= per
            ins.then_inc(s, 1)
            eng.wait_ge(s, b * per + n)
        return step

    def apart(eng, passed):
        eng.sem_inc(passed, 1)

    def rolled(eng, body):
        body(0, 0, True, False)
        with eng.Fori(0, (B - 2) // 2) as k:
            body(2 * k + 1, 1, False, False)
            body(2 * k + 2, 0, False, False)
        body(B - 1, 1, False, True)

    block = ctx.enter_context(nc.Block())

    @block.sync
    def _(sp):
        def load_x(b, first):
            if not first:
                sp.wait_ge(xposed, b)
                apart(sp, sp_passed)
            sp.dma_start(xn[:, :, :], x1_tok[b]).then_inc(xin_in, 16)

        def load_gate(b, e, first):
            s = e % len(gate)
            if e >= len(gate) or not first:
                sp.wait_ge(t_made, b * E + e - len(gate) + 1)
            apart(sp, sp_passed)
            sp.dma_start(gate[s][:, :], dram["comb1"][b, e].partition_broadcast(P)).then_inc(gate_in[s], 16)

        def store_comb(b):
            sp.wait_ge(combT_made, b + 1)
            apart(sp, sp_passed)
            sp.dma_start(dram["comb1"][b], combT).then_inc(comb_out, 16)

        def load_residual(b):
            sp.wait_ge(xo_out, 16 * (b + 1))
            apart(sp, sp_passed)
            sp.dma_start(xres[:, :, :], x1_tok[b]).then_inc(xres_in, 16)

        def store_out(b):
            sp.wait_ge(xo_made, b + 2)
            apart(sp, sp_passed)
            sp.dma_start(out_tok[b], xres[:, :, :]).then_inc(xo_out, 16)

        sp.sem_inc(xo_out, 16)
        load_x(0, True)
        sp.dma_start(wx64[:, :, :], dram["wx"].rearrange("k p n -> p k n")).then_inc(w_in, 16)
        sp.dma_start(wtmp[:, 0:5, :], dram["ws"].rearrange("k p n -> p k n")).then_inc(w_in, 16)
        sp.dma_start(wo[:, :], dram["wout"]).then_inc(w_in, 16)
        sp.dma_start(bout[:, :], dram["bout"]).then_inc(w_in, 16)
        sp.dma_start(picks[:, :, :], dram["pick"].rearrange("k p n -> p k n")).then_inc(w_in, 16)
        store_comb(0)
        sp.wait_ge(shared["x1_out"], 16 * (B + 1))

        def body(b, par, first, last):
            sp.wait_ge(comb_out, 16 * (b + 1))
            apart(sp, sp_passed)
            if not last:
                load_x(b + 1, False)
            for e in range(E):
                load_gate(b, e, first)
                if e == 1 and not first:
                    load_residual(b - 1)
            if not first:
                store_out(b - 1)
            if not last:
                store_comb(b + 1)

        rolled(sp, body)
        load_residual(B - 1)
        store_out(B - 1)
        sp.wait_ge(xo_out, 16 * (B + 1))

    @block.tensor
    def _(pe):
        def three_pass(out, wh, wl, h, l, start=True, stop=True):
            pe.matmul(out, wh, h, start=start, stop=False)
            pe.matmul(out, wl, h, start=False, stop=False)
            return pe.matmul(out, wh, l, start=False, stop=stop)

        def up(b, par, e, c, first):
            k = e * C + c
            if k == 0:
                pe.wait_ge(nl_made, b + 1)
            if k >= BANKS:
                pe.wait_ge(hid_made, b * N + k - BANKS + 1)
            elif not first:
                before = max(n for n in range(N) if n % BANKS == k)
                pe.wait_ge(hid_made, (b - 1) * N + before + 1)
            w = slice(c * P, (c + 1) * P)
            three_pass(PH[k % BANKS][:, :], w1h[:, e, w], w1l[:, e, w], nh[par][:, :], nl[par][:, :]).then_inc(up_done, 1)

        def down(b, e, c):
            lo_ready(pe, b, e, c)
            s = slot_of(e, c)
            last = three_pass(PY[:, :], w2h[:, e * C + c, :], w2l[:, e * C + c, :], hh[s][:, :], hl[s][:, :],
                              c == 0, c == C - 1)
            if c == C - 1:
                last.then_inc(y2_done, 1)

        def spread(b, n, k, bank, done, read, first):
            if n % HALF == 0:
                pe.wait_ge(set_lo, 4 * b + 2 * (n // HALF + 1))
            if not (first and n == 0):
                pe.wait_ge(read, b * NS + n)
            s = 2 * k + n // HALF
            pe.matmul(bank[:, :], pick[:, n % HALF, :], bch[:, s, :], start=True, stop=False)
            pe.matmul(bank[:, :], pick[:, n % HALF, :], bcl[:, s, :], start=False, stop=True).then_inc(done, 1)

        def spread_b(b, n, first):
            spread(b, n, 0, PB, b_done, bx_made, first)

        def spread_c(b, n, first):
            spread(b, n, 1, PC, c_done, m_made, first)

        def compact(b, par, half):
            if half == 0:
                pe.wait_ge(gap_made, b + 1)
                pe.wait_ge(v_made, b + 1)
            else:
                pe.wait_ge(combT_made, b + 1)
                pe.wait_ge(set_lo, 4 * b + 2)
            for k in range(2):
                s = 2 * k + half
                three_pass(G[k][:, :], wsh[:, s, :], wsl[:, s, :], nh[par][:, :], nl[par][:, :]).then_inc(set_done, 1)

        def step_sizes(b, par):
            pe.wait_ge(nl_made, b + 1)
            three_pass(G[1][:, :], wth[:, :], wtl[:, :], nh[par][:, :], nl[par][:, :]).then_inc(dt_done, 1)

        def transposes(dst, src, s):
            for j in range(J):
                last = pe.transpose(dst[:, j * P:(j + 1) * P], src[:, j * P:(j + 1) * P], ident[:, :])
            last.then_inc(s, 1)

        def transpose_x(b, first):
            pe.wait_ge(xn_made, b + 1)
            if not first:
                pe.wait_ge(s1_made, b - 1)
            transposes(G[0], xn[:, :, :].rearrange("p j d -> p (j d)"), xposed)

        def logits(b):
            pe.wait_ge(nT_made, b + 1)
            for j in range(J):
                last = pe.matmul(G[0][:, j * E:(j + 1) * E], xT[:, j * P:(j + 1) * P], gw[:, :], start=True, stop=True)
            last.then_inc(logits_done, 1)

        def transpose_comb(b):
            pe.wait_ge(comb_made, b + 1)
            pe.wait_ge(set_lo, 4 * b + 1)
            for j in range(J):
                last = pe.transpose(G[0][0:E, j * P:(j + 1) * P], comb[:, j, :], ident[:, :])
            last.then_inc(combT_done, 1)

        def project(b, par):
            pe.wait_ge(y_made, (b + 1) * (NS - 1))
            pe.matmul(G[0][:, :], ones[:, :], bout[:, :], start=True, stop=False)
            for j in range(J):
                tok = slice(j * P, (j + 1) * P)
                last = pe.matmul(G[0][:, tok], y[par][:, tok], wo[:, :], start=False, stop=j == J - 1)
            last.then_inc(wout_done, 1)

        def transpose_acc(b, par):
            pe.wait_ge(acc_made, (b + 1) * (E - 1))
            transposes(G[1], acc[par], accT_done)

        pe.wait_ge(w_in, 16 * 5)
        pe.matmul(G[1][:, 0:P], wx64[:, 0, :], wx64[:, 1, :], start=True, stop=True).then_inc(wt_done, 1)
        pe.wait_ge(cols_in, 16)
        transpose_x(0, True)
        pe.wait_ge(small_lo, 1)
        logits(0)
        step_sizes(0, 0)
        compact(0, 0, 0)
        transpose_comb(0)

        def body(b, par, first, last):
            if first:
                spread_b(b, 0, first)
                spread_c(b, 0, first)
            for e in range(E):
                before = (b, e - 1) if e > 0 else None if first else (b - 1, E - 1)
                n = PER * e + 1
                following = None if last and e == E - 1 else (b + 1, 0, False) if e == E - 1 else (b, n + 1, first)

                def down_before(c):
                    if before and c == 0 and not (first and e == 1):
                        pe.wait_ge(t_made, before[0] * E + before[1])
                    if before:
                        down(*before, c)

                if e == 0:
                    spread_b(b, n, first)
                up(b, par, e, 0, first)
                up(b, par, e, 1, first)
                down_before(0)
                up(b, par, e, 2, first)
                down_before(1)
                spread_c(b, n, first)
                down_before(2)
                if following:
                    spread_b(*following)
                if e == 0:
                    compact(b, par, 1)
                if e == 1 and not first:
                    pe.wait_ge(set_lo, 4 * (b + 1))
                    project(b - 1, 1 - par)
                if e == 2:
                    if not last:
                        if first:
                            pe.wait_ge(set_lo, 4 * (b + 1))
                        transpose_x(b + 1, first)
                    if not first:
                        transpose_acc(b - 1, 1 - par)
                if e == 3 and not last:
                    logits(b + 1)
                if e == 4 and not last:
                    if not first:
                        pe.wait_ge(accT_made, b)
                    step_sizes(b + 1, 1 - par)
                if e == 6 and not last:
                    compact(b + 1, 1 - par, 0)
                if e == 7 and not last:
                    transpose_comb(b + 1)
                down_before(3)
                if following:
                    spread_c(*following)
                up(b, par, e, 3, first)
                if e < E - 1:
                    spread_b(b, n + PER, first)

        rolled(pe, body)
        pe.wait_ge(t_made, B * E - 1)
        for c in range(C):
            down(B - 1, E - 1, c)
        project(B - 1, (B - 1) % 2)
        transpose_acc(B - 1, (B - 1) % 2)

    @block.scalar
    def _(act):
        def hidden(b, e, first):
            for c in range(C):
                k = e * C + c
                act.wait_ge(up_done, b * N + k + 1)
                if not (first and e < 2):
                    act.wait_ge(y2_done, b * E + e - 1)
                if k >= HID:
                    lo_ready(act, b, (k - HID) // C, (k - HID) % C)
                elif not first:
                    lo_ready(act, b - 1, E - 1, C - HID + k)
                bias = cols[:, CB1 + k:CB1 + k + 1]
                act.activation(hh[slot_of(e, c)][:, :], PH[k % BANKS][:, :], ACT.Gelu, bias=bias)
                act.activation(hid[c % HID][:, :], PH[k % BANKS][:, :], ACT.Gelu, bias=bias).then_inc(hid_made, 1)

        def evacuate_x(b, par, first):
            act.wait_ge(xposed, b + 1)
            if not first:
                act.wait_ge(u_made, b)
                act.wait_ge(logits_done, b)
            act.activation(xT[:, :], G[0][:, :], ACT.Identity)
            act.activation(nh[par][:, :], G[0][:, :], ACT.Identity).then_inc(nT_made, 1)

        def gate_tanh(b):
            act.wait_ge(gap_made, b + 1)
            act.activation(th[:, :, 0:1], gap[:, :, :], ACT.Tanh, scale=0.5 / TEMP).then_inc(th_made, 1)

        def softplus(b, par):
            act.preload_act_table_set("natural_log_exp_and_others")
            act.wait_ge(v_made, b + 1)
            act.activation(soft[:, :], soft[:, :], ACT.Exp).then_inc(e_made, 1)
            act.wait_ge(e1_made, b + 1)
            act.activation(ln[:, :], y[par][:, :], ACT.Ln).then_inc(ln_made, 1)

        def decays(b, states, first):
            act.preload_act_table_set("natural_log_exp_and_others")
            act.wait_ge(dt_made, b + 1)
            for n in states:
                decay(b, n, first)

        def decay(b, n, first):
            if not first:
                act.wait_ge(scan_made, (b - 1) * NS + n + 1)
            act.activation(abar[:, n, :], dt[:, :], ACT.Exp, scale=aneg[:, n:n + 1]).then_inc(abar_made, 1)

        def evacuate_sets(b, half, first):
            for k in range(2):
                act.wait_ge(set_done, 4 * b + 2 * half + k + 1)
                if not first:
                    act.wait_ge(b_done, (b - 1) * NS + HALF * (half + 1))
                    act.wait_ge(c_done, (b - 1) * NS + HALF * (half + 1))
                act.activation(bch[:, 2 * k + half, :], G[k][:, :], ACT.Identity).then_inc(set_hi, 1)

        def evacuate_s1(b):
            act.wait_ge(wout_done, b + 1)
            act.wait_ge(xo_made, b + 1)
            act.activation(s1[:, :, :], G[0][:, :].rearrange("p (j d) -> p j d", j=J), ACT.Identity).then_inc(s1_made, 1)

        def evacuate_acc(b):
            act.wait_ge(accT_done, b + 1)
            act.activation(z[:, :, :], G[1][:, :].rearrange("p (j d) -> p j d", j=J), ACT.Identity).then_inc(accT_made, 1)

        def tanh_z(b):
            act.wait_ge(z_made, b + 1)
            act.activation(tz[:, :, :], z[:, :, :], ACT.Tanh, scale=0.5).then_inc(tz_made, 1)

        act.dma_start(cols[:, :], dram["cols1"]).then_inc(cols_in, 16)
        act.wait_ge(cols_in, 16)
        act.activation(aneg[:, :], cols[:, CA:CA + NS], ACT.Exp).then_inc(a_made, 1)
        act.wait_ge(small_made, 1)
        act.activation(wth[:, :], wt, ACT.Identity)
        act.activation(wsh[:, :, :], wset[:, :, :], ACT.Identity)
        act.activation(pick[:, :, :], picks[:, :, :], ACT.Identity).then_inc(small_hi, 1)
        evacuate_x(0, 0, True)
        gate_tanh(0)
        softplus(0, 0)
        evacuate_sets(0, 0, True)
        decays(0, range(SOON), True)

        def body(b, par, first, last):
            for e in range(E):
                hidden(b, e, first)
                if e == 0:
                    evacuate_sets(b, 1, first)
                    decays(b, range(SOON if first else NS - LATE, NS), first)
                if e == 1 and not first:
                    evacuate_s1(b - 1)
                if e == 2:
                    if not last:
                        evacuate_x(b + 1, 1 - par, False)
                    if not first:
                        evacuate_acc(b - 1)
                if e == 4 and not last:
                    gate_tanh(b + 1)
                if e == 5 and not last:
                    softplus(b + 1, 1 - par)
                if e == 6 and not first:
                    tanh_z(b - 1)
                if e == 6 and not last:
                    evacuate_sets(b + 1, 0, False)
                    decays(b + 1, range(SOON), False)
            if not last:
                decays(b + 1, range(SOON, NS - LATE), False)

        rolled(act, body)
        evacuate_s1(B - 1)
        evacuate_acc(B - 1)
        tanh_z(B - 1)

    @block.gpsimd
    def _(pool):
        def power(b, k, made, done):
            pool.wait_ge(made, b + 1)
            pool.tensor_tensor(rstd[:, k, :], var[:, k, :], half[:, :], ALU.pow).then_inc(done, 1)

        def low_part(b, e, c):
            s = slot_of(e, c)
            pool.wait_ge(hid_made, b * N + e * C + c + 1)
            pool.tensor_tensor(hl[s][:, :], hid[c % HID][:, :], hh[s][:, :].bitcast(F32), ALU.subtract).then_inc(lo_pool, 1)

        def accumulate(b, par, e):
            pool.wait_ge(t_made, b * E + e + 1)
            if e >= 2:
                pool.wait_ge(acc_made, b * (E - 1) + e - 1)
            pool.tensor_tensor(acc[par][:, :], acc[par][:, :], t[e % 2][:, :], ALU.add).then_inc(acc_made, 1)

        def sum_states(b, par, n):
            if n == 0:
                return
            pool.wait_ge(m_made, b * NS + n + 1)
            if n >= 2:
                pool.wait_ge(y_made, b * (NS - 1) + n - 1)
            pool.tensor_tensor(y[par][:, :], y[par][:, :], bx[n % RX][:, :], ALU.add).then_inc(y_made, 1)

        pool.memset(ones[:, :], 1.0).then_inc(half_made, 1)
        pool.memset(half[:, :], -0.5).then_inc(half_made, 1)
        pool.wait_ge(half_made, 2)
        power(0, 0, var_made, rstd_made)
        def body(b, par, first, last):
            for e in range(E):
                if e > 0:
                    sum_states(b, par, PER * e - 1)
                elif not first:
                    sum_states(b - 1, 1 - par, NS - 1)
                if e < 2 and not first:
                    accumulate(b - 1, 1 - par, E - 2 + e)
                if e >= 3:
                    accumulate(b, par, e - 2)
                low_part(b, e, 0)
                sum_states(b, par, PER * e)
                low_part(b, e, 1)
                if 2 not in LO_ON_DVE[e]:
                    low_part(b, e, 2)
                if e == 3 and not first:
                    power(b - 1, 1, tvar_made, trstd_made)
                if e == 0 and not last:
                    power(b + 1, 0, var_made, rstd_made)
        rolled(pool, body)
        sum_states(B - 1, (B - 1) % 2, NS - 1)
        accumulate(B - 1, (B - 1) % 2, E - 2)
        accumulate(B - 1, (B - 1) % 2, E - 1)
        power(B - 1, 1, tvar_made, trstd_made)

    @block.vector
    def _(dve):
        chain, tchain = chained(dve, prep, PREP), chained(dve, tail, TAIL)

        def low_part(b, e):
            for c in LO_ON_DVE[e]:
                s = slot_of(e, c)
                dve.wait_ge(hid_made, b * N + e * C + c + 1)
                dve.tensor_tensor(hl[s][:, :], hid[c % HID][:, :], hh[s][:, :].bitcast(F32), ALU.subtract).then_inc(lo_dve, 1)

        def weigh(b, par, e, first):
            dve.wait_ge(y2_done, b * E + e + 1)
            s = e % len(gate)
            dve.wait_ge(gate_in[s], 16 * (b * (E // len(gate)) + e // len(gate) + 1))
            if e == 0:
                out = acc[par]
            else:
                out = t[e % 2]
                if e >= 3:
                    dve.wait_ge(acc_made, b * (E - 1) + e - 2)
                elif not first:
                    dve.wait_ge(acc_made, b * (E - 1))
            dve.scalar_tensor_tensor(out[:, :], PY[:, :], cols[:, CB2 + e:CB2 + e + 1], gate[s][:, :],
                                     ALU.add, ALU.mult).then_inc(t_made, 1)

        def states_in(b, n, first):
            dve.wait_ge(b_done, b * NS + n + 1)
            if n == 0:
                dve.wait_ge(u_made, b + 1)
            if n > RX:
                dve.wait_ge(y_made, b * (NS - 1) + n - RX)
            elif n < RX and not first:
                dve.wait_ge(y_made, (b - 1) * (NS - 1) + NS - RX + n)
            dve.tensor_tensor(bx[n % RX][:, :], u[:, :], PB[:, :], ALU.mult).then_inc(bx_made, 1)

        def state_scan(b, n):
            dve.wait_ge(bx_made, b * NS + n + 1)
            dve.wait_ge(abar_made, b * NS + n + 1)
            dve.tensor_tensor_scan(bx[n % RX][:, :], abar[:, n, :], bx[n % RX][:, :], 0.0,
                                   ALU.mult, ALU.add).then_inc(scan_made, 1)

        def states_out(b, par, n, first):
            dve.wait_ge(scan_made, b * NS + n + 1)
            dve.wait_ge(c_done, b * NS + n + 1)
            out = y[par] if n == 0 else bx[n % RX]
            dve.tensor_tensor(out[:, :], bx[n % RX][:, :], PC[:, :], ALU.mult).then_inc(m_made, 1)

        def normalise(b):
            dve.wait_ge(xin_in, 16 * (b + 1))
            for j in range(J):
                i = dve.bn_stats(st[:, j, :], xn[:, j, :])
            chain(b, 1, i)
            apart(dve, dve_passed)
            for j in range(J):
                i = dve.bn_aggr(mv[:, j, :], st[:, j, :])
            chain(b, 2, i)
            dve.tensor_scalar(var[:, 0, :], mv[:, :, 1], LN_EPS, None, ALU.add).then_inc(var_made, 1)

        def normalise2(b):
            dve.wait_ge(rstd_made, b + 1)
            for j in range(J):
                i = dve.tensor_scalar(xn[:, j, :], xn[:, j, :], mv[:, j, 0:1], rstd[:, 0, j:j + 1],
                                      ALU.subtract, ALU.mult)
            i.then_inc(xn_made, 1)

        def split_normed(b, par):
            dve.wait_ge(nT_made, b + 1)
            dve.tensor_tensor(nl[par][:, :], xT[:, :], nh[par][:, :].bitcast(F32), ALU.subtract).then_inc(nl_made, 1)

        def route(b):
            dve.wait_ge(logits_done, b + 1)
            chain(b, 3, dve.tensor_tensor(lg[:, :, :], G[0][:, 0:J * E].rearrange("p (j e) -> p j e", j=J), gb[:, :, :],
                                          ALU.add))
            apart(dve, dve_passed)
            for j in range(J):
                i = dve.max(top[:, j, :], lg[:, j, :])
            chain(b, 4, i)
            dve.tensor_tensor(gap[:, :, :], top[:, :, 0:1], top[:, :, 1:2], ALU.subtract).then_inc(gap_made, 1)

        def route2(b):
            for j in range(J):
                i = dve.max_index(idx[:, j, :], top[:, j, :], lg[:, j, :])
            chain(b, 5, i)
            chain(b, 6, dve.tensor_copy(idxf[:, :, :], idx[:, :, 0:2]))

        def softmax_of_two(b):
            dve.wait_ge(th_made, b + 1)
            for k in range(2):
                dve.tensor_tensor(eq[:, :, k, :], iota8[:, :].rearrange("p (j e) -> p j e", j=J),
                                  idxf[:, :, k:k + 1].to_broadcast([P, J, E]), ALU.is_equal)
            dve.tensor_scalar(th[:, :, 1:2], th[:, :, 0:1], -0.5, 0.5, ALU.mult, ALU.add)
            chain(b, 8, dve.tensor_scalar(gap[:, :, :], th[:, :, 0:1], 0.5, 0.5, ALU.mult, ALU.add))
            dve.tensor_tensor(eq[:, :, 1, :], eq[:, :, 1, :], th[:, :, 1:2].to_broadcast([P, J, E]), ALU.mult)
            chain(b, 9, dve.tensor_tensor(eq[:, :, 0, :], eq[:, :, 0, :], gap[:, :, :].to_broadcast([P, J, E]), ALU.mult))
            dve.tensor_tensor(comb[:, :, :], eq[:, :, 0, :], eq[:, :, 1, :], ALU.add).then_inc(comb_made, 1)

        def keep_comb(b, first):
            dve.wait_ge(combT_done, b + 1)
            if not first:
                dve.wait_ge(comb_out, 16 * b)
            dve.tensor_copy(combT, G[0][0:E, :]).then_inc(combT_made, 1)

        def step_in(b, first):
            dve.wait_ge(dt_done, b + 1)
            if not first:
                dve.wait_ge(abar_made, b * NS)
            chain(b, 7, dve.tensor_scalar(dt[:, :], G[1][:, :], cols[:, CBDT:CBDT + 1], None, ALU.add))
            dve.scalar_tensor_tensor(soft[:, :], dt[:, :], -1.0, dt[:, :], ALU.mult, ALU.min).then_inc(v_made, 1)

        def split_sets(b, half):
            for k in range(2):
                s = 2 * k + half
                dve.wait_ge(set_hi, 4 * b + 2 * half + k + 1)
                dve.tensor_tensor(bcl[:, s, :], G[k][:, :], bch[:, s, :].bitcast(F32), ALU.subtract).then_inc(set_lo, 1)

        def one_plus(b, par):
            dve.wait_ge(e_made, b + 1)
            e1 = y[par]
            dve.tensor_scalar(e1[:, :], soft[:, :], 1.0, None, ALU.add).then_inc(e1_made, 1)
            dve.wait_ge(e1_made, b + 1)
            dve.scalar_tensor_tensor(soft[:, :], e1[:, :], 1.0, soft[:, :], ALU.subtract, ALU.subtract).then_inc(left_out, 1)

        def softplus(b):
            dve.wait_ge(left_out, b + 1)
            dve.scalar_tensor_tensor(dt[:, :], dt[:, :], 0.0, soft[:, :], ALU.max, ALU.subtract).then_inc(kept_made, 1)
            dve.wait_ge(kept_made, b + 1)
            dve.wait_ge(ln_made, b + 1)
            dve.tensor_tensor(dt[:, :], dt[:, :], ln[:, :], ALU.add).then_inc(dt_made, 1)

        def states_input(b, first):
            dve.wait_ge(dt_made, b + 1)
            if not first:
                dve.wait_ge(bx_made, b * NS)
            dve.tensor_tensor(u[:, :], dt[:, :], xT[:, :], ALU.mult).then_inc(u_made, 1)

        def norm_experts(b):
            dve.wait_ge(accT_made, b + 1)
            for j in range(J):
                i = dve.bn_stats(st2[:, j, :], z[:, j, :])
            tchain(b, 1, i)
            apart(dve, dve_passed)
            for j in range(J):
                i = dve.bn_aggr(mv2[:, j, :], st2[:, j, :])
            tchain(b, 2, i)
            dve.tensor_scalar(var[:, 1, :], mv2[:, :, 1], LN_EPS, None, ALU.add).then_inc(tvar_made, 1)

        def norm_experts2(b):
            dve.wait_ge(trstd_made, b + 1)
            for j in range(J):
                i = dve.tensor_scalar(z[:, j, :], z[:, j, :], mv2[:, j, 0:1], rstd[:, 1, j:j + 1],
                                      ALU.subtract, ALU.mult)
            tchain(b, 3, i)

        def scale_experts(b):
            tchain(b, 4, dve.tensor_tensor(z[:, :, :], z[:, :, :], lng[:, None, :].to_broadcast([P, J, P]), ALU.mult))
            dve.tensor_tensor(z[:, :, :], z[:, :, :], lnb[:, None, :].to_broadcast([P, J, P]), ALU.add).then_inc(z_made, 1)

        def finish(b):
            dve.wait_ge(tz_made, b + 1)
            tchain(b, 5, dve.scalar_tensor_tensor(z[:, :, :], tz[:, :, :], 1.0, z[:, :, :], ALU.add, ALU.mult))
            dve.wait_ge(s1_made, b + 1)
            tchain(b, 6, dve.scalar_tensor_tensor(z[:, :, :], z[:, :, :], 0.5, s1[:, :, :], ALU.mult, ALU.mult))
            dve.wait_ge(xres_in, 16 * (b + 1))
            dve.tensor_tensor(xres[:, :, :], xres[:, :, :], z[:, :, :], ALU.add).then_inc(xo_made, 1)

        dve.sem_inc(xo_made, 1)
        normalise(0)
        normalise2(0)
        dve.wait_ge(cols_in, 16)
        dve.wait_ge(a_made, 1)
        dve.tensor_scalar(aneg[:, :], aneg[:, :], -1.0, None, ALU.mult)
        dve.wait_ge(w_in, 16 * 5)
        dve.wait_ge(wt_done, 1)
        dve.tensor_tensor(wt, G[1][:, 0:P], mask[:, 0, :], ALU.mult)
        dve.tensor_tensor(wset[:, :, :], wset[:, :, :], mask.to_broadcast([P, 4, P]),
                          ALU.mult).then_inc(small_made, 1)
        dve.wait_ge(small_hi, 1)
        dve.tensor_tensor(wtl[:, :], wt, wth[:, :].bitcast(F32), ALU.subtract)
        dve.tensor_tensor(wsl[:, :, :], wset[:, :, :], wsh[:, :, :].bitcast(F32), ALU.subtract).then_inc(small_lo, 1)
        split_normed(0, 0)
        route(0)
        route2(0)
        step_in(0, True)
        softmax_of_two(0)
        one_plus(0, 0)
        softplus(0)
        states_input(0, True)
        split_sets(0, 0)
        keep_comb(0, True)

        def body(b, par, first, last):
            for e in range(E):
                n = PER * e
                states_in(b, n, first)
                if e < 2 and not first:
                    weigh(b - 1, 1 - par, E - 2 + e, False)
                if e > 1:
                    weigh(b, par, e - 2, first)
                state_scan(b, n)
                states_in(b, n + 1, first)
                if e == 3 and not last:
                    split_normed(b + 1, 1 - par)
                if e == 7 and not last:
                    split_sets(b + 1, 0)
                states_out(b, par, n, first)
                if e == 6 and not last:
                    one_plus(b + 1, 1 - par)
                if e > 0:
                    low_part(b, e - 1)
                elif not first:
                    low_part(b - 1, E - 1)
                state_scan(b, n + 1)
                if e == 0 and not last:
                    normalise(b + 1)
                if e == 1:
                    split_sets(b, 1)
                    if not last:
                        normalise2(b + 1)
                if e == 3 and not first:
                    norm_experts(b - 1)
                if e == 4:
                    if not first:
                        norm_experts2(b - 1)
                    if not last:
                        route(b + 1)
                if e == 5 and not last:
                    step_in(b + 1, False)
                states_out(b, par, n + 1, first)
                if e == 4 and not last:
                    route2(b + 1)
                if e == 5 and not first:
                    scale_experts(b - 1)
                if e == 6 and not last:
                    softplus(b + 1)
                    softmax_of_two(b + 1)
                if e == 7:
                    if not first:
                        finish(b - 1)
                    if not last:
                        states_input(b + 1, False)
                        keep_comb(b + 1, False)

        rolled(dve, body)
        low_part(B - 1, E - 1)
        weigh(B - 1, (B - 1) % 2, E - 2, False)
        weigh(B - 1, (B - 1) % 2, E - 1, False)
        norm_experts(B - 1)
        norm_experts2(B - 1)
        scale_experts(B - 1)
        finish(B - 1)


def build_program(nc, dram):
    from contextlib import ExitStack

    from concourse import mybir

    F32, F32R = mybir.dt.float32, mybir.dt.float32r
    P, C = 128, 4
    EXPERTS = dram["ew1"].shape[0]
    S = dram["x"].shape[1]

    with ExitStack() as ctx:
        def sb(name, shape, dt=F32):
            return ctx.enter_context(nc.sbuf_tensor(name, shape, dt))

        def psum(name):
            return ctx.enter_context(nc.psum_tensor(name, [P, 512], F32))

        shared = {
            "w1h": sb("w1h", [P, EXPERTS, C * P], F32R), "w1l": sb("w1l", [P, EXPERTS, C * P], F32R),
            "w2h": sb("w2h", [P, EXPERTS * C, P], F32R), "w2l": sb("w2l", [P, EXPERTS * C, P], F32R),
            "hh": [sb(f"hh{i}", [P, S], F32R) for i in range(2 * C)],
            "hl": [sb(f"hl{i}", [P, S], F32R) for i in range(2 * C)],
            "t": [sb(f"t{i}", [P, S]) for i in range(2)],
            "acc": sb("acc", [P, S]),
            "xo": sb("xo", [P, S // P, P]), "x1_out": ctx.enter_context(nc.semaphore("x1_out")),
            "ident": sb("ident", [P, P]), "iota8": sb("iota8", [P, 4 * EXPERTS]),
            "PH": [psum(f"PH{i}") for i in range(4)], "PY": psum("PY"), "G": [psum(f"G{i}") for i in range(3)],
        }
        with ExitStack() as own:
            run_layer0(nc, own, shared, dram)
        with ExitStack() as own:
            run_layer1(nc, own, shared, dram)


def lay_out(i):
    import numpy as np

    P, HEADS = 128, 16
    E = i["L0_ffn_eb1"].shape[0]
    D_HEAD = P // HEADS
    NS, R = i["L1_attn_A_log"].shape[1], i["L1_attn_Wdt"].shape[1]

    def columns(a):
        return np.asarray(a).reshape(-1, P).T

    def chunks(b):
        return np.asarray(b).reshape(-1, P).T

    wx = np.asarray(i["L1_attn_Wx"])
    head = np.repeat(np.arange(HEADS), D_HEAD)
    place = np.tile(np.arange(D_HEAD), HEADS)
    same_head = head[:, None] == head[None, :]
    out = {
        "x": i["L0_attn_x"],
        "cols0": np.concatenate([chunks(i["L0_ffn_eb1"]), columns(i["L0_ffn_sb1"]), chunks(i["L0_ffn_eb2"]),
                                 columns(i["L0_ffn_sb2"]), columns(i["L0_attn_time_decay"]),
                                 columns(i["L0_attn_time_mix_v"]), columns(i["L0_attn_time_mix_r"]),
                                 columns(i["L0_ffn_norm_weight"])], axis=1),
        "rw": np.asarray(i["L0_ffn_router_w"]).T,
        "ident": np.eye(P, dtype=np.float32),
        "iota8": np.tile(np.arange(E, dtype=np.float32), (P, 4)),
        "wa": np.stack([np.asarray(i["L0_attn_Wv"]), np.asarray(i["L0_attn_Wo"]).T, np.asarray(i["L0_attn_Wr"]).T]),
        "ew1": i["L0_ffn_ew1"], "ew2": i["L0_ffn_ew2"], "sw1": i["L0_ffn_sw1"], "sw2": i["L0_ffn_sw2"],
        "cols1": np.concatenate([chunks(i["L1_ffn_b1"]), chunks(i["L1_ffn_b2"]),
                                 np.tile(np.asarray(i["L1_attn_bdt"]), HEADS)[:, None],
                                 np.repeat(np.asarray(i["L1_attn_A_log"]), D_HEAD, axis=0),
                                 np.tile(np.asarray(i["L1_ffn_gate_b"]), (P, 4)), np.asarray(i["L1_ffn_gate_w"]),
                                 np.tile(np.asarray(i["L1_ffn_ln_g"]), (P, 1)),
                                 np.tile(np.asarray(i["L1_ffn_ln_b"]), (P, 1))], axis=1),
        "wout": np.asarray(i["L1_attn_Wout"]).T,
        "bout": np.tile(np.asarray(i["L1_attn_bout"]), (1, 4)),
        "ws": np.stack([same_head.astype(np.float32)] +
                       [np.tile(wx[R + k * D_HEAD:R + (k + 1) * D_HEAD].T, (HEADS, HEADS))
                        for k in range(2 * NS // D_HEAD)]),
        "wx": np.stack([np.tile(wx[:R], (1, HEADS)), np.tile(np.asarray(i["L1_attn_Wdt"]).T, (1, HEADS))]),
        "pick": np.stack([same_head & (place == n)[:, None] for n in range(D_HEAD)]).astype(np.float32),
        "w1": i["L1_ffn_w1"], "w2": i["L1_ffn_w2"],
    }
    return {name: np.ascontiguousarray(a) for name, a in out.items()}




def kernel(**inputs):
    import concourse.bacc as bacc
    from concourse import mybir
    from concourse.bass_utils import run_bass_kernel_spmd

    nc = bacc.Bacc("TRN2", target_bir_lowering=False, num_devices=1, dynamic_dma_scratch_size=1024)
    arrays = lay_out(inputs)
    dram = {name: nc.dram_tensor("in_" + name, a.shape, mybir.dt.from_np(a.dtype), kind="ExternalInput").ap()
            for name, a in arrays.items()}
    B, S, D = arrays["x"].shape
    E = arrays["ew1"].shape[0]
    f32 = mybir.dt.float32
    dram["x1"] = nc.dram_tensor("x1", (B, S, D), f32, kind="Internal").ap()
    dram["comb0"] = nc.dram_tensor("comb0", (B, E, S), f32, kind="Internal").ap()
    dram["comb1"] = nc.dram_tensor("comb1", (B, E, S), f32, kind="Internal").ap()
    dram["out"] = nc.dram_tensor("out", (B, S, D), f32, kind="ExternalOutput").ap()
    build_program(nc, dram)
    result = run_bass_kernel_spmd(nc, [{"in_" + name: a for name, a in arrays.items()}], core_ids=[0])
    return result.results[0]["out"]
```
